# Optimizing a Trainium2 kernel written in Bass

```python
import numpy as np
import jax
import jax.numpy as jnp

def _softmax(x, axis=-1):
    return jax.nn.softmax(x, axis=axis)

def _gelu(x):
    return jax.nn.gelu(x, approximate=True)

def _silu(x):
    return jax.nn.silu(x)

def _sigmoid(x):
    return jax.nn.sigmoid(x)

def _layernorm(x, axis=-1, eps=1e-05):
    m = jnp.mean(x, axis=axis, keepdims=True)
    v = jnp.var(x, axis=axis, keepdims=True)
    return (x - m) / jnp.sqrt(v + eps)

def _scatter_add(tgt, idx, src, axis=0):
    return tgt.at[idx].add(src)

def _segment_sum(src, seg, n):
    return jax.ops.segment_sum(src, seg, n)
kernel_name = 'mk_cond_seq_d4_seqx_r8_4514a8'

def setup_inputs(seed: int=0):
    np.random.seed(seed)
    _w = jnp.asarray

    def _rec_inputs():
        import jax
        import jax.numpy as jnp
        _rk = jax.random.key(seed)
        x = -0.0003482 + 1 * jax.random.normal(jax.random.fold_in(_rk, 1), (32, 128, 144), jnp.float32)
        _lenS = 128 - jax.random.randint(jax.random.fold_in(_rk, 7), (32,), 0, max(1, 128 // 4) + 1, jnp.int32)
        _lenS2 = 128 - jax.random.randint(jax.random.fold_in(_rk, 8), (32,), 0, max(1, 128 // 4) + 1, jnp.int32)
        cond_1152 = 0.00257642 + 1.0011 * jax.random.normal(jax.random.fold_in(_rk, 11), (32, 144), jnp.float32)
        return (x, cond_1152)
    x, cond_1152 = _rec_inputs()

    def _L0_cond_setup():
        import jax, jax.numpy as jnp
        import numpy as np
        H = 144
        NH = 16
        HD = H // NH
        MLP = int(H * 4.0)
        EPS = 1e-06

        def _ln(z, scale=None):
            m = jnp.mean(z, axis=-1, keepdims=True)
            v = jnp.mean(jnp.square(z - m), axis=-1, keepdims=True)
            y = (z - m) * jax.lax.rsqrt(v + EPS)
            if scale is not None:
                y = y * scale
            return y
        key = jax.random.key(seed)
        ks = jax.random.split(key, 16)
        B, N = (16, 128)
        x = jax.random.normal(ks[0], (B, N, H), dtype=jnp.float32)
        c = jax.random.normal(ks[1], (B, H), dtype=jnp.float32)

        def xav(k, fan_in, fan_out):
            lim = np.sqrt(6.0 / (fan_in + fan_out))
            return jax.random.uniform(k, (fan_in, fan_out), jnp.float32, -lim, lim)
        w_mod = 0.02 * jax.random.normal(ks[2], (H, 6 * H), dtype=jnp.float32)
        b_mod = 0.02 * jax.random.normal(ks[3], (6 * H,), dtype=jnp.float32)
        w_qkv = xav(ks[4], H, 3 * H)
        b_qkv = jnp.zeros((3 * H,), jnp.float32)
        g_q = jnp.ones((HD,), jnp.float32)
        g_k = jnp.ones((HD,), jnp.float32)
        w_proj = xav(ks[5], H, H)
        b_proj = jnp.zeros((H,), jnp.float32)
        w1 = xav(ks[6], H, MLP)
        b1 = jnp.zeros((MLP,), jnp.float32)
        w2 = xav(ks[7], MLP, H)
        b2 = jnp.zeros((H,), jnp.float32)
        return dict(x=x, c=c, w_mod=w_mod, b_mod=b_mod, w_qkv=w_qkv, b_qkv=b_qkv, g_q=g_q, g_k=g_k, w_proj=w_proj, b_proj=b_proj, w1=w1, b1=b1, w2=w2, b2=b2)
    _L0_cond_all = _L0_cond_setup()
    _L0_cond_in = {k: v for k, v in _L0_cond_all.items() if k in ('w_mod', 'b_mod', 'w_qkv', 'b_qkv', 'g_q', 'g_k', 'w_proj', 'b_proj', 'w1', 'b1', 'w2', 'b2')}
    del _L0_cond_all

    def _L1_cond_setup():
        import jax, jax.numpy as jnp
        import numpy as np
        from jax.scipy.linalg import expm
        N, D, COND_DIM = (144, 64, 144)
        B, T = (16, 128)

        def _rotation(cond, W, b):
            v = jax.nn.silu(cond) @ W.T + b
            iu, ju = jnp.triu_indices(D, k=1)
            A = jnp.zeros((cond.shape[0], D, D), dtype=v.dtype)
            A = A.at[:, iu, ju].set(v).at[:, ju, iu].set(-v)
            return expm(A)
        key = jax.random.key(seed)
        k1, k2, k3, k4, k5 = jax.random.split(key, 5)
        x = jax.random.normal(k1, (B, T, N), dtype=jnp.float32)
        cond = jax.random.normal(k2, (B, COND_DIM), dtype=jnp.float32)
        P = jax.random.normal(k3, (N, D), dtype=jnp.float32)
        n_skew = D * (D - 1) // 2
        bound = 1.0 / np.sqrt(COND_DIM)
        W = jax.random.uniform(k4, (n_skew, COND_DIM), minval=-bound, maxval=bound, dtype=jnp.float32)
        b = jax.random.uniform(k5, (n_skew,), minval=-bound, maxval=bound, dtype=jnp.float32)
        return {'x': x, 'cond': cond, 'P': P, 'W': W, 'b': b}
    _L1_cond_all = _L1_cond_setup()
    _L1_cond_in = {k: v for k, v in _L1_cond_all.items() if k in ('P', 'W', 'b')}
    del _L1_cond_all

    def _L2_cond_setup():
        import jax, jax.numpy as jnp
        import numpy as np
        B, L, C = (8, 128, 144)
        H = 16
        D = C // H
        FF = int(C * 4.0)
        EPS = 1e-06

        def _layernorm(x):
            mu = jnp.mean(x, axis=-1, keepdims=True)
            var = jnp.mean(jnp.square(x - mu), axis=-1, keepdims=True)
            return (x - mu) * jax.lax.rsqrt(var + EPS)

        def _modulate(x, shift, scale):
            return x * (1.0 + scale) + shift

        def _attention(h, W_qkv, b_qkv, W_proj, b_proj):
            b, l, c = h.shape
            qkv = h @ W_qkv + b_qkv
            qkv = qkv.reshape(b, l, 3, H, D)
            q, k, v = (qkv[:, :, 0], qkv[:, :, 1], qkv[:, :, 2])
            scale = D ** (-0.5)
            scores = jnp.einsum('blhd,bmhd->bhlm', q * scale, k)
            attn = jax.nn.softmax(scores, axis=-1)
            o = jnp.einsum('bhlm,bmhd->blhd', attn, v).reshape(b, l, c)
            return o @ W_proj + b_proj
        key = jax.random.key(seed)
        ks = jax.random.split(key, 12)
        s = 0.02
        return {'x': jax.random.normal(ks[0], (B, L, C), jnp.float32), 'c': jax.random.normal(ks[1], (B, 1, C), jnp.float32), 'W_qkv': jax.random.normal(ks[2], (C, 3 * C), jnp.float32) * s, 'b_qkv': jnp.zeros((3 * C,), jnp.float32), 'W_proj': jax.random.normal(ks[3], (C, C), jnp.float32) * s, 'b_proj': jnp.zeros((C,), jnp.float32), 'W_fc1': jax.random.normal(ks[4], (C, FF), jnp.float32) * s, 'b_fc1': jnp.zeros((FF,), jnp.float32), 'W_fc2': jax.random.normal(ks[5], (FF, C), jnp.float32) * s, 'b_fc2': jnp.zeros((C,), jnp.float32), 'W_ada': jax.random.normal(ks[6], (C, 6 * C), jnp.float32) * s, 'b_ada': jnp.zeros((6 * C,), jnp.float32)}
    _L2_cond_all = _L2_cond_setup()
    _L2_cond_in = {k: v for k, v in _L2_cond_all.items() if k in ('W_qkv', 'b_qkv', 'W_proj', 'b_proj', 'W_fc1', 'b_fc1', 'W_fc2', 'b_fc2', 'W_ada', 'b_ada')}
    del _L2_cond_all

    def _L3_cond_setup():
        import jax, jax.numpy as jnp
        import numpy as np
        NUM_HEADS = 16
        NUM_EXPERTS = 4
        TOP_K = 2
        LN_EPS = 1e-06

        def _ln(h):
            mu = jnp.mean(h, axis=-1, keepdims=True)
            var = jnp.var(h, axis=-1, keepdims=True)
            return (h - mu) * jax.lax.rsqrt(var + LN_EPS)

        def _modulate(h, shift, scale):
            return h * (1.0 + scale[:, None, :]) + shift[:, None, :]
        key = jax.random.key(seed)
        ks = jax.random.split(key, 12)
        B, N, C = (8, 128, 144)
        H = 4 * C
        E = NUM_EXPERTS
        s = 0.02
        return {'x': jax.random.normal(ks[0], (B, N, C), jnp.float32), 'c': jax.random.normal(ks[1], (B, C), jnp.float32), 'w_adaln': jax.random.normal(ks[2], (C, 6 * C), jnp.float32) * s, 'b_adaln': jnp.zeros((6 * C,), jnp.float32), 'w_qkv': jax.random.normal(ks[3], (C, 3 * C), jnp.float32) * s, 'b_qkv': jnp.zeros((3 * C,), jnp.float32), 'w_proj': jax.random.normal(ks[4], (C, C), jnp.float32) * s, 'b_proj': jnp.zeros((C,), jnp.float32), 'w_gate': jax.random.normal(ks[5], (C, E), jnp.float32) * s, 'w1': jax.random.normal(ks[6], (E, C, H), jnp.float32) * s, 'b1': jnp.zeros((E, H), jnp.float32), 'w2': jax.random.normal(ks[7], (E, H, C), jnp.float32) * s, 'b2': jnp.zeros((E, C), jnp.float32)}
    _L3_cond_all = _L3_cond_setup()
    _L3_cond_in = {k: v for k, v in _L3_cond_all.items() if k in ('w_adaln', 'b_adaln', 'w_qkv', 'b_qkv', 'w_proj', 'b_proj', 'w_gate', 'w1', 'b1', 'w2', 'b2')}
    del _L3_cond_all
    return {'x': x, 'cond_1152': cond_1152, 'L0_cond_w_mod': _L0_cond_in['w_mod'], 'L0_cond_b_mod': _L0_cond_in['b_mod'], 'L0_cond_w_qkv': _L0_cond_in['w_qkv'], 'L0_cond_b_qkv': _L0_cond_in['b_qkv'], 'L0_cond_g_q': _L0_cond_in['g_q'], 'L0_cond_g_k': _L0_cond_in['g_k'], 'L0_cond_w_proj': _L0_cond_in['w_proj'], 'L0_cond_b_proj': _L0_cond_in['b_proj'], 'L0_cond_w1': _L0_cond_in['w1'], 'L0_cond_b1': _L0_cond_in['b1'], 'L0_cond_w2': _L0_cond_in['w2'], 'L0_cond_b2': _L0_cond_in['b2'], 'L1_cond_P': _L1_cond_in['P'], 'L1_cond_W': _L1_cond_in['W'], 'L1_cond_b': _L1_cond_in['b'], 'L2_cond_W_qkv': _L2_cond_in['W_qkv'], 'L2_cond_b_qkv': _L2_cond_in['b_qkv'], 'L2_cond_W_proj': _L2_cond_in['W_proj'], 'L2_cond_b_proj': _L2_cond_in['b_proj'], 'L2_cond_W_fc1': _L2_cond_in['W_fc1'], 'L2_cond_b_fc1': _L2_cond_in['b_fc1'], 'L2_cond_W_fc2': _L2_cond_in['W_fc2'], 'L2_cond_b_fc2': _L2_cond_in['b_fc2'], 'L2_cond_W_ada': _L2_cond_in['W_ada'], 'L2_cond_b_ada': _L2_cond_in['b_ada'], 'L3_cond_w_adaln': _L3_cond_in['w_adaln'], 'L3_cond_b_adaln': _L3_cond_in['b_adaln'], 'L3_cond_w_qkv': _L3_cond_in['w_qkv'], 'L3_cond_b_qkv': _L3_cond_in['b_qkv'], 'L3_cond_w_proj': _L3_cond_in['w_proj'], 'L3_cond_b_proj': _L3_cond_in['b_proj'], 'L3_cond_w_gate': _L3_cond_in['w_gate'], 'L3_cond_w1': _L3_cond_in['w1'], 'L3_cond_b1': _L3_cond_in['b1'], 'L3_cond_w2': _L3_cond_in['w2'], 'L3_cond_b2': _L3_cond_in['b2']}

def reference(x, cond_1152, L0_cond_w_mod, L0_cond_b_mod, L0_cond_w_qkv, L0_cond_b_qkv, L0_cond_g_q, L0_cond_g_k, L0_cond_w_proj, L0_cond_b_proj, L0_cond_w1, L0_cond_b1, L0_cond_w2, L0_cond_b2, L1_cond_P, L1_cond_W, L1_cond_b, L2_cond_W_qkv, L2_cond_b_qkv, L2_cond_W_proj, L2_cond_b_proj, L2_cond_W_fc1, L2_cond_b_fc1, L2_cond_W_fc2, L2_cond_b_fc2, L2_cond_W_ada, L2_cond_b_ada, L3_cond_w_adaln, L3_cond_b_adaln, L3_cond_w_qkv, L3_cond_b_qkv, L3_cond_w_proj, L3_cond_b_proj, L3_cond_w_gate, L3_cond_w1, L3_cond_b1, L3_cond_w2, L3_cond_b2):
    import jax
    import jax.numpy as jnp

    def _L0_cond_ref(x, c, w_mod, b_mod, w_qkv, b_qkv, g_q, g_k, w_proj, b_proj, w1, b1, w2, b2):
        import jax, jax.numpy as jnp
        import numpy as np
        H = 144
        NH = 16
        HD = H // NH
        MLP = int(H * 4.0)
        EPS = 1e-06

        def _ln(z, scale=None):
            m = jnp.mean(z, axis=-1, keepdims=True)
            v = jnp.mean(jnp.square(z - m), axis=-1, keepdims=True)
            y = (z - m) * jax.lax.rsqrt(v + EPS)
            if scale is not None:
                y = y * scale
            return y
        B, N, _ = x.shape
        mod = jax.nn.swish(c) @ w_mod + b_mod
        sh_msa, sc_msa, g_msa, sh_mlp, sc_mlp, g_mlp = jnp.split(mod, 6, axis=1)
        xn = _ln(x) * (1 + sc_msa[:, None, :]) + sh_msa[:, None, :]
        qkv = xn @ w_qkv + b_qkv
        qkv = qkv.reshape(B, N, 3, NH, HD).transpose(2, 0, 3, 1, 4)
        q, k, v = (qkv[0], qkv[1], qkv[2])
        q = _ln(q, g_q)
        k = _ln(k, g_k)
        attn = jax.nn.softmax(jnp.einsum('bhqd,bhkd->bhqk', q, k) * HD ** (-0.5), axis=-1)
        o = jnp.einsum('bhqk,bhkd->bhqd', attn, v)
        o = o.transpose(0, 2, 1, 3).reshape(B, N, H) @ w_proj + b_proj
        x = x + g_msa[:, None, :] * o
        xn2 = _ln(x) * (1 + sc_mlp[:, None, :]) + sh_mlp[:, None, :]
        h = jax.nn.gelu(xn2 @ w1 + b1, approximate=True)
        x = x + g_mlp[:, None, :] * (h @ w2 + b2)
        return x

    def _L1_cond_ref(x, cond, P, W, b):
        import jax, jax.numpy as jnp
        import numpy as np
        from jax.scipy.linalg import expm
        N, D, COND_DIM = (144, 64, 144)
        B, T = (16, 128)

        def _rotation(cond, W, b):
            v = jax.nn.silu(cond) @ W.T + b
            iu, ju = jnp.triu_indices(D, k=1)
            A = jnp.zeros((cond.shape[0], D, D), dtype=v.dtype)
            A = A.at[:, iu, ju].set(v).at[:, ju, iu].set(-v)
            return expm(A)
        U, _ = jnp.linalg.qr(P)
        R = _rotation(cond, W, b)
        z = jnp.einsum('btn,nd->btd', x, U)
        z_rot = jnp.einsum('btd,bde->bte', z, R)
        x_rot = x + jnp.einsum('btd,nd->btn', z_rot - z, U)
        return x_rot

    def _L2_cond_ref(x, c, W_qkv, b_qkv, W_proj, b_proj, W_fc1, b_fc1, W_fc2, b_fc2, W_ada, b_ada):
        import jax, jax.numpy as jnp
        import numpy as np
        B, L, C = (8, 128, 144)
        H = 16
        D = C // H
        FF = int(C * 4.0)
        EPS = 1e-06

        def _layernorm(x):
            mu = jnp.mean(x, axis=-1, keepdims=True)
            var = jnp.mean(jnp.square(x - mu), axis=-1, keepdims=True)
            return (x - mu) * jax.lax.rsqrt(var + EPS)

        def _modulate(x, shift, scale):
            return x * (1.0 + scale) + shift

        def _attention(h, W_qkv, b_qkv, W_proj, b_proj):
            b, l, c = h.shape
            qkv = h @ W_qkv + b_qkv
            qkv = qkv.reshape(b, l, 3, H, D)
            q, k, v = (qkv[:, :, 0], qkv[:, :, 1], qkv[:, :, 2])
            scale = D ** (-0.5)
            scores = jnp.einsum('blhd,bmhd->bhlm', q * scale, k)
            attn = jax.nn.softmax(scores, axis=-1)
            o = jnp.einsum('bhlm,bmhd->blhd', attn, v).reshape(b, l, c)
            return o @ W_proj + b_proj
        ada = jax.nn.silu(c) @ W_ada + b_ada
        shift_msa, scale_msa, gate_msa, shift_mlp, scale_mlp, gate_mlp = jnp.split(ada, 6, axis=-1)
        h = _modulate(_layernorm(x), shift_msa, scale_msa)
        x = x + gate_msa * _attention(h, W_qkv, b_qkv, W_proj, b_proj)
        h = _modulate(_layernorm(x), shift_mlp, scale_mlp)
        mlp = jax.nn.gelu(h @ W_fc1 + b_fc1, approximate=True) @ W_fc2 + b_fc2
        x = x + gate_mlp * mlp
        return x

    def _L3_cond_ref(x, c, w_adaln, b_adaln, w_qkv, b_qkv, w_proj, b_proj, w_gate, w1, b1, w2, b2):
        import jax, jax.numpy as jnp
        import numpy as np
        NUM_HEADS = 16
        NUM_EXPERTS = 4
        TOP_K = 2
        LN_EPS = 1e-06

        def _ln(h):
            mu = jnp.mean(h, axis=-1, keepdims=True)
            var = jnp.var(h, axis=-1, keepdims=True)
            return (h - mu) * jax.lax.rsqrt(var + LN_EPS)

        def _modulate(h, shift, scale):
            return h * (1.0 + scale[:, None, :]) + shift[:, None, :]
        B, N, C = x.shape
        nh = NUM_HEADS
        hd = C // nh
        mod = jax.nn.silu(c) @ w_adaln + b_adaln
        sh_msa, sc_msa, g_msa, sh_mlp, sc_mlp, g_mlp = jnp.split(mod, 6, axis=-1)
        h = _modulate(_ln(x), sh_msa, sc_msa)
        qkv = (h @ w_qkv + b_qkv).reshape(B, N, 3, nh, hd).transpose(2, 0, 3, 1, 4)
        q, k, v = (qkv[0], qkv[1], qkv[2])
        attn = jax.nn.softmax(jnp.einsum('bhqd,bhkd->bhqk', q, k) * hd ** (-0.5), axis=-1)
        o = jnp.einsum('bhqk,bhkd->bhqd', attn, v).transpose(0, 2, 1, 3).reshape(B, N, C)
        o = o @ w_proj + b_proj
        x = x + g_msa[:, None, :] * o
        xn = _modulate(_ln(x), sh_mlp, sc_mlp)
        xf = xn.reshape(-1, C)
        gate_logits = xf @ w_gate
        topk_logits, topk_idx = jax.lax.top_k(gate_logits, TOP_K)
        gates = jax.nn.softmax(topk_logits, axis=-1)
        cw = jnp.sum(jax.nn.one_hot(topk_idx, NUM_EXPERTS, dtype=xf.dtype) * gates[..., None], axis=1)
        hmid = jax.nn.gelu(jnp.einsum('tc,ech->eth', xf, w1) + b1[:, None, :], approximate=True)
        eo = jnp.einsum('eth,ehc->etc', hmid, w2) + b2[:, None, :]
        moe = jnp.einsum('te,etc->tc', cw, eo).reshape(B, N, C)
        return x + g_mlp[:, None, :] * moe
    x = _L0_cond_ref(x, cond_1152, L0_cond_w_mod, L0_cond_b_mod, L0_cond_w_qkv, L0_cond_b_qkv, L0_cond_g_q, L0_cond_g_k, L0_cond_w_proj, L0_cond_b_proj, L0_cond_w1, L0_cond_b1, L0_cond_w2, L0_cond_b2)
    x = _L1_cond_ref(x, cond_1152, L1_cond_P, L1_cond_W, L1_cond_b)
    x = _L2_cond_ref(x, cond_1152[:, None, :], L2_cond_W_qkv, L2_cond_b_qkv, L2_cond_W_proj, L2_cond_b_proj, L2_cond_W_fc1, L2_cond_b_fc1, L2_cond_W_fc2, L2_cond_b_fc2, L2_cond_W_ada, L2_cond_b_ada)
    x = _L3_cond_ref(x, cond_1152, L3_cond_w_adaln, L3_cond_b_adaln, L3_cond_w_qkv, L3_cond_b_qkv, L3_cond_w_proj, L3_cond_b_proj, L3_cond_w_gate, L3_cond_w1, L3_cond_b1, L3_cond_w2, L3_cond_b2)
    return x

_drawn_inputs = setup_inputs


def setup_inputs(seed=0):
    import zlib

    import numpy as np

    out = dict(_drawn_inputs(seed))
    spreads = {'L0_cond_b_qkv': (0.0, 0.549),
     'L0_cond_g_q': (1.0, 0.6),
     'L0_cond_g_k': (1.0, 0.6),
     'L0_cond_b_proj': (0.0, 0.558),
     'L0_cond_b1': (0.0, 0.647),
     'L0_cond_b2': (0.0, 0.556),
     'L2_cond_b_qkv': (0.0, 0.8),
     'L2_cond_b_proj': (0.0, 0.493),
     'L2_cond_b_fc1': (0.0, 0.8),
     'L2_cond_b_fc2': (0.0, 0.448),
     'L2_cond_b_ada': (0.0, 0.484),
     'L3_cond_b_adaln': (0.0, 0.526),
     'L3_cond_b_qkv': (0.0, 0.8),
     'L3_cond_b_proj': (0.0, 0.414),
     'L3_cond_b1': (0.0, 0.8),
     'L3_cond_b2': (0.0, 0.598)}
    factors = {'L0_cond_b_mod': 5.12,
     'L2_cond_W_qkv': 8.0,
     'L2_cond_W_proj': 8.0,
     'L2_cond_W_fc1': 5.228,
     'L2_cond_W_fc2': 4.769,
     'L3_cond_w_adaln': 2.808,
     'L3_cond_w_qkv': 8.0,
     'L3_cond_w_proj': 8.0,
     'L3_cond_w_gate': 5.211,
     'L3_cond_w1': 7.109,
     'L3_cond_w2': 6.509}
    for name, (base, spread) in spreads.items():
        noise = np.random.default_rng([zlib.crc32(name.encode()), seed]).standard_normal(out[name].shape)
        drawn = base * np.exp(spread * noise) if base else spread * noise
        out[name] = jnp.asarray(drawn.astype(out[name].dtype))
    for name, factor in factors.items():
        out[name] = (out[name] * factor).astype(out[name].dtype)
    return out
```

```python
from collections import deque
from contextlib import ExitStack

import numpy as np

import concourse.bass as bass
from concourse import mybir

F32 = mybir.dt.float32
BF = mybir.dt.bfloat16
ALU = mybir.AluOpType
ACT = mybir.ActivationFunctionType
AX = mybir.AxisListType

B, T, C, NH, HD, FF, D = 32, 128, 144, 16, 9, 576, 64
G = 4
NG = B // G
NPAIR = B // 2
NW = 3
S_SQ = 14
SCALE = HD ** -0.5
EPS = 1e-6
SEM_SPAN = 4000

SH_A, SC_A, G_A, SH_M, SC_M, G_M = range(6)


class I:

    @staticmethod
    def memset(*a, **k):
        return lambda e: e.memset(*a, **k)

    @staticmethod
    def tensor_scalar(*a, **k):
        return lambda e: e.tensor_scalar(*a, **k)

    @staticmethod
    def activation(*a, **k):
        return lambda e: e.activation(*a, **k)

    @staticmethod
    def scalar_tensor_tensor(*a, **k):
        return lambda e: e.scalar_tensor_tensor(*a, **k)

    @staticmethod
    def bn_stats(*a, **k):
        return lambda e: e.bn_stats(*a, **k)

    @staticmethod
    def dma_start(*a, **k):
        return lambda e: e.dma_start(*a, **k)

    @staticmethod
    def transpose(*a, **k):
        return lambda e: e.transpose(*a, **k)

    @staticmethod
    def reciprocal(*a, **k):
        return lambda e: e.reciprocal(*a, **k)

    @staticmethod
    def mul(*a, **k):
        return lambda e: e.mul(*a, **k)

    @staticmethod
    def nop(*a, **k):
        return lambda e: e.nop(*a, **k)

    @staticmethod
    def bn_aggr(*a, **k):
        return lambda e: e.bn_aggr(*a, **k)

    @staticmethod
    def tensor_tensor(*a, **k):
        return lambda e: e.tensor_tensor(*a, **k)

    @staticmethod
    def tensor_reduce(*a, **k):
        return lambda e: e.tensor_reduce(*a, **k)

    @staticmethod
    def matmul(*a, **k):
        return lambda e: e.matmul(*a, **k)

    @staticmethod
    def copy(*a, **k):
        return lambda e: e.copy(*a, **k)

    @staticmethod
    def tensor_tensor_reduce(*a, **k):
        return lambda e: e.tensor_tensor_reduce(*a, **k)

    @staticmethod
    def tensor_copy(*a, **k):
        return lambda e: e.tensor_copy(*a, **k)


class Op:

    __slots__ = ("eng", "emit", "waits", "used", "at", "dma", "sem")

    def __init__(self, eng, emit, waits, dma=None):
        self.eng, self.emit, self.dma = eng, emit, dma
        self.waits = waits
        self.used, self.at, self.sem = False, None, None


def flat(ws):
    for w in ws:
        if w is None:
            continue
        if isinstance(w, (list, tuple)):
            yield from flat(w)
        else:
            yield w


class Queues:

    ENG = ("tensor", "vector", "scalar", "gpsimd", "sync")

    def __init__(self):
        self.q = {e: [] for e in self.ENG}
        self.ndma = 0

    def put(self, eng, emit, *waits, dma=False):
        ws = list(flat(waits))
        for w in ws:
            w.used = True
        op = Op(eng, emit, ws, self.ndma if dma else None)
        if dma:
            self.ndma += 1
        self.q[eng].append(op)
        return op

    def count(self, sem):
        for e in self.ENG:
            n = 0
            for op in self.q[e]:
                if op.dma is not None:
                    op.sem, op.at = sem(f"d{op.dma}"), 16
                elif op.used:
                    op.sem, op.at = sem(f"{e}{n // SEM_SPAN}"), n % SEM_SPAN + 1
                    n += 1

    def play(self, name, eng):
        seen = {}
        for op in self.q[name]:
            need = {}
            for w in op.waits:
                if w.at > need.get(id(w.sem), (None, 0))[1]:
                    need[id(w.sem)] = (w.sem, w.at)
            for k, (s, v) in need.items():
                if seen.get(k, 0) < v:
                    seen[k] = v
                    eng.wait_ge(s, v)
            ins = op.emit(eng)
            if op.dma is not None:
                ins.then_inc(op.sem, 16)
            elif op.used:
                ins.then_inc(op.sem, 1)


class Ring:

    def __init__(self, banks):
        self.banks, self.free, self.n = banks, [[] for _ in banks], 0

    def take(self):
        while True:
            for _ in self.banks:
                i = self.n % len(self.banks)
                self.n += 1
                if self.free[i] is not None:
                    w, self.free[i] = self.free[i], None
                    return i, self.banks[i], w
            yield

    def give(self, i, *ops):
        self.free[i] = list(flat(ops))


def program(nc, a, out):
    q = Queues()
    st = ExitStack()
    with st:
        def sb(name, shape, dt=F32):
            return st.enter_context(nc.sbuf_tensor("s_" + name, shape, dt))

        def pst(name, shape, dt=F32):
            return st.enter_context(nc.psum_tensor("p_" + name, shape, dt))

        sems = {}

        def sem(name):
            if name not in sems:
                sems[name] = st.enter_context(nc.semaphore("m_" + name))
            return sems[name]

        PE = lambda f, *w: q.put("tensor", f, *w)
        DV = lambda f, *w: q.put("vector", f, *w)
        AC = lambda f, *w: q.put("scalar", f, *w)
        PO = lambda f, *w: q.put("gpsimd", f, *w)
        DMA = lambda o, i, *w: q.put("sync", I.dma_start(o, i), *w, dma=True)

        LAY = (0, 2, 3)
        NE = {0: 1, 2: 1, 3: 4}

        X = sb("X", [128, B, C])
        eye = sb("eye", [128, 128])
        eyeb = sb("eyeb", [128, 128], BF)
        eye2 = sb("eye2", [128, 64])
        e3 = sb("e3", [96, 32], BF)
        e3f = sb("e3f", [96, 32])
        ltm = sb("ltm", [128, 64])
        half = sb("half", [128, 32])
        gqk = sb("gqk", [128, 32, HD])
        wq1, wq2, wp, w11, w12, b1, w2, wg = {}, {}, {}, {}, {}, {}, {}, {}
        mainA, mainB, packC = {}, {}, {}
        for l in LAY:
            n = NE[l]
            wm = 432 + n * FF + C + (4 if l == 3 else 0)
            if l == 2:
                mainA[l], mainB[l], packC[l] = mainA[0], mainB[0], packC[0]
            else:
                mainA[l] = sb(f"mA{l}", [128, wm])
                mainB[l] = sb(f"mB{l}", [32, wm])
                packC[l] = sb(f"pC{l}", [128, n * 720 + n * 5])
            wq1[l], wq2[l] = mainA[l][:, 0:432], mainB[l][0:17, 0:432]
            w11[l] = mainA[l][:, 432:432 + n * FF]
            w12[l] = mainB[l][0:16, 432:432 + n * FF]
            wp[l] = mainA[l][:, 432 + n * FF:576 + n * FF], mainB[l][0:17, 432 + n * FF:576 + n * FF]
            w2[l] = packC[l][:, 0:n * 720].rearrange("p (k c) -> p k c", c=C)
            b1[l] = packC[l][:, n * 720:]
        wg1, wg2 = mainA[3][:, 576 + 4 * FF:], mainB[3][0:16, 576 + 4 * FF:]
        MT1 = {l: sb(f"MT1{l}", [128, 4, B]) for l in LAY}
        MT2 = {l: sb(f"MT2{l}", [16, 4, B]) for l in LAY}
        MS = {l: sb(f"MS{l}", [96, 2 * C], BF) for l in LAY}
        condT1, condT2 = sb("cT1", [128, B]), sb("cT2", [17, B])
        ex1, ex2 = sb("ex1", [128, B]), sb("ex2", [16, B])
        sT1, sT2 = sb("sT1", [128, B]), sb("sT2", [17, B])

        QA = [sb(f"QA{i}", [128, NH, 64], BF) for i in range(NW)]
        KA = [sb(f"KA{i}", [128, NH, 64], BF) for i in range(NW)]
        RQ = [sb(f"RQ{i}", [128, 2, NH, HD]) for i in range(NW)]
        CQ = [sb(f"CQ{i}", [128, 32, HD]) for i in range(NW)]
        CS2 = sb("CS2", [128, 32, HD])
        s32 = [sb(f"s32{i}", [128, 4, 32]) for i in range(NW)]
        VA = [sb(f"VA{i}", [128, NH, 32]) for i in range(NW)]
        KT = [sb(f"KT{i}", [128, 8, 128], BF) for i in range(NW)]
        QT = [sb(f"QT{i}", [128, 8, 128], BF) for i in range(NW)]
        MX = [sb(f"MX{i}", [128, 2, NH]) for i in range(NW)]
        Pm = [sb(f"Pm{i}", [128, 1024]) for i in range(4)]
        RP = Ring(Pm)
        OT = [sb(f"OT{i}", [128, 512]) for i in range(NW)]
        ON = [sb(f"ON{i}", [128, C]) for i in range(NW)]
        RD = [sb(f"RD{i}", [128, NH]) for i in range(NW)]
        OF = [(sb(f"OF1{i}", [128, 128]), sb(f"OF2{i}", [17, 128])) for i in range(NW)]
        TY = [sb(f"TY{i}", [128, C]) for i in range(NW)]
        Gt = [sb(f"Gt{i}", [128, G, 2 * C]) for i in range(2)]
        XTA = [(sb(f"XA1{i}", [128, 512]), sb(f"XA2{i}", [17, 512])) for i in range(2)]
        XTM = (sb("XM1", [128, 512]), sb("XM2", [17, 512]))
        XH = [sb(f"XH{i}", [128, G, C]) for i in range(2)]
        ST = [sb(f"ST{i}", [128, G, 6]) for i in range(2)]
        MV = [sb(f"MV{i}", [128, G, 2]) for i in range(2)]
        VE = [sb(f"VE{i}", [128, 2, G]) for i in range(2)]
        H = sb("H", [128, 5, 512])
        TYM = sb("TYM", [128, 2, C])
        MA = sb("MA", [128, G, C])
        rt = sb("rt", [128, 12, 16])
        rt3 = sb("rt3", [128, 2, 64])
        SC = packC[3][:, 0:2048].rearrange("p (a b c) -> p a b c", a=NPAIR, b=2)
        BD = mainA[3][:, 0:2048].rearrange("p (a b) -> p a b", a=NPAIR)
        BQ = sb("BQ", [128, 4, 128])[:, :, :]
        ROT = [((packC, mainA)[i][3][:, 2048:2560], mainB[3][0:17, 512 * i:512 * i + 512]) for i in range(2)]
        VR = [mainB[3][0:32, 1024 + 512 * i:1536 + 512 * i] for i in range(2)]
        HS = sb("HS", [128, NPAIR, D])
        U1, U2, UT = sb("U1", [128, 128]), sb("U2", [16, 128]), sb("UT", [128, C])
        T1, T2 = sb("T1", [128, C]), sb("T2", [80, C])
        VS, sc, JK = sb("VS", [128, C]), sb("scq", [128, 16]), sb("JK", [128, C])
        ZT = sb("ZT", [128, 512])
        WZ = sb("WZ", [128, 512])
        WM = [(Pm[2 * i][:, :], Pm[2 * i + 1][0:17, :]) for i in range(2)]
        MR = H[0:32, 0:2, :].rearrange("p a b -> p (a b)")[:, 0:864]
        MR2 = H[0:32, 2:4, :].rearrange("p a b -> p (a b)")[:, 0:864]

        SB = [pst(f"S{i}", [128, 1024]) for i in range(2)]
        bank = [pst(f"B{i}", [128, 512]) for i in range(4)]
        RS = Ring(SB)
        RA = Ring(bank[0:2])
        RM = Ring(bank[2:4])

        vsc = nc.dram_tensor("vscratch", (B, 4096), F32, kind="Internal").ap()

        d_cond = [DMA(condT1[:], a["condT"][0:128]), DMA(condT2[:], a["condT"][128:145])]
        d_mod = {}
        d_eye = DMA(eye[:], a["eye"])
        for j, l in enumerate((0,)):
            w = WM[j]
            d_mod[l] = [DMA(w[0][:, 0:864], a[f"mod{l}"][0:128]), DMA(w[1][:, 0:864], a[f"mod{l}"][128:145])]
        d_x = []
        xr = a["x"].rearrange("(g b) t c -> g t b c", b=G)
        d_x.append(DMA(X[:, 0:G, :], xr[0]))
        d_eyeb = DV(I.tensor_copy(eyeb[:], eye[:]), d_eye)
        d_e3 = DV(I.tensor_copy(e3[:], e3f[:]), DMA(e3f[:], a["e3"]))
        d_half = DMA(half[:], a["half"])
        d_w = {0: [DMA(mainA[0][:], a["main0"][0:128]), DMA(mainB[0][0:17, :], a["main0"][128:145]),
                   DMA(packC[0][:], a["pack0"])]}
        d_g = DMA(gqk[:], a["gqk"].rearrange("a (h d) -> a h d", d=HD).to_broadcast([128, 32, HD]))
        d_qr = [DMA(T1[:], a["qr1"]), DMA(T2[:], a["qr2"])]
        d_mod[2] = [DMA(WM[1][0][:, 0:864], a["mod2"][0:128]), DMA(WM[1][1][:, 0:864], a["mod2"][128:145])]
        for g in range(1, NG):
            d_x.append(DMA(X[:, G * g:G * g + G, :], xr[g]))
        d_eye2 = DMA(eye2[:], a["eye2"])
        d_ltm = DMA(ltm[:], a["ltm"])

        def load_weights(l, *w):
            d_w[l] = [DMA(mainA[l][:], a[f"main{l}"][0:128], w), DMA(mainB[l][0:17, :], a[f"main{l}"][128:145], w),
                      DMA(packC[l][:], a[f"pack{l}"], w)]

        cst = []
        for i in range(NW):
            m1 = PO(I.memset(QA[i][:], 0.0))
            m2 = PO(I.memset(KA[i][:], 0.0))
            m3 = PO(I.memset(VA[i][:], 0.0))
            cst.append([m1,
                        PO(I.memset(KA[i][:, :, 54:57], 1.0), m2),
                        PO(I.memset(VA[i][:, :, HD:HD + 1], 1.0), m3)])
        ones_o = [DV(I.memset(OF[i][1][:], 1.0)) for i in range(NW)]
        ones_a = [DV(I.memset(XTA[i][1][:], 1.0)) for i in range(2)]
        ones_m = DV(I.memset(XTM[1][:], 1.0))
        ones_h = None
        ones_s = DV(I.memset(sT2[:], 1.0))
        z_bd = PO(I.memset(BD, 0.0))

        sil = []
        for cT, ex, sT, n, dd in ((condT1, ex1, sT1, 128, d_cond[0]), (condT2, ex2, sT2, 16, d_cond[1])):
            o = AC(I.activation(ex[0:n, :], cT[0:n, :], ACT.Exp, scale=-1.0), dd)
            o = DV(I.tensor_scalar(ex[0:n, :], ex[0:n, :], 1.0, None, ALU.add), o)
            o = DV(I.reciprocal(ex[0:n, :], ex[0:n, :]), o)
            sil.append(DV(I.tensor_tensor(sT[0:n, :], ex[0:n, :], cT[0:n, :], ALU.mult),
                          o, ones_s))

        mod_t, mod_s = {}, {}

        def modulation(l, w, dw, mr, rwait):
            cp = []
            for hf in range(2):
                i, bk, fr = yield from RM.take()
                PE(I.matmul(bk[0:32, 0:432], sT1[:, :], w[0][:, 432 * hf:432 * hf + 432],
                                                    start=True, stop=False), fr, sil, dw)
                m = PE(I.matmul(bk[0:32, 0:432], sT2[:, :], w[1][:, 432 * hf:432 * hf + 432],
                                                        start=False, stop=True))
                c = AC(I.copy(mr[:, 432 * hf:432 * hf + 432], bk[0:32, 0:432]), m, rwait)
                RM.give(i, c)
                cp.append(c)
            yield
            i, bk, fr = yield from RM.take()
            for k, kind in enumerate((SH_A, SC_A, SH_M, SC_M)):
                PE(I.transpose(bk[:, 64 * k:64 * k + 32], mr[:, C * kind:C * kind + 128],
                                                                eye[0:32, 0:32]), fr, cp, d_eye)
                t = PE(I.transpose(bk[0:16, 64 * k + 32:64 * k + 64],
                                                                    mr[:, C * kind + 128:C * kind + 144], eye[0:32, 0:32]))
            bv = bk[:, 0:256].rearrange("p (k c) -> p k c", k=4)
            e1 = DV(I.tensor_copy(MT1[l][:, :, :], bv[:, :, 0:32]), t)
            e2 = DV(I.tensor_copy(MT2[l][:, :, :], bv[0:16, :, 32:64]), t)
            s1 = DV(I.tensor_scalar(MT1[l][:, 1:4:2, :], MT1[l][:, 1:4:2, :], 1.0, None, ALU.add), e1)
            s2 = DV(I.tensor_scalar(MT2[l][:, 1:4:2, :], MT2[l][:, 1:4:2, :], 1.0, None, ALU.add), e2)
            RM.give(i, e1, e2)
            mod_t[l] = [s1, s2]
            yield
            last = []
            for k, kind in enumerate((G_A, G_M)):
                src = mr[:, C * kind:C * kind + C]
                dst = [MS[l][32 * j:32 * j + 32, C * k:C * k + C] for j in range(3)]
                h = DV(I.tensor_copy(dst[0], src), cp)
                r = DV(I.tensor_tensor(src, src, dst[0], ALU.subtract), h)
                m = DV(I.tensor_copy(dst[1], src), r)
                mm = DV(I.tensor_copy(JK[0:32, :], dst[1]), m, jk_free[0])
                r = DV(I.tensor_tensor(src, src, JK[0:32, :], ALU.subtract), mm)
                jk_free[0] = r
                last.append(DV(I.tensor_copy(dst[2], src), r))
            mod_s[l] = last
            yield

        jk_free = [None]

        xw = [d_x[b // G] for b in range(B)]
        xr_ = [[] for _ in range(B)]
        xh_free = [None, None]
        gt_ready, gt_free = {}, [None, None]
        xta_free, xta_ready = [[], []], {}
        xtm_free = [[]]

        def norm_t(l, g, which, XT, xt_free, ring, keep, ones):
            p = which
            bs = range(G * g, G * g + G)
            st_ops = []
            for i, b in enumerate(bs):
                o = DV(I.bn_stats(ST[p][:, i, :], X[:, b, :]), xw[b], st_free[p])
                st_ops.append(DV(I.bn_aggr(MV[p][:, i, :], ST[p][:, i, :]), o))
            o = DV(I.tensor_scalar(VE[p][:, 0, :], MV[p][:, :, 1], EPS, None, ALU.add), st_ops, ve_free[p])
            o = PO(I.tensor_tensor(VE[p][:, 1, :], VE[p][:, 0, :], half[:, 0:G], ALU.pow), o, d_half)
            yield
            yield
            nz = []
            for i, b in enumerate(bs):
                n = DV(I.tensor_scalar(XH[p][:, i, :], X[:, b, :], MV[p][:, i, 0:1],
                                                           VE[p][:, 1, i:i + 1], ALU.subtract, ALU.mult), o, xh_free[p])
                nz.append(n)
                xr_[b] = [n]
            st_free[p] = ve_free[p] = nz[-1]
            yield
            yield from turn(XH[p], nz, l, g, p, XT, xt_free, ring, keep, ones)

        st_free, ve_free = [None, None], [None, None]

        def turn(src, ready, l, g, p, XT, xt_free, ring, keep, ones):
            outs, tr = [], []
            for i in range(G):
                k, bk, fr = yield from ring.take()
                PE(I.transpose(bk[:, 0:128], src[:, i, 0:128], eye[:, :]), fr, ready[i], d_eye)
                t = PE(I.transpose(bk[0:16, 128:256], src[:, i, 128:144], eye[:, :]))
                tr.append(t)
                o1, o2 = XT[0][:, 128 * i:128 * i + 128], XT[1][0:16, 128 * i:128 * i + 128]
                if l is None:
                    c1 = DV(I.tensor_copy(o1, bk[:, 0:128]), t, xt_free)
                    c2 = AC(I.copy(o2, bk[0:16, 128:256]), t, c1, xt_free, ones)
                else:
                    b = G * g + i
                    f = 2 * p
                    c1 = DV(I.tensor_scalar(
                        o1, bk[:, 0:128], MT1[l][:, f + 1, b:b + 1], MT1[l][:, f, b:b + 1], ALU.mult, ALU.add),
                        t, xt_free, mod_t[l])
                    c2 = AC(I.activation(
                        o2, bk[0:16, 128:256], ACT.Identity, bias=MT2[l][:, f, b:b + 1],
                        scale=MT2[l][:, f + 1, b:b + 1]), t, c1, xt_free, mod_t[l], ones)
                ring.give(k, c1, c2)
                outs += [c1, c2]
                yield
            xh_free[p] = tr[-1]
            keep.append(outs)

        def gates(l, g, i, ring):
            b = G * g + i
            k, bk, fr = yield from ring.take()
            m = PE(I.matmul(bk[:, 0:288], e3[:, b:b + 1].to_broadcast([96, 128]), MS[l][:, :],
                                                  start=True, stop=True), fr, mod_s[l], d_e3)
            c = AC(I.copy(Gt[g % 2][:, i, :], bk[:, 0:288]), m, gt_free[g % 2])
            ring.give(k, c)
            return c

        def prep_att(l, g):
            p = g % 2
            keep = []
            yield from norm_t(l, g, 0, XTA[p], xta_free[p], RA, keep, ones_a[p])
            gts = []
            for i in range(G):
                gts.append((yield from gates(l, g, i, RA)))
                if i % 2:
                    yield
            gt_ready[l, g] = gts
            xta_ready[l, g] = keep[0]
            xta_free[p] = []

        abuf = {n: [None] * NW for n in ("QA", "KA", "RQ", "CQ", "VA", "KT", "QT", "OT", "ON", "OF", "TY", "MX", "s32")}
        cs2_free = [None]

        def att(l, b):
            g, i, p = b // G, b % G, (b + B * LAY.index(l)) % NW
            xt1, xt2 = XTA[g % 2]
            c0 = cst[p]
            kb, bk, fr = yield from RA.take()
            PE(I.matmul(bk[:, 0:432], xt1[:, 128 * i:128 * i + 128], wq1[l], start=True, stop=False),
               fr, xta_ready[l, g], d_w[l])
            m = PE(I.matmul(bk[:, 0:432], xt2[:, 128 * i:128 * i + 128], wq2[l], start=False, stop=True))
            xta_free[g % 2].append(m)
            yield
            cv = AC(I.copy(VA[p][:, :, 0:HD], bk[:, 288:432].rearrange("p (h d) -> p h d", d=HD)),
                    m, abuf["VA"][p], c0[2])
            if l == 0:
                x3 = bk[:, 0:288].rearrange("p (h d) -> p h d", d=HD)
                s = s32[p]
                o = DV(I.tensor_reduce(s[:, 0, :], x3, AX.X, ALU.add), m, cv, abuf["s32"][p])
                o = DV(I.tensor_scalar(s[:, 1, :], s[:, 0, :], 1.0 / HD, None, ALU.mult), o)
                cc = DV(I.tensor_tensor(CQ[p][:, :, :], x3, s[:, 1, :].unsqueeze(2).to_broadcast([128, 32, HD]),
                                                  ALU.subtract), o, abuf["CQ"][p], cv)
                o = DV(I.tensor_tensor(CS2[:], CQ[p][:], CQ[p][:], ALU.mult), cc, cs2_free[0])
                o = DV(I.tensor_reduce(s[:, 0, :], CS2[:], AX.X, ALU.add), o)
                cs2_free[0] = o
                o = DV(I.tensor_scalar(s[:, 2, :], s[:, 0, :], 1.0 / HD, EPS, ALU.mult, ALU.add), o)
                o = PO(I.tensor_tensor(s[:, 3, :], s[:, 2, :], half[:, :], ALU.pow), o, d_half)
                RA.give(kb, cc, cv)
                yield
                yield
                o = DV(I.tensor_tensor(CQ[p][:], CQ[p][:], s[:, 3, :].unsqueeze(2).to_broadcast([128, 32, HD]),
                                                 ALU.mult), o)
                abuf["s32"][p] = o
                m = DV(I.tensor_tensor(CQ[p][:], CQ[p][:], gqk[:], ALU.mult), o, d_g)
                src = CQ[p][:].rearrange("p (w h) d -> p w h d", w=2)
            else:
                src = bk[:, 0:288].rearrange("p (w h d) -> p w h d", w=2, d=HD)
            qs = QA[p][:, :, 0:54].rearrange("p h (s d) -> p h s d", d=HD)
            ks = KA[p][:, :, 0:54].rearrange("p h (s d) -> p h s d", d=HD)

            def bc(x, n):
                return x.unsqueeze(2).to_broadcast([128, NH, n, HD])

            hq = AC(I.copy(qs[:, :, 0:5:2, :], bc(src[:, 0], 3)), m, cv, abuf["QA"][p], c0[0])
            hk = AC(I.copy(ks[:, :, 3:6, :], bc(src[:, 1], 3)), m, abuf["KA"][p], c0[1])
            R = RQ[p]
            rq = DV(I.tensor_tensor(R[:, 0], src[:, 0], qs[:, :, 0, :], ALU.subtract), hk, abuf["RQ"][p])
            rk = DV(I.tensor_tensor(R[:, 1], src[:, 1], ks[:, :, 3, :], ALU.subtract), hk)
            if l == 0:
                abuf["CQ"][p] = rk
            else:
                RA.give(kb, rk, hk)
            mq = AC(I.copy(qs[:, :, 1:4:2, :], bc(R[:, 0], 2)), rq)
            mk = AC(I.copy(ks[:, :, 0:2, :], bc(R[:, 1], 2)), rk)
            yield
            lq = DV(I.tensor_tensor(qs[:, :, 5, :], R[:, 0], qs[:, :, 1, :], ALU.subtract), mq)
            lk = DV(I.tensor_tensor(ks[:, :, 2, :], R[:, 1], ks[:, :, 0, :], ALU.subtract), mk)
            abuf["RQ"][p] = lk
            z = DV(I.memset(QA[p][:, :, 54:57], 0.0), abuf["QA"][p], c0[0])

            def turn_b(src, ready, dst, name, eng, *more):
                kb2, bk2, fr2 = yield from RA.take()
                pb = bk2[:, :].bitcast(BF)
                for j in range(8):
                    t = PE(I.transpose(pb[:, 128 * j:128 * j + 128],
                                                      src[:, 2 * j:2 * j + 2, :].rearrange("p a b -> p (a b)"), eyeb[:, :]),
                           fr2, ready, d_eyeb)
                pv = pb.rearrange("p (j t) -> p j t", j=8)
                if eng == "v":
                    c = DV(I.tensor_copy(dst[:], pv), t, abuf[name][p], *more)
                else:
                    c = AC(I.copy(dst[:], pv), t, abuf[name][p], *more)
                RA.give(kb2, c)
                return t, c
            yield
            tq, cq = yield from turn_b(QA[p], [lq, z, mq, hq], QT[p], "QT", "v")
            yield
            tk, ck = yield from turn_b(KA[p], [lk, mk, hk], KT[p], "KT", "a")
            abuf["KA"][p] = tk
            yield
            red = []
            for w in range(2):
                ks_, S, frs = yield from RS.take()
                for hh in range(8):
                    h = 8 * w + hh
                    r = 64 * (h % 2)
                    col = 512 * (h % 2) + 128 * (hh // 2)
                    m = PE(I.matmul(
                        S[:, col:col + 128], QT[p][r:r + 64, h // 2, :], KT[p][r:r + 64, h // 2, :],
                        start=True, stop=True), frs, cq, ck)
                o = DV(I.tensor_reduce(
                    MX[p][:, 0, :].rearrange("p (w j r) -> p w r j", w=2, r=2)[:, w],
                    S[:, :].rearrange("p (r j k) -> p r j k", r=2, j=4), AX.X, ALU.max, negate=True), m, abuf["MX"][p])
                RS.give(ks_, o)
                red.append(o)
                yield
            s1_last = m
            f = MX[p]
            a0 = DV(I.tensor_copy(QA[p][:, :, 54], f[:, 0, :]), red, tq)
            a1 = DV(I.tensor_tensor(f[:, 1, :], f[:, 0, :], QA[p][:, :, 54], ALU.subtract), a0)
            a2 = DV(I.tensor_copy(QA[p][:, :, 55], f[:, 1, :]), a1)
            a3 = DV(I.tensor_tensor(QA[p][:, :, 56], f[:, 1, :], QA[p][:, :, 55], ALU.subtract), a2)
            abuf["MX"][p] = a3
            abuf["QT"][p] = s1_last
            yield
            tq, cq = yield from turn_b(QA[p], [a3], QT[p], "QT", "v")
            abuf["QA"][p] = tq
            yield
            ex, ph = [], []
            for w in range(2):
                kp, Pw, frp = yield from RP.take()
                ph.append((kp, Pw))
                ks_, S, frs = yield from RS.take()
                for hh in range(8):
                    h = 8 * w + hh
                    r = 64 * (h % 2)
                    col = 512 * (h % 2) + 128 * (hh // 2)
                    m = PE(I.matmul(
                        S[:, col:col + 128], KT[p][r:r + 64, h // 2, :], QT[p][r:r + 64, h // 2, :],
                        start=True, stop=True), frs, cq)
                o = AC(I.activation(Pw[:, :], S[:, :], ACT.Exp, scale=SCALE), m, frp)
                RS.give(ks_, o)
                ex.append(o)
                yield
            abuf["KT"][p] = abuf["QT"][p] = m
            ko, bo, fro = yield from RA.take()
            for h in range(NH):
                w, hh = h // 8, h % 8
                col = 512 * (h % 2) + 128 * (hh // 2)
                m = PE(I.matmul(
                    bo[32 * (h % 4):32 * (h % 4) + 32, 128 * (h // 4):128 * (h // 4) + 128],
                    VA[p][:, h, :], ph[w][1][:, col:col + 128], start=True, stop=True),
                    fro, ex[w], cv)
                if h == 7:
                    RP.give(ph[0][0], m)
                    yield
            RP.give(ph[1][0], m)
            abuf["VA"][p] = m
            oc = AC(I.copy(OT[p][:], bo[:, :]), m, abuf["OT"][p])
            RA.give(ko, oc)
            yield
            kd, bd_, frd = yield from RA.take()
            for j in range(4):
                m = PE(I.transpose(bd_[:, 128 * j:128 * j + 128], OT[p][:, 128 * j:128 * j + 128], eye[:, :]), frd, oc)
            abuf["OT"][p] = m
            o3 = bd_[:, :].rearrange("p (h s) -> p h s", s=32)
            r = DV(I.reciprocal(RD[p][:, :], o3[:, :, HD]), m, abuf["ON"][p])
            n = DV(I.tensor_tensor(ON[p][:].rearrange("p (h d) -> p h d", d=HD), o3[:, :, 0:HD],
                                   RD[p][:].unsqueeze(2).to_broadcast([128, NH, HD]), ALU.mult), r)
            RA.give(kd, n)
            yield
            kt, bt, frt = yield from RA.take()
            PE(I.transpose(bt[:, 0:128], ON[p][:, 0:128], eye[:, :]), frt, n)
            m = PE(I.transpose(bt[0:16, 128:256], ON[p][:, 128:144], eye[:, :]))
            abuf["ON"][p] = m
            c1 = DV(I.tensor_copy(OF[p][0][:, :], bt[:, 0:128]), m, abuf["OF"][p])
            c2 = AC(I.copy(OF[p][1][0:16, :], bt[0:16, 128:256]), c1, abuf["OF"][p], ones_o[p])
            RA.give(kt, c1, c2)
            yield
            ky, by, fry = yield from RA.take()
            PE(I.matmul(by[:, 0:C], OF[p][0][:, :], wp[l][0], start=True, stop=False), fry, c1, c2)
            m = PE(I.matmul(by[:, 0:C], OF[p][1][:, :], wp[l][1], start=False, stop=True))
            abuf["OF"][p] = m
            y = DV(I.tensor_tensor(TY[p][:], by[:, 0:C], Gt[g % 2][:, i, 0:C], ALU.mult),
                   m, gt_ready[l, g], abuf["TY"][p])
            RA.give(ky, y)
            xx = PO(I.tensor_tensor(X[:, b, :], X[:, b, :], TY[p][:], ALU.add), y, xw[b], xr_[b])
            abuf["TY"][p] = xx
            xw[b], xr_[b] = xx, []
            yield

        h_free = [[mod_done] for mod_done in (None, None)]
        hbufs = 1
        tym_free, ma_free = [None], [None]

        def mlp(l, g):
            keep = []
            p = g % 2
            yield from norm_t(l, g, 1, XTM, xtm_free[0], RM, keep, ones_m)
            ready = keep[0]
            users = []
            cw = []
            if l == 3:
                k, bk, fr = yield from RM.take()
                for i in range(G):
                    PE(I.matmul(bk[:, 4 * i:4 * i + 4], XTM[0][:, 128 * i:128 * i + 128], wg1,
                                                      start=True, stop=False), fr, ready, d_w[3])
                    m = PE(I.matmul(bk[:, 4 * i:4 * i + 4], XTM[1][0:16, 128 * i:128 * i + 128],
                                                          wg2, start=False, stop=True))
                R = lambda j: rt[:, j, :]
                R2 = lambda j: rt[:, j, :].rearrange("p (b e) -> p b e", e=4)
                o = DV(I.tensor_copy(R(0), bk[:, 0:16]), m, rt_free[0])
                RM.give(k, o)
                yield
                mx = DV(I.tensor_reduce(rt[:, 1, 0:4], R2(0), AX.X, ALU.max), o)
                d = DV(I.tensor_tensor(R2(2), R2(0), rt[:, 1, 0:4].unsqueeze(2).to_broadcast([128, 4, 4]),
                                                 ALU.subtract), mx)
                exq = AC(I.activation(R(3), R(2), ACT.Exp), d)
                r3 = lambda j: rt3[:, j, :].rearrange("p (b e f) -> p b e f", b=4, e=4)
                le = R2(0).unsqueeze(3).to_broadcast([128, 4, 4, 4])
                lf = R2(0).unsqueeze(2).to_broadcast([128, 4, 4, 4])
                g1 = DV(I.tensor_tensor(r3(0), lf, le, ALU.is_gt), o)
                g2 = DV(I.tensor_tensor(r3(1), lf, le, ALU.is_equal), o)
                g2 = DV(I.tensor_tensor(rt3[:, 1, :], rt3[:, 1, :], ltm[:], ALU.mult), g2, d_ltm)
                g2 = DV(I.tensor_tensor(rt3[:, 0, :], rt3[:, 0, :], rt3[:, 1, :], ALU.add), g1, g2)
                g2 = DV(I.tensor_reduce(R2(4), r3(0), AX.X, ALU.add), g2)
                g2 = DV(I.tensor_scalar(R(4), R(4), 1.5, None, ALU.is_lt), g2)
                g2 = DV(I.tensor_tensor(R(5), R(4), R(3), ALU.mult), g2, exq)
                s = DV(I.tensor_reduce(rt[:, 6, 0:4], R2(5), AX.X, ALU.add), g2)
                s = DV(I.reciprocal(rt[:, 7, 0:4], rt[:, 6, 0:4]), s)
                s = DV(I.tensor_tensor(R2(8), R2(5), rt[:, 7, 0:4].unsqueeze(2).to_broadcast([128, 4, 4]),
                                                 ALU.mult), s)
                cw = [s]
                yield
            acc = [None] * G
            for x in range(NE[l]):
                ev = []
                for c in range(5):
                    n = 128 if c < 4 else 64
                    k, bk, fr = yield from RM.take()
                    lo = FF * x + 128 * c
                    PE(I.matmul(bk[0:n, :], w11[l][:, lo:lo + n], XTM[0][:, :],
                                                             start=True, stop=False), fr, ready, d_w[l])
                    m = PE(I.matmul(bk[0:n, :], w12[l][:, lo:lo + n], XTM[1][0:16, :],
                                                                 start=False, stop=True))
                    bias = b1[l][0:n, 5 * x + c:5 * x + c + 1]
                    if c % 2:
                        o = AC(I.activation(
                            H[0:n, c, :], bk[0:n, :], ACT.Identity, bias=bias), m, h_free[0])
                    else:
                        o = DV(I.tensor_scalar(
                            H[0:n, c, :], bk[0:n, :], bias, None, ALU.add), m, h_free[0])
                    RM.give(k, o)
                    ev.append(o)
                    yield
                if x == NE[l] - 1:
                    xtm_free[0] = [m]
                a1 = AC(I.activation(H[:, 0:4, :], H[:, 0:4, :], ACT.Gelu_apprx_tanh), ev)
                a2 = AC(I.activation(H[0:64, 4, :], H[0:64, 4, :], ACT.Gelu_apprx_tanh), ev)
                yield
                for hf in range(2):
                    k, bk, fr = yield from RM.take()
                    for i2 in range(2):
                        i = 2 * hf + i2
                        for c in range(5):
                            n = 128 if c < 4 else 65
                            m = PE(I.matmul(
                                bk[:, 256 * i2:256 * i2 + C], H[0:n, c, 128 * i:128 * i + 128], w2[l][0:n, 5 * x + c, :],
                                start=(c == 0), stop=(c == 4)), fr, a2, ones_h)
                        if i2 == 0:
                            yield
                    bs = slice(G * g + 2 * hf, G * g + 2 * hf + 2)
                    yv = bk[:, :].rearrange("p (i c) -> p i c", i=2)[:, :, 0:C]
                    gv = Gt[p][:, 2 * hf:2 * hf + 2, C:2 * C]
                    if l == 3:
                        os = []
                        for i2 in range(2):
                            i = 2 * hf + i2
                            s = rt[:, 8, 4 * i + x:4 * i + x + 1]
                            if x == 0:
                                o = DV(I.tensor_scalar(
                                    MA[:, i, :], bk[:, 256 * i2:256 * i2 + C], s, None, ALU.mult), m, cw, ma_free[0])
                            else:
                                o = DV(I.scalar_tensor_tensor(
                                    MA[:, i, :], bk[:, 256 * i2:256 * i2 + C], s, MA[:, i, :], ALU.mult, ALU.add),
                                    m, cw, acc[i])
                            acc[i] = o
                            os.append(o)
                        RM.give(k, os)
                        if x == NE[l] - 1:
                            rt_free[0] = os
                            y = DV(I.tensor_tensor(
                                TYM[:], MA[:, 2 * hf:2 * hf + 2, :], gv, ALU.mult), os, tym_free[0])
                            ma_free[0] = y
                    else:
                        y = DV(I.tensor_tensor(TYM[:], yv, gv, ALU.mult),
                               m, tym_free[0])
                        RM.give(k, y)
                    if x == NE[l] - 1:
                        ws = [xw[b] for b in range(bs.start, bs.stop)] + [xr_[b] for b in range(bs.start, bs.stop)]
                        xx = PO(I.tensor_tensor(X[:, bs, :], X[:, bs, :], TYM[:], ALU.add), y, ws)
                        tym_free[0] = xx
                        for b in range(bs.start, bs.stop):
                            xw[b], xr_[b] = xx, []
                    yield
                h_free[0] = [m]
            gt_free[p] = y
            if l == 0 and g == NG - 1:
                load_weights(2, m)
            if l == 3:
                outs.append(DMA(out[G * g:G * g + G].rearrange("b t c -> t b c"), X[:, G * g:G * g + G, :],
                                [xw[b] for b in range(G * g, G * g + G)]))

        rt_free = [None]
        outs = []

        u_ready = []

        def qr():
            w1 = list(d_qr)
            w2_ = [d_qr[1]]
            for k in range(D):
                n = C - k
                i, bk, fr = yield from RM.take()
                m = PE(I.matmul(bk[:, 0:n], eye[:, k:k + 1].to_broadcast([128, 128]),
                                                           T1[:, k:C], start=True, stop=True), fr, w1, d_eye)
                c = DV(I.tensor_copy(VS[:, 0:n], bk[:, 0:n]), m, w1, w2_)
                RM.give(i, c)
                s0 = DV(I.tensor_tensor_reduce(JK[:, 0:n], VS[:, 0:n], VS[:, 0:n], 1.0, 0.0, ALU.mult,
                                                              ALU.add, sc[:, 0:1]), c, jk_free[0])
                p0 = PO(I.tensor_tensor(sc[:, 1:2], sc[:, 0:1], half_p[:, :], ALU.pow), s0, d_half2)
                s1 = DV(I.tensor_scalar(sc[:, 2:3], VS[:, 0:1], 0.0, 2.0, ALU.is_ge, ALU.mult), c)
                s1 = DV(I.tensor_scalar(sc[:, 2:3], sc[:, 2:3], -1.0, None, ALU.add), s1)
                yield
                s1 = DV(I.tensor_tensor(sc[:, 3:4], sc[:, 1:2], sc[:, 2:3], ALU.mult), s1, p0)
                s2 = DV(I.scalar_tensor_tensor(sc[:, 4:5], VS[:, 0:1], sc[:, 3:4], sc[:, 0:1],
                                                         ALU.mult, ALU.add), s1)
                s3 = DV(I.tensor_tensor(VS[:, 0:1], VS[:, 0:1], sc[:, 3:4], ALU.add), s2)
                s2 = DV(I.reciprocal(sc[:, 5:6], sc[:, 4:5]), s2)
                t1 = DV(I.tensor_tensor_reduce(JK[:, 0:n], T1[:, k:C], VS[:, 0:n], 1.0, 0.0, ALU.mult,
                                                                   ALU.add, sc[:, 6:7]), s3, s0)
                t2 = DV(I.tensor_tensor_reduce(JK[0:80, 0:n], T2[:, k:C], VS[0:80, 0:n], 1.0, 0.0,
                                                                   ALU.mult, ALU.add, sc[0:80, 7:8]), s3, t1)
                jk_free[0] = t2
                u = DV(I.tensor_scalar(sc[:, 8:10], sc[:, 6:8], sc[:, 5:6], -1.0, ALU.mult, ALU.mult), t2, s2)
                w1 = [DV(I.scalar_tensor_tensor(T1[:, k:C], VS[:, 0:n], sc[:, 8:9], T1[:, k:C],
                                                                    ALU.mult, ALU.add), u)]
                w2_ = [DV(I.scalar_tensor_tensor(T2[:, k:C], VS[0:80, 0:n], sc[0:80, 9:10], T2[:, k:C],
                                                                     ALU.mult, ALU.add), u)]
                yield
            a = []
            for h in range(2):
                a.append(DMA(U1[0:64, 64 * h:64 * h + 64], T1[64:128, 0:64], w1))
                a.append(DMA(U1[64:128, 64 * h:64 * h + 64], T2[0:64, 0:64], w2_))
                a.append(DMA(U2[:, 64 * h:64 * h + 64], T2[64:80, 0:64], w2_))
            yield
            yield
            i, bk, fr = yield from RM.take()
            PE(I.transpose(bk[:, 0:128], U1[:, :], eye[:, :]), fr, a)
            m = PE(I.transpose(bk[:, 128:144], U2[:, :], eye[0:16, 0:16]))
            c = AC(I.copy(UT[:, :], bk[:, 0:C]), m)
            RM.give(i, c)
            u_ready.append(c)
            u_ready.extend(a)
            yield

        half_p = sb("halfp", [128, 1])
        d_half2 = PO(I.memset(half_p[:], 0.5))
        z_sc = PO(I.memset(sc[:], 0.0))
        cs_ready = []

        def rot():
            wr = []
            stg = [None, None]
            for n in range(8):
                p = n % 2
                w1_, w2s = ROT[p]
                dd = [DMA(w1_, a["rotw"][0:128, 512 * n:512 * n + 512], stg[p]),
                      DMA(w2s, a["rotw"][128:145, 512 * n:512 * n + 512], stg[p])]
                i, bk, fr = yield from RM.take()
                PE(I.matmul(bk[0:32, :], sT1[:, :], w1_, start=True, stop=False), fr, dd, sil)
                m = PE(I.matmul(bk[0:32, :], sT2[:, :], w2s, start=False, stop=True))
                stg[p] = m
                c = AC(I.copy(VR[p][:, :], bk[0:32, :]), m, wr[-2:-1])
                RM.give(i, c)
                wr.append(DMA(vsc[:, 512 * n:512 * n + 512], VR[p][:, :], c))
                yield
            vv = vsc.rearrange("(q t) (i j) -> t i q j", t=2, j=D)
            ld = []
            for t in range(2):
                ld.append(DMA(HS[64 * t:64 * t + 64, :, :], vv[t], wr))
                ld.append(DMA(BD[64 * t:64 * t + 64, :, 64 * t:64 * t + 64], vv[t], wr, z_bd))
            for _ in range(4):
                yield
            S, Cc = SC[:, :, 0, :], SC[:, :, 1, :]
            w = []
            for n in range(4):
                i, bk, fr = yield from RM.take()
                for j in range(4):
                    m = PE(I.matmul(bk[:, 64 * j:64 * j + 64], BD[:, 4 * n + j, :], eye2[:, :],
                                                               start=True, stop=True), fr, ld, d_eye2)
                o = DV(I.tensor_tensor(HS[:, 4 * n:4 * n + 4, :], HS[:, 4 * n:4 * n + 4, :],
                                                             bk[:, 0:256].rearrange("p (a b) -> p a b", a=4),
                                                             ALU.subtract), m)
                RM.give(i, o)
                w.append(o)
                yield

            def spread(n, src, scale, ready, wd):
                o = []
                for t in range(2):
                    r = slice(64 * t, 64 * t + 64)
                    o.append(AC(I.mul(BD[r, 4 * n:4 * n + 4, 64 * t:64 * t + 64],
                                                          src[r, 4 * n:4 * n + 4, :], scale), ready, wd))
                return o
            f = 2.0 ** -S_SQ
            bds, q4 = [], []
            for n in range(4):
                r = slice(4 * n, 4 * n + 4)
                s = DV(I.tensor_scalar(S[:, r, :], HS[:, r, :], f, None, ALU.mult), w[n])
                bds.append([s] + spread(n, HS, f, w[n], None))
                yield
            qs_, pre = [], []
            for n in range(4):
                r = slice(4 * n, 4 * n + 4)
                i, bk, fr = yield from RM.take()
                for j in range(4):
                    m = PE(I.matmul(bk[:, 128 * j:128 * j + 64], BD[:, 4 * n + j, :],
                                                               S[:, 4 * n + j, :], start=True, stop=True), fr, bds[n])
                bv = bk[:, :].rearrange("p (a b) -> p a b", a=4)[:, :, 0:64]
                o = AC(I.mul(HS[:, r, :], bv, -1.0), m)
                RM.give(i, o)
                qs_.append(o)
                yield
            e_ = eye2[:, :].unsqueeze(1).to_broadcast([128, 4, D])
            fin = []
            for n in range(4):
                r = slice(4 * n, 4 * n + 4)
                t0 = DV(I.tensor_scalar(Cc[:, r, :], HS[:, r, :], 1.0 / 24, None, ALU.mult), qs_[n])
                z = [AC(I.copy(BQ[64 * t:64 * t + 64, :, 64 * t:64 * t + 64],
                                                   HS[64 * t:64 * t + 64, r, :]), qs_[n], bq_free[0], z_bq)
                     for t in range(2)]
                i, bk, fr = yield from RM.take()
                for j in range(4):
                    m = PE(I.matmul(bk[:, 128 * j:128 * j + 64], BQ[:, j, :],
                                                               HS[:, 4 * n + j, :], start=True, stop=True), fr, z, t0)
                bq_free[0] = m
                bv = bk[:, :].rearrange("p (a b) -> p a b", a=4)[:, :, 0:64]
                q2 = DV(I.tensor_scalar(Q2[:, :, :], bv, 1.0 / 24, None, ALU.mult), m, q2_free[0])
                RM.give(i, q2)
                cc = DV(I.scalar_tensor_tensor(Cc[:, r, :], HS[:, r, :], 0.5, Q2[:, :, :], ALU.mult,
                                                              ALU.add), q2, t0)
                g1 = DV(I.tensor_scalar(Q2[:, :, :], Q2[:, :, :], 0.2, None, ALU.mult), cc)
                gg = DV(I.scalar_tensor_tensor(Q3[:, :, :], HS[:, r, :], 1.0 / 6, Q2[:, :, :], ALU.mult,
                                                              ALU.add), g1, q3_free[0])
                q2_free[0] = gg
                yield
                i, bk, fr = yield from RM.take()
                for j in range(4):
                    m = PE(I.matmul(bk[:, 128 * j:128 * j + 64], BD[:, 4 * n + j, :],
                                                               Q3[:, j, :], start=True, stop=True), fr, gg)
                q3_free[0] = m
                bv = bk[:, :].rearrange("p (a b) -> p a b", a=4)[:, :, 0:64]
                ss = DV(I.tensor_tensor(HS[:, r, :], S[:, r, :], bv, ALU.subtract), m)
                RM.give(i, ss)
                s2 = DV(I.tensor_copy(S[:, r, :], HS[:, r, :]), ss)
                fin.append([cc, s2] + spread(n, HS, 1.0, ss, m))
                yield
            for k in range(S_SQ):
                nxt = []
                for n in range(4):
                    r = slice(4 * n, 4 * n + 4)
                    i, bk, fr = yield from RM.take()
                    for j in range(4):
                        m = PE(I.matmul(
                            bk[:, 128 * j:128 * j + 128], BD[:, 4 * n + j, :],
                            SC[:, 4 * n + j, :, :].rearrange("p a b -> p (a b)"), start=True, stop=True), fr, fin[n])
                    bv = bk[:, :].rearrange("p (a b) -> p a b", a=4)
                    c = AC(I.mul(Cc[:, r, :], bv[:, :, 0:64], -2.0), m)
                    o = DV(I.tensor_tensor(HS[:, r, :], S[:, r, :], bv[:, :, 64:128],
                                                                 ALU.subtract), m, c)
                    RM.give(i, c, o)
                    s = DV(I.tensor_scalar(S[:, r, :], HS[:, r, :], 2.0, None, ALU.mult), o)
                    nxt.append([c, s] + (spread(n, HS, 2.0, o, m) if k < S_SQ - 1 else []))
                    yield
                fin = nxt
            o = []
            for n in range(4):
                r = slice(4 * n, 4 * n + 4)
                o.append(DV(I.tensor_tensor(HS[:, r, :], S[:, r, :], Cc[:, r, :], ALU.add), fin[n]))
            cs_ready.extend(o)
            load_weights(3, o, m)
            yield

        Q2, Q3 = sb("Q2", [128, 4, D]), sb("Q3", [128, 4, D])
        z_bq = PO(I.memset(BQ, 0.0))
        bq_free, q2_free, q3_free = [None], [None], [None]
        zt_free, wz_free = [None], [None]

        def rotate(g):
            keep = []
            yield from turn(X[:, G * g:G * g + G, :], [xw[b] for b in range(G * g, G * g + G)], None, g, 1, XTM,
                            xtm_free[0], RM, keep, ones_m)
            k, bk, fr = yield from RM.take()
            PE(I.matmul(bk[:, :], U1[:, :], XTM[0][:, :], start=True, stop=False), fr, keep[0], u_ready)
            m = PE(I.matmul(bk[:, :], U2[:, :], XTM[1][0:16, :], start=False, stop=True))
            xtm_free[0] = [m]
            z = AC(I.copy(ZT[:, :], bk[:, :]), m, zt_free[0])
            RM.give(k, z)
            yield
            k, bk, fr = yield from RM.take()
            for i in (0, 2, 1, 3):
                b = G * g + i
                r = 64 * (b % 2)
                m = PE(I.matmul(
                    bk[r:r + 64, 128 * i:128 * i + 128], HS[r:r + 64, b // 2, :], ZT[r:r + 64, 128 * i:128 * i + 128],
                    start=True, stop=True), fr, z, cs_ready)
            zt_free[0] = m
            wv = []
            for t in range(2):
                half_of = lambda x, t=t: x[64 * t:64 * t + 64, :].rearrange("p (a b) -> p a b", a=4)[:, t:4:2, :]
                wv.append(AC(I.copy(half_of(WZ), half_of(bk)), m, wz_free[0]))
            RM.give(k, wv)
            yield
            for t in range(2):
                k, bk, fr = yield from RM.take()
                for i2 in range(2):
                    i = 2 * i2 + t
                    m = PE(I.matmul(bk[:, 256 * i2:256 * i2 + C],
                                              WZ[64 * t:64 * t + 64, 128 * i:128 * i + 128], UT[64 * t:64 * t + 64, :],
                                              start=True, stop=True), fr, wv)
                bs = range(G * g + t, G * g + G, 2)
                xv = X[:, G * g + t:G * g + G:2, :]
                yv = bk[:, :].rearrange("p (i c) -> p i c", i=2)[:, :, 0:C]
                o = DV(I.tensor_tensor(xv, xv, yv, ALU.add), m, [xr_[b] for b in bs])
                RM.give(k, o)
                for b in bs:
                    xw[b], xr_[b] = o, []
                yield
            wz_free[0] = m

        for _ in modulation(0, WM[0], d_mod[0], MR, None):
            pass
        for _ in modulation(2, WM[1], d_mod[2], MR2, None):
            pass
        m2q = q.q["tensor"][-1]
        d_mod[3] = [DMA(WM[1][0][:, 0:864], a["mod3"][0:128], m2q), DMA(WM[1][1][:, 0:864], a["mod3"][128:145], m2q)]
        for _ in modulation(3, WM[1], d_mod[3], MR2, mod_s[2]):
            pass
        ones_h = DV(I.memset(H[64:128, 4, :], 1.0))
        for i in range(4):
            RP.give(i, q.q["tensor"][-1])
        h_free[0] = [mod_s[0], mod_s[3], ones_h]

        done = set()
        pj, aj, mj = deque(), deque(), deque()
        for l in LAY:
            for g in range(NG):
                need = {0: set(), 2: {("r", g)}, 3: {("m", 2, g)}}[l]
                prev = {("a", LAY[LAY.index(l) - (g < 2)], b) for b in range(G * ((g - 2) % NG), G * ((g - 2) % NG) + G)} \
                    if (l, g) > (0, 1) else set()
                gfree = {("m", LAY[LAY.index(l) - (g < 2)], (g - 2) % NG)} if (l, g) > (0, 1) else set()
                pj.append((("p", l, g), need | prev | gfree, lambda l=l, g=g: prep_att(l, g)))
                for i in range(G):
                    b = G * g + i
                    aj.append((("a", l, b), {("p", l, g)}, lambda l=l, b=b: att(l, b)))
                mj.append((("m", l, g), {("a", l, b) for b in range(G * g, G * g + G)}, lambda l=l, g=g: mlp(l, g)))
                if l == 0 and g == NG - 1:
                    for g2 in range(NG):
                        mj.append((("r", g2), {("m", 0, g2), "qr", "rot"}, lambda g2=g2: rotate(g2)))
        qj = deque([("rot", set(), rot), ("qr", set(), qr)])
        run = {"p": [], "a": [], "m": [], "q": []}

        def advance(kind, jobs, width, gap=0):
            act = run[kind]
            for j in list(act):
                try:
                    next(j[1])
                    j[2] += 1
                except StopIteration:
                    done.add(j[0])
                    act.remove(j)
            while len(act) < width and jobs and jobs[0][1] <= done and (not act or act[-1][2] >= gap):
                name, _, make = jobs.popleft()
                act.append([name, make(), 0])
                if gap:
                    break

        tick = 0
        while pj or aj or mj or qj or any(run.values()):
            advance("p", pj, 1)
            advance("a", aj, NW, 6)
            advance("m", mj, 1)
            if not aj and not run["a"] or (mj and mj[0][0][1] == 3) or (run["m"] and run["m"][0][0][1] == 3):
                advance("m", mj, 1)
            advance("q", qj, 1)
            tick += 1
            assert tick < 20000

        q.put("sync", I.nop(), outs)

        q.count(sem)
        block = st.enter_context(nc.Block())
        block.sync(lambda e: q.play("sync", e))
        block.gpsimd(lambda e: q.play("gpsimd", e))
        block.scalar(lambda e: q.play("scalar", e))
        block.vector(lambda e: q.play("vector", e))
        block.tensor(lambda e: q.play("tensor", e))


def layout(inputs):
    f = np.float32
    g = {k: np.asarray(v) for k, v in inputs.items()}
    a = {"x": np.ascontiguousarray(g["x"])}
    a["condT"] = np.concatenate([g["cond_1152"].T, np.ones((1, B), f)], 0)

    def rows(w, b):
        return np.concatenate([w, b[None, :]], 0)

    names = {0: ("L0_cond_", "w_mod", "b_mod", "w_qkv", "b_qkv", "w_proj", "b_proj", "w1", "b1", "w2", "b2"),
             2: ("L2_cond_", "W_ada", "b_ada", "W_qkv", "b_qkv", "W_proj", "b_proj", "W_fc1", "b_fc1", "W_fc2", "b_fc2"),
             3: ("L3_cond_", "w_adaln", "b_adaln", "w_qkv", "b_qkv", "w_proj", "b_proj", "w1", "b1", "w2", "b2")}
    for l, (pre, *ns) in names.items():
        wm, bm, wq, bq, wp, bp, w1, b1, w2, b2 = (g[pre + n] for n in ns)
        a[f"mod{l}"] = rows(wm, bm)
        if l != 3:
            w1, b1, w2, b2 = w1[None], b1[None], w2[None], b2[None]
        n = len(w1)
        z = np.zeros((1, n * FF), f)
        parts = [rows(wq, bq), np.concatenate([w1.transpose(1, 0, 2).reshape(C, n * FF), z], 0), rows(wp, bp)]
        if l == 3:
            parts.append(np.concatenate([g["L3_cond_w_gate"], np.zeros((1, 4), f)], 0))
        a[f"main{l}"] = np.concatenate(parts, 1)
        ww = np.zeros((n, 5, 128, C), f)
        ww[:, 0:4] = w2[:, 0:512].reshape(n, 4, 128, C)
        ww[:, 4, 0:64] = w2[:, 512:576]
        ww[:, 4, 64] = b2
        bb = np.zeros((n, 5, 128), f)
        bb[:, 0:4] = b1[:, 0:512].reshape(n, 4, 128)
        bb[:, 4, 0:64] = b1[:, 512:576]
        a[f"pack{l}"] = np.concatenate([ww.reshape(n * 5, 128, C).transpose(1, 0, 2).reshape(128, -1),
                                        bb.reshape(n * 5, 128).T], 1)
    a["gqk"] = np.concatenate([np.tile(g["L0_cond_g_q"], NH), np.tile(g["L0_cond_g_k"], NH)])[None, :]
    qr1 = np.zeros((128, C), f)
    qr1[0:D] = g["L1_cond_P"].T
    qr1[64:128, 0:64] = np.eye(64, dtype=f)
    qr2 = np.zeros((80, C), f)
    qr2[:, 64:144] = np.eye(80, dtype=f)
    a["qr1"], a["qr2"] = qr1, qr2
    iu, ju = np.triu_indices(D, k=1)
    rw = np.zeros((C + 1, D, D), f)
    rw[0:C, iu, ju] = g["L1_cond_W"].T
    rw[C, iu, ju] = g["L1_cond_b"]
    a["rotw"] = rw.reshape(C + 1, D * D)
    a["eye"] = np.eye(128, dtype=f)
    a["eye2"] = np.concatenate([np.eye(64, dtype=f)] * 2, 0)
    a["e3"] = np.concatenate([np.eye(32, dtype=f)] * 3, 0)
    a["half"] = np.full((128, 32), -0.5, f)
    lt = np.zeros((4, 4, 4), f)
    for e in range(4):
        lt[:, e, 0:e] = 1.0
    a["ltm"] = np.broadcast_to(lt.reshape(1, 64), (128, 64))
    return {k: np.ascontiguousarray(v) for k, v in a.items()}


def kernel(**inputs):
    from concourse import bacc
    from concourse.bass_utils import run_bass_kernel_spmd

    nc = bacc.Bacc("TRN2", target_bir_lowering=False, num_devices=1)
    arrays, aps = {}, {}
    for k, v in layout(inputs).items():
        arrays["in_" + k] = v
        aps[k] = nc.dram_tensor("in_" + k, v.shape, mybir.dt.from_np(v.dtype), kind="ExternalInput").ap()
    out = nc.dram_tensor("out_0", (B, T, C), F32, kind="ExternalOutput").ap()
    program(nc, aps, out)
    r = run_bass_kernel_spmd(nc, [arrays], core_ids=[0])
    return r.results[0]["out_0"]
```

```python
from collections import deque
from contextlib import ExitStack

import numpy as np

import concourse.bass as bass
from concourse import mybir

F32 = mybir.dt.float32
F32R = mybir.dt.float32r
BF = mybir.dt.bfloat16
ALU = mybir.AluOpType
ACT = mybir.ActivationFunctionType
AX = mybir.AxisListType

B, T, C, NH, HD, FF, D = 32, 128, 144, 16, 9, 576, 64
G = 4
GP = 2
NG = B // G
NPAIR = B // 2
NW = 4
SGC = 176
S_SQ = 14
SCALE = HD ** -0.5
EPS = 1e-6
SEM_SPAN = 4000

SH_A, SC_A, G_A, SH_M, SC_M, G_M = range(6)


def cols(x):
    return int(np.prod(x.shape[1:]))


class I:

    @staticmethod
    def memset(*a, **k):
        return 60 + cols(a[0]), lambda e: e.memset(*a, **k)

    @staticmethod
    def tensor_scalar(*a, **k):
        return 130 + cols(a[0]), lambda e: e.tensor_scalar(*a, **k)

    @staticmethod
    def activation(*a, **k):
        return 190 + 0.7 * cols(a[0]), lambda e: e.activation(*a, **k)

    @staticmethod
    def scalar_tensor_tensor(*a, **k):
        return 130 + cols(a[0]), lambda e: e.scalar_tensor_tensor(*a, **k)

    @staticmethod
    def bn_stats(*a, **k):
        return 75 + cols(a[1]), lambda e: e.bn_stats(*a, **k)

    @staticmethod
    def dma_start(*a, **k):
        return 2000, lambda e: e.dma_start(*a, **k)

    @staticmethod
    def transpose(*a, **k):
        return 65 if a[0].dtype == BF else 150, lambda e: e.transpose(*a, **k)

    @staticmethod
    def reciprocal(*a, **k):
        return 60 + 6.4 * cols(a[0]), lambda e: e.reciprocal(*a, **k)

    @staticmethod
    def mul(*a, **k):
        return 120 + 0.7 * cols(a[0]), lambda e: e.mul(*a, **k)

    @staticmethod
    def nop(*a, **k):
        return 0, lambda e: e.nop(*a, **k)

    @staticmethod
    def bn_aggr(*a, **k):
        return 70 + cols(a[0]), lambda e: e.bn_aggr(*a, **k)

    @staticmethod
    def tensor_tensor(*a, **k):
        return 80 + cols(a[0]) if a[-1] != ALU.pow else 250 + 166 * cols(a[0]), lambda e: e.tensor_tensor(*a, **k)

    @staticmethod
    def tensor_reduce(*a, **k):
        return 70 + cols(a[1]), lambda e: e.tensor_reduce(*a, **k)

    @staticmethod
    def matmul(*a, **k):
        return 25 + cols(a[0]) * (0.42 if a[2].dtype != F32 else 2.1 if cols(a[1]) > 32 else 0.55), lambda e: e.matmul(*a, **k)

    @staticmethod
    def copy(*a, **k):
        return 120 + 0.7 * cols(a[0]), lambda e: e.copy(*a, **k)

    @staticmethod
    def tensor_tensor_reduce(*a, **k):
        return 80 + cols(a[1]), lambda e: e.tensor_tensor_reduce(*a, **k)

    @staticmethod
    def tensor_copy(*a, **k):
        return 70 + cols(a[0]) * (0.5 if a[1].dtype == BF else 1), lambda e: e.tensor_copy(*a, **k)


class Op:

    __slots__ = ("eng", "emit", "waits", "used", "at", "dma", "sem", "end")

    def __init__(self, eng, emit, waits, dma=None):
        self.eng, self.emit, self.dma = eng, emit, dma
        self.waits = waits
        self.used, self.at, self.sem = False, None, None


def flat(ws):
    for w in ws:
        if w is None:
            continue
        if isinstance(w, (list, tuple)):
            yield from flat(w)
        else:
            yield w


class Queues:

    ENG = ("tensor", "vector", "scalar", "gpsimd", "sync")
    HOP = {("tensor", "tensor"): 0, ("vector", "tensor"): 200, ("scalar", "tensor"): 240, ("gpsimd", "tensor"): 200,
           ("tensor", "vector"): 197, ("tensor", "scalar"): 197, ("vector", "gpsimd"): 155}

    def __init__(self):
        self.q = {e: [] for e in self.ENG}
        self.ndma = 0
        self.clock = {e: 0.0 for e in self.ENG}
        self.last = 0.0
        self.func = None

    def put(self, eng, emit, *waits, dma=False):
        ns, emit = emit
        ws = list(flat(waits))
        for w in ws:
            w.used = True
        op = Op(eng, emit, ws, self.ndma if dma else None)
        t = max([self.clock[eng]] + [w.end + self.HOP.get((w.eng, eng), 130) for w in ws])
        op.end = t + ns
        self.clock[eng] = t + 60 if dma else op.end
        self.last = max(self.last, op.end)
        if dma:
            self.ndma += 1
        self.q[eng].append(op)
        return op

    def count(self, sem):
        for e in self.ENG:
            n = 0
            for op in self.q[e]:
                if op.dma is not None:
                    op.sem, op.at = sem(f"d{op.dma}"), 16
                elif op.used:
                    op.sem, op.at = sem(f"{e}{n // SEM_SPAN}"), n % SEM_SPAN + 1
                    n += 1

    def play(self, name, eng):
        seen = {}
        for op in self.q[name]:
            need = {}
            for w in op.waits:
                if w.at > need.get(id(w.sem), (None, 0))[1]:
                    need[id(w.sem)] = (w.sem, w.at)
            for k, (s, v) in need.items():
                if seen.get(k, 0) < v:
                    seen[k] = v
                    eng.wait_ge(s, v)
            ins = op.emit(eng)
            if op.dma is not None:
                ins.then_inc(op.sem, 16)
            elif op.used:
                ins.then_inc(op.sem, 1)


class Ring:

    def __init__(self, q, banks):
        self.q, self.banks, self.free = q, banks, [[] for _ in banks]

    def take(self):
        while True:
            t, i = min((max([o.end for o in f], default=0.0), i) if f is not None else (np.inf, i)
                       for i, f in enumerate(self.free))
            if t < np.inf:
                w, self.free[i] = self.free[i], None
                if t > self.q.clock["tensor"]:
                    yield t
                return i, self.banks[i], w
            yield -1

    def give(self, i, *ops):
        self.free[i] = list(flat(ops))


def program(nc, a, out):
    q = Queues()
    st = ExitStack()
    with st:
        def sb(name, shape, dt=F32):
            return st.enter_context(nc.sbuf_tensor("s_" + name, shape, dt))

        def pst(name, shape, dt=F32):
            return st.enter_context(nc.psum_tensor("p_" + name, shape, dt))

        sems = {}

        def sem(name):
            if name not in sems:
                sems[name] = st.enter_context(nc.semaphore("m_" + name))
            return sems[name]

        PE = lambda f, *w: q.put("tensor", f, *w)
        DV = lambda f, *w: q.put("vector", f, *w)
        AC = lambda f, *w: q.put("scalar", f, *w)
        PO = lambda f, *w: q.put("gpsimd", f, *w)
        DMA = lambda o, i, *w: q.put("sync", I.dma_start(o, i), *w, dma=True)

        LAY = (0, 2, 3)
        NE = {0: 1, 2: 1, 3: 4}

        X = sb("X", [128, B, C])
        eye = sb("eye", [128, 128])
        eyeb = sb("eyeb", [128, 128], BF)
        e3 = sb("e3", [96, 32], BF)
        ltm = sb("ltm", [128, 64])
        half = sb("half", [128, 32])
        WQ, WF, wp, packC, packP, w2, b1 = {}, {}, {}, {}, {}, {}, {}
        FCOLS = {l: NE[l] * FF + 64 for l in LAY}
        PC = C + 4
        for l in LAY:
            n = NE[l]
            if l == 2:
                packC[l] = packC[0]
            else:
                if l == 0:
                    packC[l] = sb("pC0", [128, 725])
            packP[l] = (sb(f"pP1{l}", [128, PC]), sb(f"pP2{l}", [17, PC]))
            wp[l] = packP[l][0][:, 0:C], packP[l][1][:, 0:C]
            if l != 3:
                w2[l] = packC[l][:, 0:720].rearrange("p (k c) -> p k c", c=C)
                b1[l] = packC[l][:, 720:]
        wg1, wg2 = packP[3][0][:, C:PC], packP[3][1][0:16, C:PC]
        with ExitStack() as early:
            def eb(name, shape):
                return early.enter_context(nc.sbuf_tensor("s_" + name, shape, F32))
            SC = eb("SC", [128, NPAIR, 2, D])[:, :, :, :]
            BD = eb("BD", [128, NPAIR, 128])[:, :, :]
            BQ = eb("BQ", [128, 4, 128])[:, :, :]
            RW1 = [eb(f"RW1{i}", [128, 512]) for i in range(2)]
            RW2 = [eb(f"RW2{i}", [128, 512]) for i in range(2)]
            ROT = [(RW1[i][:, :], RW2[i][0:17, :]) for i in range(2)]
            VR = [eb(f"VR{i}", [32, 512])[:, :] for i in range(2)]
            HS = eb("HS", [128, NPAIR, D])
            CS2 = eb("CS2", [128, 32, HD])
            MRS = [eb(f"MRS{i}", [32, 4, 80]) for i in range(2)]
            condT1, condT2 = eb("cT1", [128, B]), eb("cT2", [17, B])
            ex1, ex2 = eb("ex1", [128, B]), eb("ex2", [16, B])
            sT1, sT2 = eb("sT1", [128, B]), eb("sT2", [17, B])
            eye2, e3f, gqk = eb("eye2", [128, 64]), eb("e3f", [96, 32]), eb("gqk", [128, 32, HD])
            U1, U2, UT = eb("U1", [128, 128]), eb("U2", [16, 128]), eb("UT", [128, C])
            T1, T2 = eb("T1", [128, C]), eb("T2", [80, C])
            VS, sc, JK = eb("VS", [128, C]), eb("scq", [128, 16]), eb("JK", [128, C])
            ZT, WZ = RW1
            Q2, Q3 = (RW2[i][:, 0:4 * D].rearrange("p (a b) -> p a b", a=4) for i in range(2))
        def split_tiles(name, n, width):
            return tuple(sb(f"{name}{x}{n}", [80 if x == "s" else 128, width], F32R) for x in "hls")

        for l in (3, 0):
            if l == 3:
                packC[3] = sb("pC3", [128, 4 * 725])
                w2[3] = packC[3][:, 0:2880].rearrange("p (k c) -> p k c", c=C)
                b1[3] = packC[3][:, 2880:]
            WF[l] = split_tiles("WF", l, FCOLS[l])
            WQ[l] = split_tiles("WQ", l, 432)
        WQ[2], WF[2] = split_tiles("WQ", 2, 432), WF[0]
        SG, SGS = sb("SG", [128, 2, SGC]), sb("SGS", [80, 2, SGC])
        MT1 = {l: sb(f"MT1{l}", [128, 4, B]) for l in LAY}
        MT2 = {l: sb(f"MT2{l}", [80, 4, B]) for l in LAY}
        MS = {l: sb(f"MS{l}", [96, 2 * C], BF) for l in LAY}

        QA = [sb(f"QA{i}", [128, NH, 64], BF) for i in range(NW)]
        VA = [sb(f"VA{i}", [128, NH, 32]) for i in range(NW)]
        KT = [sb(f"KT{i}", [128, 8, 128], BF) for i in range(NW)]
        QT = [sb(f"QT{i}", [128, 8, 128], BF) for i in range(NW)]
        MX = [sb(f"MX{i}", [128, 2, NH]) for i in range(NW)]
        KA = [sb(f"KA{i}", [128, NH, 64], BF) for i in range(2)]
        RQ = [sb(f"RQ{i}", [128, 2, NH, HD]) for i in range(2)]
        CQ = [sb(f"CQ{i}", [128, 32, HD]) for i in range(2)]
        s32 = [sb(f"s32{i}", [128, 4, 32]) for i in range(2)]
        Pm = [sb(f"Pm{i}", [128, 1024]) for i in range(4)]
        RP = Ring(q, Pm)
        OT = [sb(f"OT{i}", [128, 512]) for i in range(2)]
        ON = [sb(f"ON{i}", [128, C]) for i in range(2)]
        RD = [sb(f"RD{i}", [128, NH]) for i in range(2)]
        OF = [(sb(f"OF1{i}", [128, 128]), sb(f"OF2{i}", [17, 128])) for i in range(2)]
        GA = [sb(f"GA{i}", [128, C]) for i in range(2)]
        RFr = Ring(q, [(KA[i], RQ[i], CQ[i], s32[i]) for i in range(2)])
        RBk = Ring(q, [(OT[i], ON[i], RD[i], OF[i], GA[i]) for i in range(2)])
        GM = [sb(f"GM{i}", [128, 2, C]) for i in range(2)]
        XTA = [split_tiles("XA", i, 128 * GP) for i in range(2)]
        XTM = split_tiles("XM", 0, 512)
        XF = [(sb(f"XF1{i}", [128, 128 * n]), sb(f"XF2{i}", [80, 128 * n])) for i, n in enumerate((GP, G))]
        XH = [sb(f"XH{i}", [128, n, 208]) for i, n in enumerate((GP, G))]
        ST = [sb(f"ST{i}", [128, G, 6]) for i in range(2)]
        MV = [sb(f"MV{i}", [128, n, 2]) for i, n in enumerate((GP, G))]
        VE = [sb(f"VE{i}", [128, 2, n]) for i, n in enumerate((GP, G))]
        H = [sb(f"H{i}", [128, 5, 512]) for i in range(2)]
        MA = [CQ[n // 2][:].rearrange("p a b -> p (a b)")[:, C * (n % 2):C * (n % 2) + C] for n in range(4)]
        rt = sb("rt", [128, 8, 16])
        rw = sb("rw", [128, 2, 16])
        rt3 = sb("rt3", [128, 2, 64])
        WM = [(Pm[2 * i][:, :], Pm[2 * i + 1][0:17, :]) for i in range(2)]
        MR = H[0][0:32, 0:2, :].rearrange("p a b -> p (a b)")[:, 0:864]
        MR2 = H[0][0:32, 2:4, :].rearrange("p a b -> p (a b)")[:, 0:864]

        SB = [pst(f"S{i}", [128, 1024]) for i in range(2)]
        bank = [pst(f"B{i}", [128, 512]) for i in range(4)]
        RS = Ring(q, SB)
        RA = Ring(q, bank)
        RM = RA
        RH = Ring(q, H)
        RN = Ring(q, [XTM])
        RMA = Ring(q, [CQ])
        RG = Ring(q, GM)

        vsc = nc.dram_tensor("vscratch", (B, 4096), F32, kind="Internal").ap()

        d_cond = [DMA(condT1[:], a["condT"][0:128]), DMA(condT2[:], a["condT"][128:145])]
        d_mod = {}
        d_eye = DMA(eye[:], a["eye"])
        for j, l in enumerate((0,)):
            w = WM[j]
            d_mod[l] = [DMA(w[0][:, 0:864], a[f"mod{l}"][0:128]), DMA(w[1][:, 0:864], a[f"mod{l}"][128:145])]
        d_x = []
        xr = a["x"].rearrange("(g b) t c -> g t b c", b=G)
        d_x.append(DMA(X[:, 0:G, :], xr[0]))
        d_eyeb = DV(I.tensor_copy(eyeb[:], eye[:]), d_eye)
        d_e3 = DV(I.tensor_copy(e3[:], e3f[:]), DMA(e3f[:], a["e3"]))
        d_half = DMA(half[:], a["half"])
        d_w = {}
        d_g = DMA(gqk[:], a["gqk"].rearrange("a (h d) -> a h d", d=HD).to_broadcast([128, 32, HD]))
        d_qr = [DMA(T1[:], a["qr1"]), DMA(T2[:], a["qr2"])]
        d_mod[2] = [DMA(WM[1][0][:, 0:864], a["mod2"][0:128]), DMA(WM[1][1][:, 0:864], a["mod2"][128:145])]
        for g in range(1, NG):
            d_x.append(DMA(X[:, G * g:G * g + G, :], xr[g]))
        d_eye2 = DMA(eye2[:], a["eye2"])
        d_ltm = DMA(ltm[:], a["ltm"])

        sg_free = [None, None]

        def load_split(W_, l, lo, width, *w):
            ops = []
            for c0 in range(0, width, SGC):
                k, r = nstage[0] % 2, slice(c0, min(c0 + SGC, width))
                nstage[0] += 1
                c = r.stop - c0
                d1 = DMA(SG[:, k, 0:c], a[f"main{l}"][0:128, lo + c0:lo + c0 + c], sg_free[k])
                d2 = DMA(SGS[:, k, 0:c], a[f"mains{l}"][:, lo + c0:lo + c0 + c], sg_free[k])
                h1 = AC(I.copy(W_[0][:, r], SG[:, k, 0:c]), d1, w)
                h2 = AC(I.copy(W_[2][:, r], SGS[:, k, 0:c]), d2, w)
                l1 = DV(I.tensor_tensor(W_[1][:, r], SG[:, k, 0:c], W_[0][:, r].bitcast(F32), ALU.subtract), h1)
                l2 = DV(I.tensor_tensor(W_[2][32:49, r], SGS[32:49, k, 0:c], W_[2][32:49, r].bitcast(F32), ALU.subtract),
                        h2)
                sg_free[k] = [h1, h2, l1, l2]
                ops += [l1, l2, h2]
                yield
            return ops

        nstage = [0]

        def load_att(l, *w):
            d_p = [DMA(packP[l][0][:], a[f"proj{l}"][0:128], w), DMA(packP[l][1][:], a[f"proj{l}"][128:145], w)]
            d_w[l] = yield from load_split(WQ[l], l, 0, 432, w)
            d_wp[l] = d_p

        def load_mlp(l, *w):
            d_c = DMA(packC[l][:], a[f"pack{l}"], w)
            o = yield from load_split(WF[l], l, 432, FCOLS[l], w)
            d_wf[l] = [d_c, o]

        d_wp, d_wf = {}, {}

        cst = []
        for i in range(NW):
            m1 = PO(I.memset(QA[i][:], 0.0))
            m3 = PO(I.memset(VA[i][:], 0.0))
            cst.append([m1, PO(I.memset(VA[i][:, :, HD:HD + 1], 1.0), m3)])
        for i in range(2):
            m2 = PO(I.memset(KA[i][:], 0.0))
            RFr.give(i, PO(I.memset(KA[i][:, :, 54:57], 1.0), m2))
            RBk.give(i, DV(I.memset(OF[i][1][:], 1.0)))
        z_xh = [PO(I.memset(XH[i][:], 0.0)) for i in range(2)]
        z_mrs = []
        for i in range(2):
            o = DV(I.memset(MRS[i][:], 0.0))
            z_mrs.append(DV(I.memset(MRS[i][:, 0:4:2, 16:49:32], 1.0), o))
        ones_h = None
        ones_s = DV(I.memset(sT2[:], 1.0))
        z_bd = PO(I.memset(BD, 0.0))

        sil = []
        for cT, ex, sT, n, dd in ((condT1, ex1, sT1, 128, d_cond[0]), (condT2, ex2, sT2, 16, d_cond[1])):
            o = AC(I.activation(ex[0:n, :], cT[0:n, :], ACT.Exp, scale=-1.0), dd)
            o = DV(I.tensor_scalar(ex[0:n, :], ex[0:n, :], 1.0, None, ALU.add), o)
            o = DV(I.reciprocal(ex[0:n, :], ex[0:n, :]), o)
            sil.append(DV(I.tensor_tensor(sT[0:n, :], ex[0:n, :], cT[0:n, :], ALU.mult),
                          o, ones_s))

        mod_t, mod_s = {}, {}

        def modulation(l, w, dw, mr, mrs, rwait):
            cp = []
            for hf in range(2):
                i, bk, fr = yield from RM.take()
                PE(I.matmul(bk[0:32, 0:432], sT1[:, :], w[0][:, 432 * hf:432 * hf + 432],
                                                    start=True, stop=False), fr, sil, dw)
                m = PE(I.matmul(bk[0:32, 0:432], sT2[:, :], w[1][:, 432 * hf:432 * hf + 432],
                                                        start=False, stop=True))
                c = AC(I.copy(mr[:, 432 * hf:432 * hf + 432], bk[0:32, 0:432]), m, rwait)
                RM.give(i, c)
                cp.append(c)
            yield
            rs = []
            for k, kind in enumerate((SH_A, SC_A, SH_M, SC_M)):
                rs.append(DV(I.tensor_copy(mrs[:, k, :].rearrange("p (a c) -> p a c", c=16)[:, 0:5:2, :],
                                           mr[:, C * kind + 128:C * kind + 144].unsqueeze(1).to_broadcast([32, 3, 16])),
                             cp, z_mrs, rwait))
            i, bk, fr = yield from RM.take()
            for k, kind in enumerate((SH_A, SC_A, SH_M, SC_M)):
                PE(I.transpose(bk[:, 64 * k:64 * k + 32], mr[:, C * kind:C * kind + 128],
                                                                eye[0:32, 0:32]), fr, cp, d_eye)
                t = PE(I.transpose(bk[0:80, 64 * k + 32:64 * k + 64], mrs[:, k, :], eye[0:32, 0:32]), rs)
            bv = bk[:, 0:256].rearrange("p (k c) -> p k c", k=4)
            e1 = DV(I.tensor_copy(MT1[l][:, :, :], bv[:, :, 0:32]), t)
            e2 = DV(I.tensor_copy(MT2[l][:, :, :], bv[0:80, :, 32:64]), t)
            s1 = DV(I.tensor_scalar(MT1[l][:, 1:4:2, :], MT1[l][:, 1:4:2, :], 1.0, None, ALU.add), e1)
            s2 = DV(I.tensor_scalar(MT2[l][:, 1:4:2, :], MT2[l][:, 1:4:2, :], 1.0, None, ALU.add), e2)
            RM.give(i, e1, e2)
            mod_t[l] = [s1, s2]
            yield
            last = []
            for k, kind in enumerate((G_A, G_M)):
                src = mr[:, C * kind:C * kind + C]
                dst = [MS[l][32 * j:32 * j + 32, C * k:C * k + C] for j in range(3)]
                h = DV(I.tensor_copy(dst[0], src), cp)
                r = DV(I.tensor_tensor(src, src, dst[0], ALU.subtract), h)
                m = DV(I.tensor_copy(dst[1], src), r)
                mm = DV(I.tensor_copy(JK[0:32, :], dst[1]), m, jk_free[0])
                r = DV(I.tensor_tensor(src, src, JK[0:32, :], ALU.subtract), mm)
                jk_free[0] = r
                last.append(DV(I.tensor_copy(dst[2], src), r))
            mod_s[l] = last
            yield

        jk_free = [None]

        xw = [d_x[b // G] for b in range(B)]
        xr_ = [[] for _ in range(B)]
        xh_free = [None, None]
        xta_free, xta_ready = [[], []], {}
        xtm_free = [[]]

        def norm_t(l, bs, which, XT, xt_free, ring, keep):
            p = which
            st_ops = []
            for i, b in enumerate(bs):
                o = DV(I.bn_stats(ST[p][:, i, :], X[:, b, :]), xw[b], st_free[p])
                st_ops.append(DV(I.bn_aggr(MV[p][:, i, :], ST[p][:, i, :]), o))
            o = DV(I.tensor_scalar(VE[p][:, 0, :], MV[p][:, :, 1], EPS, None, ALU.add), st_ops, ve_free[p])
            yield
            o = PO(I.tensor_tensor(VE[p][:, 1, :], VE[p][:, 0, :], half[:, 0:len(bs)], ALU.pow), o, d_half)
            yield
            nz = []
            for i, b in enumerate(bs):
                m_, r_ = MV[p][:, i, 0:1], VE[p][:, 1, i:i + 1]
                n = DV(I.tensor_scalar(XH[p][:, i, 0:128], X[:, b, 0:128], m_, r_, ALU.subtract, ALU.mult), o, xh_free[p],
                       z_xh[p])
                n = DV(I.tensor_scalar(XH[p][:, i, 128:208].rearrange("p (a c) -> p a c", c=16)[:, 0:5:2, :],
                                       X[:, b, 128:144].unsqueeze(1).to_broadcast([128, 3, 16]), m_, r_,
                                       ALU.subtract, ALU.mult))
                nz.append(n)
                xr_[b] = [n]
            st_free[p] = ve_free[p] = nz[-1]
            yield
            yield from turn(XH[p], nz, l, bs, p, XT, xt_free, ring, keep)

        st_free, ve_free = [None, None], [None, None]

        def turn(src, ready, l, bs, p, XT, xt_free, ring, keep):
            outs, tr = [], []
            F1, F2 = XF[p]
            for i, b in enumerate(bs):
                k, bk, fr = yield from ring.take()
                PE(I.transpose(bk[:, 0:128], src[:, i, 0:128], eye[:, :]), fr, ready[i], d_eye)
                o1 = F1[:, 128 * i:128 * i + 128]
                if l is None:
                    t = PE(I.transpose(bk[0:16, 128:256], src[:, i, 128:144], eye[:, :]))
                    yield
                    c1 = DV(I.tensor_copy(o1, bk[:, 0:128]), t, xf_free[p])
                    c2 = AC(I.copy(F2[0:16, 128 * i:128 * i + 128], bk[0:16, 128:256]), t, c1, xf_free[p])
                else:
                    f = 2 * p
                    t = PE(I.transpose(bk[0:80, 128:256], src[:, i, 128:208], eye[:, :]))
                    yield
                    c1 = DV(I.tensor_scalar(o1, bk[:, 0:128], MT1[l][:, f + 1, b:b + 1], MT1[l][:, f, b:b + 1],
                                            ALU.mult, ALU.add), t, xf_free[p], mod_t[l])
                    c2 = AC(I.activation(F2[:, 128 * i:128 * i + 128], bk[0:80, 128:256], ACT.Identity,
                                         bias=MT2[l][:, f, b:b + 1], scale=MT2[l][:, f + 1, b:b + 1]),
                            t, c1, xf_free[p], mod_t[l])
                tr.append(t)
                ring.give(k, c1, c2)
                outs += [c1, c2]
                yield
            xh_free[p] = tr[-1]
            if l is None:
                keep.append(outs)
                return
            h1 = AC(I.copy(XT[0][:, :], F1[:, :]), outs, xt_free)
            h2 = AC(I.copy(XT[2][:, :], F2[:, :]), outs, xt_free)
            yield
            l1 = DV(I.tensor_tensor(XT[1][:, :], F1[:, :], XT[0][:, :].bitcast(F32), ALU.subtract), h1, xt_free)
            l2 = DV(I.tensor_tensor(XT[2][64:80, :], F2[64:80, :], XT[2][64:80, :].bitcast(F32), ALU.subtract), h2)
            xf_free[p] = [l1, l2]
            keep.append([l1, l2, h2])
            keep.append(outs)

        xf_free = [None, None]

        def mm_split(o, X_, W_, m, n, swap, *w):
            for j, (x_, w_) in enumerate(((0, 0), (1, 0), (0, 1), (2, 2))):
                x, y = X_[x_][:, m], W_[w_][:, n]
                r = PE(I.matmul(o, x if swap else y, y if swap else x, start=(j == 0), stop=(j == 3)), w)
            return r

        def gates(l, bs, k, dst, ring, free):
            kb, bk, fr = yield from ring.take()
            for n, b in enumerate(bs):
                m = PE(I.matmul(bk[:, 256 * n:256 * n + C], e3[:, b:b + 1].to_broadcast([96, 128]),
                                MS[l][:, C * k:C * k + C], start=True, stop=True), fr, mod_s[l], d_e3)
            yield
            c = AC(I.copy(dst, bk[:, :].rearrange("p (n c) -> p n c", n=2)[:, 0:len(bs), 0:C]), m, free)
            ring.give(kb, c)
            return c


        def prep_att(l, u):
            p = u % 2
            keep = []
            yield from norm_t(l, range(GP * u, GP * u + GP), 0, XTA[p], xta_free[p], RA, keep)
            xta_ready[l, u] = keep[0]
            xta_free[p] = []

        abuf = {n: [None] * NW for n in ("QA", "VA", "KT", "QT", "MX")}
        cs2_free = [None]

        def att(l, b):
            u, i, p = b // GP, b % GP, (b + B * LAY.index(l)) % NW
            c0 = cst[p]
            fi, (KA_, R, CQ_, s), frf = yield from RFr.take()
            kb, bk, fr = yield from RA.take()
            m = mm_split(bk[:, 0:432], XTA[u % 2], WQ[l], slice(128 * i, 128 * i + 128),
                         slice(0, 432), True, fr, xta_ready[l, u], d_w[l])
            xta_free[u % 2].append(m)
            done["x", l, b] = m.end
            yield
            cv = AC(I.copy(VA[p][:, :, 0:HD], bk[:, 288:432].rearrange("p (h d) -> p h d", d=HD)),
                    m, abuf["VA"][p], c0[1])
            if l == 0:
                yield
                x3 = bk[:, 0:288].rearrange("p (h d) -> p h d", d=HD)
                o = DV(I.tensor_reduce(s[:, 0, :], x3, AX.X, ALU.add), m, cv, frf)
                o = DV(I.tensor_scalar(s[:, 1, :], s[:, 0, :], 1.0 / HD, None, ALU.mult), o)
                cc = DV(I.tensor_tensor(CQ_[:], x3, s[:, 1, :].unsqueeze(2).to_broadcast([128, 32, HD]),
                                                  ALU.subtract), o, frf, cv)
                o = DV(I.tensor_tensor(CS2[:], CQ_[:], CQ_[:], ALU.mult), cc, cs2_free[0])
                o = DV(I.tensor_reduce(s[:, 0, :], CS2[:], AX.X, ALU.add), o)
                cs2_free[0] = o
                o = DV(I.tensor_scalar(s[:, 2, :], s[:, 0, :], 1.0 / HD, EPS, ALU.mult, ALU.add), o)
                o = PO(I.tensor_tensor(s[:, 3, :], s[:, 2, :], half[:, :], ALU.pow), o, d_half)
                RA.give(kb, cc, cv)
                yield
                o = DV(I.tensor_tensor(CQ_[:], CQ_[:], s[:, 3, :].unsqueeze(2).to_broadcast([128, 32, HD]),
                                                 ALU.mult), o)
                m = DV(I.tensor_tensor(CQ_[:], CQ_[:], gqk[:], ALU.mult), o, d_g)
                src = CQ_[:].rearrange("p (w h) d -> p w h d", w=2)
            else:
                src = bk[:, 0:288].rearrange("p (w h d) -> p w h d", w=2, d=HD)
            qs = QA[p][:, :, 0:54].rearrange("p h (s d) -> p h s d", d=HD)
            ks = KA_[:, :, 0:54].rearrange("p h (s d) -> p h s d", d=HD)

            def bc(x, n):
                return x.unsqueeze(2).to_broadcast([128, NH, n, HD])

            hq = AC(I.copy(qs[:, :, 0:5:2, :], bc(src[:, 0], 3)), m, cv, abuf["QA"][p], c0[0])
            hk = AC(I.copy(ks[:, :, 3:6, :], bc(src[:, 1], 3)), m, frf)
            yield
            rq = DV(I.tensor_tensor(R[:, 0], src[:, 0], qs[:, :, 0, :], ALU.subtract), hk, frf)
            rk = DV(I.tensor_tensor(R[:, 1], src[:, 1], ks[:, :, 3, :], ALU.subtract), hk)
            if l != 0:
                RA.give(kb, rk, hk)
            yield
            mq = AC(I.copy(qs[:, :, 1:4:2, :], bc(R[:, 0], 2)), rq)
            mk = AC(I.copy(ks[:, :, 0:2, :], bc(R[:, 1], 2)), rk)
            yield
            lq = DV(I.tensor_tensor(qs[:, :, 5, :], R[:, 0], qs[:, :, 1, :], ALU.subtract), mq)
            lk = DV(I.tensor_tensor(ks[:, :, 2, :], R[:, 1], ks[:, :, 0, :], ALU.subtract), mk)
            z = DV(I.memset(QA[p][:, :, 54:57], 0.0), abuf["QA"][p], c0[0])

            def turn_b(src, ready, dst, name, eng, *more):
                kb2, bk2, fr2 = yield from RA.take()
                pb = bk2[:, :].bitcast(BF)
                for j in range(8):
                    t = PE(I.transpose(pb[:, 128 * j:128 * j + 128],
                                                      src[:, 2 * j:2 * j + 2, :].rearrange("p a b -> p (a b)"), eyeb[:, :]),
                           fr2, ready, d_eyeb)
                yield
                pv = pb.rearrange("p (j t) -> p j t", j=8)
                if eng == "v":
                    c = DV(I.tensor_copy(dst[:], pv), t, abuf[name][p], *more)
                else:
                    c = AC(I.copy(dst[:], pv), t, abuf[name][p], *more)
                RA.give(kb2, c)
                return t, c
            yield
            tq, cq = yield from turn_b(QA[p], [lq, z, mq, hq], QT[p], "QT", "v")
            yield
            tk, ck = yield from turn_b(KA_, [lk, mk, hk], KT[p], "KT", "a")
            RFr.give(fi, tk, lk)
            yield
            red = []
            for w in range(2):
                ks_, S, frs = yield from RS.take()
                for hh in range(8):
                    h = 8 * w + hh
                    r = 64 * (h % 2)
                    col = 512 * (h % 2) + 128 * (hh // 2)
                    m = PE(I.matmul(
                        S[:, col:col + 128], QT[p][r:r + 64, h // 2, :], KT[p][r:r + 64, h // 2, :],
                        start=True, stop=True), frs, cq, ck)
                yield
                o = DV(I.tensor_reduce(
                    MX[p][:, 0, :].rearrange("p (w j r) -> p w r j", w=2, r=2)[:, w],
                    S[:, :].rearrange("p (r j k) -> p r j k", r=2, j=4), AX.X, ALU.max, negate=True), m, abuf["MX"][p])
                RS.give(ks_, o)
                red.append(o)
                yield
            s1_last = m
            f = MX[p]
            a0 = DV(I.tensor_copy(QA[p][:, :, 54], f[:, 0, :]), red, tq)
            a1 = DV(I.tensor_tensor(f[:, 1, :], f[:, 0, :], QA[p][:, :, 54], ALU.subtract), a0)
            a2 = DV(I.tensor_copy(QA[p][:, :, 55], f[:, 1, :]), a1)
            a3 = DV(I.tensor_tensor(QA[p][:, :, 56], f[:, 1, :], QA[p][:, :, 55], ALU.subtract), a2)
            abuf["MX"][p] = a3
            abuf["QT"][p] = s1_last
            yield
            tq, cq = yield from turn_b(QA[p], [a3], QT[p], "QT", "v")
            abuf["QA"][p] = tq
            yield
            ex, ph = [], []
            for w in range(2):
                kp, Pw, frp = yield from RP.take()
                ph.append((kp, Pw))
                ks_, S, frs = yield from RS.take()
                for hh in range(8):
                    h = 8 * w + hh
                    r = 64 * (h % 2)
                    col = 512 * (h % 2) + 128 * (hh // 2)
                    m = PE(I.matmul(
                        S[:, col:col + 128], KT[p][r:r + 64, h // 2, :], QT[p][r:r + 64, h // 2, :],
                        start=True, stop=True), frs, cq)
                yield
                o = AC(I.activation(Pw[:, :], S[:, :], ACT.Exp, scale=SCALE), m, frp)
                RS.give(ks_, o)
                ex.append(o)
                yield
            abuf["KT"][p] = abuf["QT"][p] = m
            bi, (OT_, ON_, RD_, OF_, GA_), frb = yield from RBk.take()
            ko, bo, fro = yield from RA.take()
            for h in range(NH):
                w, hh = h // 8, h % 8
                col = 512 * (h % 2) + 128 * (hh // 2)
                m = PE(I.matmul(
                    bo[32 * (h % 4):32 * (h % 4) + 32, 128 * (h // 4):128 * (h // 4) + 128],
                    VA[p][:, h, :], ph[w][1][:, col:col + 128], start=True, stop=True),
                    fro, ex[w], cv)
                if h == 7:
                    RP.give(ph[0][0], m)
                    yield
            RP.give(ph[1][0], m)
            abuf["VA"][p] = m
            yield
            oc = AC(I.copy(OT_[:], bo[:, :]), m, frb)
            RA.give(ko, oc)
            yield
            ga = yield from gates(l, [b], 0, GA_[:, :].unsqueeze(1), RA, frb)
            kd, bd_, frd = yield from RA.take()
            for j in range(4):
                m = PE(I.transpose(bd_[:, 128 * j:128 * j + 128], OT_[:, 128 * j:128 * j + 128], eye[:, :]), frd, oc)
            yield
            o3 = bd_[:, :].rearrange("p (h s) -> p h s", s=32)
            r = DV(I.reciprocal(RD_[:, :], o3[:, :, HD]), m, frb)
            n = DV(I.tensor_tensor(ON_[:].rearrange("p (h d) -> p h d", d=HD), o3[:, :, 0:HD],
                                   RD_[:].unsqueeze(2).to_broadcast([128, NH, HD]), ALU.mult), r)
            RA.give(kd, n)
            yield
            kt, bt, frt = yield from RA.take()
            PE(I.transpose(bt[:, 0:128], ON_[:, 0:128], eye[:, :]), frt, n)
            m = PE(I.transpose(bt[0:16, 128:256], ON_[:, 128:144], eye[:, :]))
            yield
            c1 = DV(I.tensor_copy(OF_[0][:, :], bt[:, 0:128]), m, frb)
            c2 = AC(I.copy(OF_[1][0:16, :], bt[0:16, 128:256]), c1, frb)
            RA.give(kt, c1, c2)
            yield
            ky, by, fry = yield from RA.take()
            PE(I.matmul(by[:, 0:C], OF_[0][:, :], wp[l][0], start=True, stop=False), fry, c1, c2, d_wp[l])
            m = PE(I.matmul(by[:, 0:C], OF_[1][:, :], wp[l][1], start=False, stop=True))
            yield
            y = DV(I.tensor_tensor(GA_[:], by[:, 0:C], GA_[:, :], ALU.mult), m, ga, frb)
            RA.give(ky, y)
            yield
            xx = PO(I.tensor_tensor(X[:, b, :], X[:, b, :], GA_[:], ALU.add), y, xw[b], xr_[b])
            xw[b], xr_[b] = xx, []
            RBk.give(bi, xx, y, m)
            yield

        rt_free = [None]

        def route(l, ready, p):
            k, bk, fr = yield from RM.take()
            for i in range(G):
                PE(I.matmul(bk[:, 4 * i:4 * i + 4], XF[1][0][:, 128 * i:128 * i + 128], wg1,
                            start=True, stop=False), fr, ready, d_wp[3])
                m = PE(I.matmul(bk[:, 4 * i:4 * i + 4], XF[1][1][0:16, 128 * i:128 * i + 128],
                                wg2, start=False, stop=True))
            xf_free[1].append(m)
            yield
            R = lambda j: rt[:, j, :]
            R2 = lambda j: rt[:, j, :].rearrange("p (b e) -> p b e", e=4)
            W2 = rw[:, p, :].rearrange("p (b e) -> p b e", e=4)
            o = DV(I.tensor_copy(R(0), bk[:, 0:16]), m, rt_free[0])
            RM.give(k, o)
            mx = DV(I.tensor_reduce(rt[:, 1, 0:4], R2(0), AX.X, ALU.max), o)
            d = DV(I.tensor_tensor(R2(2), R2(0), rt[:, 1, 0:4].unsqueeze(2).to_broadcast([128, 4, 4]),
                                   ALU.subtract), mx)
            exq = AC(I.activation(R(3), R(2), ACT.Exp), d)
            r3 = lambda j: rt3[:, j, :].rearrange("p (b e f) -> p b e f", b=4, e=4)
            le = R2(0).unsqueeze(3).to_broadcast([128, 4, 4, 4])
            lf = R2(0).unsqueeze(2).to_broadcast([128, 4, 4, 4])
            g1 = DV(I.tensor_tensor(r3(0), lf, le, ALU.is_gt), o)
            g2 = DV(I.tensor_tensor(r3(1), lf, le, ALU.is_equal), o)
            g2 = DV(I.tensor_tensor(rt3[:, 1, :], rt3[:, 1, :], ltm[:], ALU.mult), g2, d_ltm)
            g2 = DV(I.tensor_tensor(rt3[:, 0, :], rt3[:, 0, :], rt3[:, 1, :], ALU.add), g1, g2)
            g2 = DV(I.tensor_reduce(R2(4), r3(0), AX.X, ALU.add), g2)
            g2 = DV(I.tensor_scalar(R(4), R(4), 1.5, None, ALU.is_lt), g2)
            yield
            g2 = DV(I.tensor_tensor(R(5), R(4), R(3), ALU.mult), g2, exq)
            s = DV(I.tensor_reduce(rt[:, 6, 0:4], R2(5), AX.X, ALU.add), g2)
            s = DV(I.reciprocal(rt[:, 7, 0:4], rt[:, 6, 0:4]), s)
            s = DV(I.tensor_tensor(W2, R2(5), rt[:, 7, 0:4].unsqueeze(2).to_broadcast([128, 4, 4]),
                                   ALU.mult), s)
            rt_free[0] = s
            yield
            return s

        def mlp(l, g):
            keep = []
            ni, XT, xfree = yield from RN.take()
            yield from norm_t(l, range(G * g, G * g + G), 1, XT, xfree, RM, keep)
            ready = keep[0]
            cw = None
            if l == 3:
                cw = yield from route(l, keep[1], g % 2)

            def up(x):
                hi, Hx, hfree = yield from RH.take()
                ev = []
                for c in range(5):
                    n = 128 if c < 4 else 64
                    k, bk, fr = yield from RM.take()
                    lo = FF * x + 128 * c
                    m = mm_split(bk[:, :], XT, WF[l], slice(0, 512), slice(lo, lo + 128), False, fr, ready, d_wf[l])
                    yield
                    bias = b1[l][0:n, 5 * x + c:5 * x + c + 1]
                    if c % 2:
                        o = AC(I.activation(Hx[0:n, c, :], bk[0:n, :], ACT.Identity, bias=bias), m, hfree)
                    else:
                        o = DV(I.tensor_scalar(Hx[0:n, c, :], bk[0:n, :], bias, None, ALU.add), m, hfree)
                    RM.give(k, o)
                    ev.append(o)
                if x == NE[l] - 1:
                    RN.give(ni, m)
                yield
                a1 = AC(I.activation(Hx[:, 0:4, :], Hx[:, 0:4, :], ACT.Gelu_apprx_tanh), ev)
                a2 = AC(I.activation(Hx[0:64, 4, :], Hx[0:64, 4, :], ACT.Gelu_apprx_tanh), ev)
                return hi, Hx, [a1, a2]

            hs = [(yield from up(0))]
            if l == 3:
                ai, acc_t, afree = yield from RMA.take()
            for x in range(NE[l]):
                if x + 1 < NE[l]:
                    hs.append((yield from up(x + 1)))
                hi, Hx, hready = hs[x]
                yield
                for hf in range(2):
                    last = x == NE[l] - 1
                    if last:
                        gi, gmt, gfree = yield from RG.take()
                        gm = yield from gates(l, range(G * g + 2 * hf, G * g + 2 * hf + 2), 1, gmt[:], RM, gfree)
                    k, bk, fr = yield from RM.take()
                    for i2 in range(2):
                        i = 2 * hf + i2
                        for c in range(5):
                            n = 128 if c < 4 else 65
                            m = PE(I.matmul(
                                bk[:, 256 * i2:256 * i2 + C], Hx[0:n, c, 128 * i:128 * i + 128], w2[l][0:n, 5 * x + c, :],
                                start=(c == 0), stop=(c == 4)), fr, hready)
                        yield
                    bs = slice(G * g + 2 * hf, G * g + 2 * hf + 2)
                    yv = bk[:, :].rearrange("p (i c) -> p i c", i=2)[:, :, 0:C]
                    if l == 3:
                        os = []
                        ma = acc_t[hf][:].rearrange("p a b -> p (a b)").rearrange("p (n c) -> p n c", n=2)
                        for i2 in range(2):
                            i = 2 * hf + i2
                            s = rw[:, g % 2, 4 * i + x:4 * i + x + 1]
                            if x == 0:
                                o = DV(I.tensor_scalar(ma[:, i2, :], yv[:, i2, :], s, None, ALU.mult), m, cw, afree)
                            else:
                                o = DV(I.scalar_tensor_tensor(ma[:, i2, :], yv[:, i2, :], s, ma[:, i2, :], ALU.mult,
                                                              ALU.add), m, acc[hf])
                            os.append(o)
                        if x == 0 and hf == 0:
                            acc = [None, None]
                        acc[hf] = os
                        RM.give(k, os)
                        if last:
                            y = DV(I.tensor_tensor(gmt[:], ma, gmt[:], ALU.mult), os, gm)
                    else:
                        y = DV(I.tensor_tensor(gmt[:], yv, gmt[:], ALU.mult), m, gm)
                        RM.give(k, y)
                    if last:
                        if l == 3 and hf == 1:
                            RMA.give(ai, y)
                        ws = [xw[b] for b in range(bs.start, bs.stop)] + [xr_[b] for b in range(bs.start, bs.stop)]
                        xx = PO(I.tensor_tensor(X[:, bs, :], X[:, bs, :], gmt[:], ALU.add), y, ws)
                        RG.give(gi, xx)
                        for b in range(bs.start, bs.stop):
                            xw[b], xr_[b] = xx, []
                    yield
                RH.give(hi, m)
            if l == 3:
                outs.append(DMA(out[G * g:G * g + G].rearrange("b t c -> t b c"), X[:, G * g:G * g + G, :],
                                [xw[b] for b in range(G * g, G * g + G)]))

        outs = []

        u_ready = []

        def qr():
            w1 = list(d_qr) + [z_sc]
            w2_ = [d_qr[1]]
            for k in range(D):
                n = C - k
                i, bk, fr = yield from RM.take()
                m = PE(I.matmul(bk[:, 0:n], eye[:, k:k + 1].to_broadcast([128, 128]),
                                                           T1[:, k:C], start=True, stop=True), fr, w1, d_eye)
                yield
                c = DV(I.tensor_copy(VS[:, 0:n], bk[:, 0:n]), m, w1, w2_)
                RM.give(i, c)
                s0 = DV(I.tensor_tensor_reduce(JK[:, 0:n], VS[:, 0:n], VS[:, 0:n], 1.0, 0.0, ALU.mult,
                                                              ALU.add, sc[:, 0:1]), c, jk_free[0])
                p0 = PO(I.tensor_tensor(sc[:, 1:2], sc[:, 0:1], half_p[:, :], ALU.pow), s0, d_half2)
                s1 = DV(I.tensor_scalar(sc[:, 2:3], VS[:, 0:1], 0.0, 2.0, ALU.is_ge, ALU.mult), c)
                s1 = DV(I.tensor_scalar(sc[:, 2:3], sc[:, 2:3], -1.0, None, ALU.add), s1)
                yield
                s1 = DV(I.tensor_tensor(sc[:, 3:4], sc[:, 1:2], sc[:, 2:3], ALU.mult), s1, p0)
                s2 = DV(I.scalar_tensor_tensor(sc[:, 4:5], VS[:, 0:1], sc[:, 3:4], sc[:, 0:1],
                                                         ALU.mult, ALU.add), s1)
                s3 = DV(I.tensor_tensor(VS[:, 0:1], VS[:, 0:1], sc[:, 3:4], ALU.add), s2)
                s2 = DV(I.reciprocal(sc[:, 5:6], sc[:, 4:5]), s2)
                t1 = DV(I.tensor_tensor_reduce(JK[:, 0:n], T1[:, k:C], VS[:, 0:n], 1.0, 0.0, ALU.mult,
                                                                   ALU.add, sc[:, 6:7]), s3, s0)
                t2 = DV(I.tensor_tensor_reduce(JK[0:80, 0:n], T2[:, k:C], VS[0:80, 0:n], 1.0, 0.0,
                                                                   ALU.mult, ALU.add, sc[0:80, 7:8]), s3, t1)
                jk_free[0] = t2
                u = DV(I.tensor_scalar(sc[:, 8:10], sc[:, 6:8], sc[:, 5:6], -1.0, ALU.mult, ALU.mult), t2, s2)
                w1 = [DV(I.scalar_tensor_tensor(T1[:, k:C], VS[:, 0:n], sc[:, 8:9], T1[:, k:C],
                                                                    ALU.mult, ALU.add), u)]
                w2_ = [DV(I.scalar_tensor_tensor(T2[:, k:C], VS[0:80, 0:n], sc[0:80, 9:10], T2[:, k:C],
                                                                     ALU.mult, ALU.add), u)]
                yield
            a = []
            for h in range(2):
                a.append(DMA(U1[0:64, 64 * h:64 * h + 64], T1[64:128, 0:64], w1))
                a.append(DMA(U1[64:128, 64 * h:64 * h + 64], T2[0:64, 0:64], w2_))
                a.append(DMA(U2[:, 64 * h:64 * h + 64], T2[64:80, 0:64], w2_))
            yield
            yield
            i, bk, fr = yield from RM.take()
            PE(I.transpose(bk[:, 0:128], U1[:, :], eye[:, :]), fr, a)
            m = PE(I.transpose(bk[:, 128:144], U2[:, :], eye[0:16, 0:16]))
            c = AC(I.copy(UT[:, :], bk[:, 0:C]), m)
            RM.give(i, c)
            u_ready.append(c)
            u_ready.extend(a)
            yield

        half_p = sb("halfp", [128, 1])
        d_half2 = PO(I.memset(half_p[:], 0.5))
        z_sc = PO(I.memset(sc[:], 0.0))
        cs_ready = []

        def rot():
            wr = []
            stg = [None, None]
            for n in range(8):
                p = n % 2
                w1_, w2s = ROT[p]
                dd = [DMA(w1_, a["rotw"][0:128, 512 * n:512 * n + 512], stg[p]),
                      DMA(w2s, a["rotw"][128:145, 512 * n:512 * n + 512], stg[p])]
                i, bk, fr = yield from RM.take()
                PE(I.matmul(bk[0:32, :], sT1[:, :], w1_, start=True, stop=False), fr, dd, sil)
                m = PE(I.matmul(bk[0:32, :], sT2[:, :], w2s, start=False, stop=True))
                stg[p] = m
                c = AC(I.copy(VR[p][:, :], bk[0:32, :]), m, wr[-2:-1])
                RM.give(i, c)
                wr.append(DMA(vsc[:, 512 * n:512 * n + 512], VR[p][:, :], c))
                yield
            vv = vsc.rearrange("(q t) (i j) -> t i q j", t=2, j=D)
            ld = []
            for t in range(2):
                ld.append(DMA(HS[64 * t:64 * t + 64, :, :], vv[t], wr))
                ld.append(DMA(BD[64 * t:64 * t + 64, :, 64 * t:64 * t + 64], vv[t], wr, z_bd))
            for _ in range(4):
                yield
            S, Cc = SC[:, :, 0, :], SC[:, :, 1, :]
            w = []
            for n in range(4):
                i, bk, fr = yield from RM.take()
                for j in range(4):
                    m = PE(I.matmul(bk[:, 64 * j:64 * j + 64], BD[:, 4 * n + j, :], eye2[:, :],
                                                               start=True, stop=True), fr, ld, d_eye2)
                o = DV(I.tensor_tensor(HS[:, 4 * n:4 * n + 4, :], HS[:, 4 * n:4 * n + 4, :],
                                                             bk[:, 0:256].rearrange("p (a b) -> p a b", a=4),
                                                             ALU.subtract), m)
                RM.give(i, o)
                w.append(o)
                yield

            def spread(n, src, scale, ready, wd):
                o = []
                for t in range(2):
                    r = slice(64 * t, 64 * t + 64)
                    o.append(AC(I.mul(BD[r, 4 * n:4 * n + 4, 64 * t:64 * t + 64],
                                                          src[r, 4 * n:4 * n + 4, :], scale), ready, wd))
                return o
            f = 2.0 ** -S_SQ
            bds, q4 = [], []
            for n in range(4):
                r = slice(4 * n, 4 * n + 4)
                s = DV(I.tensor_scalar(S[:, r, :], HS[:, r, :], f, None, ALU.mult), w[n])
                bds.append([s] + spread(n, HS, f, w[n], None))
                yield
            qs_, pre = [], []
            for n in range(4):
                r = slice(4 * n, 4 * n + 4)
                i, bk, fr = yield from RM.take()
                for j in range(4):
                    m = PE(I.matmul(bk[:, 128 * j:128 * j + 64], BD[:, 4 * n + j, :],
                                                               S[:, 4 * n + j, :], start=True, stop=True), fr, bds[n])
                bv = bk[:, :].rearrange("p (a b) -> p a b", a=4)[:, :, 0:64]
                o = AC(I.mul(HS[:, r, :], bv, -1.0), m)
                RM.give(i, o)
                qs_.append(o)
                yield
            e_ = eye2[:, :].unsqueeze(1).to_broadcast([128, 4, D])
            fin = []
            for n in range(4):
                r = slice(4 * n, 4 * n + 4)
                t0 = DV(I.tensor_scalar(Cc[:, r, :], HS[:, r, :], 1.0 / 24, None, ALU.mult), qs_[n])
                z = [AC(I.copy(BQ[64 * t:64 * t + 64, :, 64 * t:64 * t + 64],
                                                   HS[64 * t:64 * t + 64, r, :]), qs_[n], bq_free[0], z_bq)
                     for t in range(2)]
                i, bk, fr = yield from RM.take()
                for j in range(4):
                    m = PE(I.matmul(bk[:, 128 * j:128 * j + 64], BQ[:, j, :],
                                                               HS[:, 4 * n + j, :], start=True, stop=True), fr, z, t0)
                bq_free[0] = m
                bv = bk[:, :].rearrange("p (a b) -> p a b", a=4)[:, :, 0:64]
                q2 = DV(I.tensor_scalar(Q2[:, :, :], bv, 1.0 / 24, None, ALU.mult), m, q2_free[0])
                RM.give(i, q2)
                cc = DV(I.scalar_tensor_tensor(Cc[:, r, :], HS[:, r, :], 0.5, Q2[:, :, :], ALU.mult,
                                                              ALU.add), q2, t0)
                g1 = DV(I.tensor_scalar(Q2[:, :, :], Q2[:, :, :], 0.2, None, ALU.mult), cc)
                gg = DV(I.scalar_tensor_tensor(Q3[:, :, :], HS[:, r, :], 1.0 / 6, Q2[:, :, :], ALU.mult,
                                                              ALU.add), g1, q3_free[0])
                q2_free[0] = gg
                yield
                i, bk, fr = yield from RM.take()
                for j in range(4):
                    m = PE(I.matmul(bk[:, 128 * j:128 * j + 64], BD[:, 4 * n + j, :],
                                                               Q3[:, j, :], start=True, stop=True), fr, gg)
                q3_free[0] = m
                bv = bk[:, :].rearrange("p (a b) -> p a b", a=4)[:, :, 0:64]
                ss = DV(I.tensor_tensor(HS[:, r, :], S[:, r, :], bv, ALU.subtract), m)
                RM.give(i, ss)
                s2 = DV(I.tensor_copy(S[:, r, :], HS[:, r, :]), ss)
                fin.append([cc, s2] + spread(n, HS, 1.0, ss, m))
                yield
            for k in range(S_SQ):
                nxt = []
                for n in range(4):
                    r = slice(4 * n, 4 * n + 4)
                    i, bk, fr = yield from RM.take()
                    for j in range(4):
                        m = PE(I.matmul(
                            bk[:, 128 * j:128 * j + 128], BD[:, 4 * n + j, :],
                            SC[:, 4 * n + j, :, :].rearrange("p a b -> p (a b)"), start=True, stop=True), fr, fin[n])
                    bv = bk[:, :].rearrange("p (a b) -> p a b", a=4)
                    c = AC(I.mul(Cc[:, r, :], bv[:, :, 0:64], -2.0), m)
                    o = DV(I.tensor_tensor(HS[:, r, :], S[:, r, :], bv[:, :, 64:128],
                                                                 ALU.subtract), m, c)
                    RM.give(i, c, o)
                    s = DV(I.tensor_scalar(S[:, r, :], HS[:, r, :], 2.0, None, ALU.mult), o)
                    nxt.append([c, s] + (spread(n, HS, 2.0, o, m) if k < S_SQ - 1 else []))
                    yield
                fin = nxt
            o = []
            for n in range(4):
                r = slice(4 * n, 4 * n + 4)
                o.append(DV(I.tensor_tensor(HS[:, r, :], S[:, r, :], Cc[:, r, :], ALU.add), fin[n]))
            cs_ready.extend(o)
            yield

        z_bq = PO(I.memset(BQ, 0.0))
        bq_free, q2_free, q3_free = [None], [None], [None]
        RZ = Ring(q, [(ZT, WZ)])

        def rotate(g):
            keep = []
            ni, _, _ = yield from RN.take()
            yield from turn(X[:, G * g:G * g + G, :], [xw[b] for b in range(G * g, G * g + G)], None, range(G), 1, None,
                            None, RM, keep)
            k, bk, fr = yield from RM.take()
            PE(I.matmul(bk[:, :], U1[:, :], XF[1][0][:, :], start=True, stop=False), fr, keep[0], u_ready)
            m = PE(I.matmul(bk[:, :], U2[:, :], XF[1][1][0:16, :], start=False, stop=True))
            xf_free[1] = [m]
            RN.give(ni, m)
            zi, _, zfree = yield from RZ.take()
            z = AC(I.copy(ZT[:, :], bk[:, :]), m, zfree, cs_ready)
            RM.give(k, z)
            yield
            k, bk, fr = yield from RM.take()
            for i in (0, 2, 1, 3):
                b = G * g + i
                r = 64 * (b % 2)
                m = PE(I.matmul(
                    bk[r:r + 64, 128 * i:128 * i + 128], HS[r:r + 64, b // 2, :], ZT[r:r + 64, 128 * i:128 * i + 128],
                    start=True, stop=True), fr, z, cs_ready)
            wv = []
            for t in range(2):
                half_of = lambda x, t=t: x[64 * t:64 * t + 64, :].rearrange("p (a b) -> p a b", a=4)[:, t:4:2, :]
                wv.append(AC(I.copy(half_of(WZ), half_of(bk)), m))
            RM.give(k, wv)
            yield
            for t in range(2):
                k, bk, fr = yield from RM.take()
                for i2 in range(2):
                    i = 2 * i2 + t
                    m = PE(I.matmul(bk[:, 256 * i2:256 * i2 + C],
                                              WZ[64 * t:64 * t + 64, 128 * i:128 * i + 128], UT[64 * t:64 * t + 64, :],
                                              start=True, stop=True), fr, wv)
                bs = range(G * g + t, G * g + G, 2)
                xv = X[:, G * g + t:G * g + G:2, :]
                yv = bk[:, :].rearrange("p (i c) -> p i c", i=2)[:, :, 0:C]
                o = DV(I.tensor_tensor(xv, xv, yv, ALU.add), m, [xr_[b] for b in bs])
                RM.give(k, o)
                for b in bs:
                    xw[b], xr_[b] = o, []
                yield
            RZ.give(zi, m)

        def load3():
            w = [q.q[e][-1] for e in ("tensor", "scalar", "vector")]
            yield from load_att(3, w)
            yield from load_mlp(3, w)

        for _ in load_att(0):
            pass
        jobs_l = deque([(("w", 0), set(), lambda: load_mlp(0)), (("wa", 2), set(), lambda: load_att(2)),
                        (("w", 2), {("m", 0, g) for g in range(NG)}, lambda: load_mlp(2, q.q["tensor"][-1])),
                        (("w", 3), {("r", g) for g in range(NG)}, load3)])
        for _ in modulation(0, WM[0], d_mod[0], MR, MRS[0], None):
            pass
        for _ in modulation(2, WM[1], d_mod[2], MR2, MRS[1], None):
            pass
        m2q = q.q["tensor"][-1]
        d_mod[3] = [DMA(WM[1][0][:, 0:864], a["mod3"][0:128], m2q), DMA(WM[1][1][:, 0:864], a["mod3"][128:145], m2q)]
        for _ in modulation(3, WM[1], d_mod[3], MR2, MRS[1], mod_s[2] + mod_t[2]):
            pass
        ones_h = [DV(I.memset(x[64:128, 4, :], 1.0)) for x in H]
        for i in range(4):
            RP.give(i, q.q["tensor"][-1])
        RH.give(0, mod_s[0], mod_s[3], ones_h[0])
        RH.give(1, ones_h[1])

        done = {}
        pj, aj, mj = deque(), deque(), deque()
        prep = [(l, u) for l in LAY for u in range(B // GP)]
        for n, (l, u) in enumerate(prep):
            g = GP * u // G
            need = {0: set(), 2: {("r", g)}, 3: {("m", 2, g), ("w", 3)}}[l]
            prev = {("x", l0, b) for l0, v in prep[max(n - 2, 0):max(n - 1, 0)] for b in range(GP * v, GP * v + GP)}
            pj.append((("p", l, u), need | prev, lambda l=l, u=u: prep_att(l, u)))
            for b in range(GP * u, GP * u + GP):
                aj.append((("a", l, b), {("p", l, u), {0: ("p", 0, 0), 2: ("wa", 2), 3: ("w", 3)}[l]},
                           lambda l=l, b=b: att(l, b)))
        for l in LAY:
            for g in range(NG):
                mj.append((("m", l, g), {("a", l, b) for b in range(G * g, G * g + G)} | {("w", l)},
                           lambda l=l, g=g: mlp(l, g)))
            if l == 0:
                for g in range(NG):
                    mj.append((("r", g), {("m", 0, g), "qr", "rot"}, lambda g=g: rotate(g)))
        lanes = [(jobs_l, 1), (pj, 1), (aj, NW), (mj, 2), (deque([("rot", set(), rot)]), 1), (deque([("qr", set(), qr)]), 1)]
        act = []

        def admit():
            for n, (jobs, width) in enumerate(lanes):
                while jobs and jobs[0][1] <= done.keys() and sum(j[0] == n for j in act) < width:
                    name, need, make = jobs.popleft()
                    act.append([n, name, make(), max([done[x] for x in need], default=0.0)])

        admit()
        while act:
            now = q.clock["tensor"]
            j = min(act, key=lambda j: (max(j[3], now), j[3]))
            q.last = 0.0
            try:
                t = next(j[2])
            except StopIteration:
                done[j[1]] = max(q.last, j[3])
                act.remove(j)
                admit()
                continue
            if t == -1:
                j[3] = min([max(k[3], now) for k in act if k is not j]) + 1
            else:
                j[3] = max(q.last, t or 0.0, j[3])
            admit()
        assert not any(jobs for jobs, _ in lanes)

        q.put("sync", I.nop(), outs)

        q.count(sem)
        block = st.enter_context(nc.Block())
        block.sync(lambda e: q.play("sync", e))
        block.gpsimd(lambda e: q.play("gpsimd", e))
        block.scalar(lambda e: q.play("scalar", e))
        block.vector(lambda e: q.play("vector", e))
        block.tensor(lambda e: q.play("tensor", e))


def layout(inputs):
    f = np.float32
    g = {k: np.asarray(v) for k, v in inputs.items()}
    a = {"x": np.ascontiguousarray(g["x"])}
    a["condT"] = np.concatenate([g["cond_1152"].T, np.ones((1, B), f)], 0)

    def rows(w, b):
        return np.concatenate([w, b[None, :]], 0)

    names = {0: ("L0_cond_", "w_mod", "b_mod", "w_qkv", "b_qkv", "w_proj", "b_proj", "w1", "b1", "w2", "b2"),
             2: ("L2_cond_", "W_ada", "b_ada", "W_qkv", "b_qkv", "W_proj", "b_proj", "W_fc1", "b_fc1", "W_fc2", "b_fc2"),
             3: ("L3_cond_", "w_adaln", "b_adaln", "w_qkv", "b_qkv", "w_proj", "b_proj", "w1", "b1", "w2", "b2")}
    for l, (pre, *ns) in names.items():
        wm, bm, wq, bq, wp, bp, w1, b1, w2, b2 = (g[pre + n] for n in ns)
        a[f"mod{l}"] = rows(wm, bm)
        if l != 3:
            w1, b1, w2, b2 = w1[None], b1[None], w2[None], b2[None]
        n = len(w1)
        z = np.zeros((1, n * FF), f)
        m = np.concatenate([rows(wq, bq), np.concatenate([w1.transpose(1, 0, 2).reshape(C, n * FF), z], 0),
                            np.zeros((C + 1, 64), f)], 1)
        ms = np.zeros((80, m.shape[1]), f)
        ms[0:17] = ms[32:49] = m[128:145]
        ms[64:80] = m[128:144]
        a[f"main{l}"], a[f"mains{l}"] = m[0:128], ms
        gate = np.concatenate([g["L3_cond_w_gate"], np.zeros((1, 4), f)], 0) if l == 3 else np.zeros((C + 1, 4), f)
        a[f"proj{l}"] = np.concatenate([rows(wp, bp), gate], 1)
        ww = np.zeros((n, 5, 128, C), f)
        ww[:, 0:4] = w2[:, 0:512].reshape(n, 4, 128, C)
        ww[:, 4, 0:64] = w2[:, 512:576]
        ww[:, 4, 64] = b2
        bb = np.zeros((n, 5, 128), f)
        bb[:, 0:4] = b1[:, 0:512].reshape(n, 4, 128)
        bb[:, 4, 0:64] = b1[:, 512:576]
        a[f"pack{l}"] = np.concatenate([ww.reshape(n * 5, 128, C).transpose(1, 0, 2).reshape(128, -1),
                                        bb.reshape(n * 5, 128).T], 1)
    a["gqk"] = np.concatenate([np.tile(g["L0_cond_g_q"], NH), np.tile(g["L0_cond_g_k"], NH)])[None, :]
    qr1 = np.zeros((128, C), f)
    qr1[0:D] = g["L1_cond_P"].T
    qr1[64:128, 0:64] = np.eye(64, dtype=f)
    qr2 = np.zeros((80, C), f)
    qr2[:, 64:144] = np.eye(80, dtype=f)
    a["qr1"], a["qr2"] = qr1, qr2
    iu, ju = np.triu_indices(D, k=1)
    rw = np.zeros((C + 1, D, D), f)
    rw[0:C, iu, ju] = g["L1_cond_W"].T
    rw[C, iu, ju] = g["L1_cond_b"]
    a["rotw"] = rw.reshape(C + 1, D * D)
    a["eye"] = np.eye(128, dtype=f)
    a["eye2"] = np.concatenate([np.eye(64, dtype=f)] * 2, 0)
    a["e3"] = np.concatenate([np.eye(32, dtype=f)] * 3, 0)
    a["half"] = np.full((128, 32), -0.5, f)
    lt = np.zeros((4, 4, 4), f)
    for e in range(4):
        lt[:, e, 0:e] = 1.0
    a["ltm"] = np.broadcast_to(lt.reshape(1, 64), (128, 64))
    return {k: np.ascontiguousarray(v) for k, v in a.items()}


def kernel(**inputs):
    from concourse import bacc
    from concourse.bass_utils import run_bass_kernel_spmd

    nc = bacc.Bacc("TRN2", target_bir_lowering=False, num_devices=1)
    arrays, aps = {}, {}
    for k, v in layout(inputs).items():
        arrays["in_" + k] = v
        aps[k] = nc.dram_tensor("in_" + k, v.shape, mybir.dt.from_np(v.dtype), kind="ExternalInput").ap()
    out = nc.dram_tensor("out_0", (B, T, C), F32, kind="ExternalOutput").ap()
    program(nc, aps, out)
    r = run_bass_kernel_spmd(nc, [arrays], core_ids=[0])
    return r.results[0]["out_0"]
```

```python
from collections import deque
from contextlib import ExitStack

import numpy as np

import concourse.bass as bass
from concourse import mybir

F32 = mybir.dt.float32
F32R = mybir.dt.float32r
BF = mybir.dt.bfloat16
ALU = mybir.AluOpType
ACT = mybir.ActivationFunctionType
AX = mybir.AxisListType

B, T, C, NH, HD, FF, D = 32, 128, 144, 16, 9, 576, 64
G = 4
GP = 2
NG = B // G
NPAIR = B // 2
NW = 5
LEAD = {"qr": 400, "rot": 100, "a": 0, "m": 200, "p": 50, "r": 0, "w": 100, "wa": 0, "ho": 0, "mods": 200}
SGC = 144
S_SQ = 12
SCALE = HD ** -0.5
EPS = 1e-6
SEM_SPAN = 4000

SH_A, SC_A, G_A, SH_M, SC_M, G_M = range(6)


def cols(x):
    return int(np.prod(x.shape[1:]))


class I:

    @staticmethod
    def memset(*a, **k):
        return 60 + cols(a[0]), lambda e: e.memset(*a, **k)

    @staticmethod
    def tensor_scalar(*a, **k):
        return 130 + cols(a[0]), lambda e: e.tensor_scalar(*a, **k)

    @staticmethod
    def activation(*a, **k):
        return 190 + 0.7 * cols(a[0]), lambda e: e.activation(*a, **k)

    @staticmethod
    def scalar_tensor_tensor(*a, **k):
        return 130 + cols(a[0]), lambda e: e.scalar_tensor_tensor(*a, **k)

    @staticmethod
    def bn_stats(*a, **k):
        return 75 + cols(a[1]), lambda e: e.bn_stats(*a, **k)

    @staticmethod
    def dma_start(*a, **k):
        return 5000, lambda e: e.dma_start(*a, **k)

    @staticmethod
    def transpose(*a, **k):
        return 65 if a[0].dtype == BF else 150, lambda e: e.transpose(*a, **k)

    @staticmethod
    def reciprocal(*a, **k):
        return 60 + 6.4 * cols(a[0]), lambda e: e.reciprocal(*a, **k)

    @staticmethod
    def mul(*a, **k):
        return 120 + 0.7 * cols(a[0]), lambda e: e.mul(*a, **k)

    @staticmethod
    def nop(*a, **k):
        return 0, lambda e: e.nop(*a, **k)

    @staticmethod
    def bn_aggr(*a, **k):
        return 70 + cols(a[0]), lambda e: e.bn_aggr(*a, **k)

    @staticmethod
    def tensor_tensor(*a, **k):
        return 80 + cols(a[0]) if a[-1] != ALU.pow else 250 + 166 * cols(a[0]), lambda e: e.tensor_tensor(*a, **k)

    @staticmethod
    def tensor_reduce(*a, **k):
        return 70 + cols(a[1]), lambda e: e.tensor_reduce(*a, **k)

    @staticmethod
    def matmul(*a, **k):
        return 25 + cols(a[0]) * (0.42 if a[2].dtype != F32 else 2.1 if cols(a[1]) > 32 else 0.55), lambda e: e.matmul(*a, **k)

    @staticmethod
    def copy(*a, **k):
        return 120 + 0.7 * cols(a[0]), lambda e: e.copy(*a, **k)

    @staticmethod
    def tensor_tensor_reduce(*a, **k):
        return 80 + cols(a[1]), lambda e: e.tensor_tensor_reduce(*a, **k)

    @staticmethod
    def tensor_copy(*a, **k):
        return 70 + cols(a[0]) * (0.5 if a[1].dtype == BF else 1), lambda e: e.tensor_copy(*a, **k)


class Op:

    __slots__ = ("eng", "emit", "waits", "used", "at", "dma", "sem", "end")

    def __init__(self, eng, emit, waits, dma=None):
        self.eng, self.emit, self.dma = eng, emit, dma
        self.waits = waits
        self.used, self.at, self.sem = False, None, None


def flat(ws):
    for w in ws:
        if w is None:
            continue
        if isinstance(w, (list, tuple)):
            yield from flat(w)
        else:
            yield w


class Queues:

    ENG = ("tensor", "vector", "scalar", "gpsimd", "sync")
    HOP = {("tensor", "tensor"): 0, ("vector", "tensor"): 200, ("scalar", "tensor"): 240, ("gpsimd", "tensor"): 200,
           ("tensor", "vector"): 197, ("tensor", "scalar"): 197, ("vector", "gpsimd"): 155}

    def __init__(self):
        self.q = {e: [] for e in self.ENG}
        self.ndma = 0
        self.clock = {e: 0.0 for e in self.ENG}
        self.last = 0.0
        self.func = None

    def put(self, eng, emit, *waits, dma=False):
        ns, emit = emit
        ws = list(flat(waits))
        for w in ws:
            w.used = True
        op = Op(eng, emit, ws, self.ndma if dma else None)
        t = max([self.clock[eng]] + [w.end + self.HOP.get((w.eng, eng), 130) for w in ws])
        op.end = t + ns
        self.clock[eng] = t + 60 if dma else op.end
        self.last = max(self.last, op.end)
        if dma:
            self.ndma += 1
        self.q[eng].append(op)
        return op

    def count(self, sem):
        for e in self.ENG:
            n = 0
            for op in self.q[e]:
                if op.dma is not None:
                    op.sem, op.at = sem(f"d{op.dma}"), 16
                elif op.used:
                    op.sem, op.at = sem(f"{e}{n // SEM_SPAN}"), n % SEM_SPAN + 1
                    n += 1

    def play(self, name, eng):
        seen = {}
        for op in self.q[name]:
            need = {}
            for w in op.waits:
                if w.at > need.get(id(w.sem), (None, 0))[1]:
                    need[id(w.sem)] = (w.sem, w.at)
            for k, (s, v) in need.items():
                if seen.get(k, 0) < v:
                    seen[k] = v
                    eng.wait_ge(s, v)
            ins = op.emit(eng)
            if op.dma is not None:
                ins.then_inc(op.sem, 16)
            elif op.used:
                ins.then_inc(op.sem, 1)


class Ring:

    def __init__(self, q, banks):
        self.q, self.banks, self.free = q, banks, [[] for _ in banks]

    def take(self):
        while True:
            t, i = min((max([o.end for o in f], default=0.0), i) if f is not None else (np.inf, i)
                       for i, f in enumerate(self.free))
            if t < np.inf:
                w, self.free[i] = self.free[i], None
                if t > self.q.clock["tensor"]:
                    yield t
                return i, self.banks[i], w
            yield -1

    def give(self, i, *ops):
        self.free[i] = list(flat(ops))


def program(nc, a, out):
    q = Queues()
    st = ExitStack()
    with st:
        def sb(name, shape, dt=F32):
            return st.enter_context(nc.sbuf_tensor("s_" + name, shape, dt))

        def pst(name, shape, dt=F32):
            return st.enter_context(nc.psum_tensor("p_" + name, shape, dt))

        sems = {}

        def sem(name):
            if name not in sems:
                sems[name] = st.enter_context(nc.semaphore("m_" + name))
            return sems[name]

        PE = lambda f, *w: q.put("tensor", f, *w)
        DV = lambda f, *w: q.put("vector", f, *w)
        AC = lambda f, *w: q.put("scalar", f, *w)
        PO = lambda f, *w: q.put("gpsimd", f, *w)
        DMA = lambda o, i, *w: q.put("sync", I.dma_start(o, i), *w, dma=True)

        LAY = (0, 2, 3)
        NE = {0: 1, 2: 1, 3: 4}

        X = sb("X", [128, B, C])
        eye = sb("eye", [128, 128])
        eyeb = sb("eyeb", [128, 128], BF)
        e3 = sb("e3", [96, 32], BF)
        ltm = sb("ltm", [128, 64])
        half = sb("half", [128, 32])
        WQ, WF, wp, packC, packP, w2, b1 = {}, {}, {}, {}, {}, {}, {}
        FCOLS = {l: NE[l] * FF + 64 for l in LAY}
        PC = C + 4
        for l in LAY:
            n = NE[l]
            if l == 2:
                packC[l] = packC[0]
            else:
                if l == 0:
                    packC[l] = sb("pC0", [128, 725])
            packP[l] = (sb(f"pP1{l}", [128, PC]), sb(f"pP2{l}", [17, PC]))
            wp[l] = packP[l][0][:, 0:C], packP[l][1][:, 0:C]
            if l != 3:
                w2[l] = packC[l][:, 0:720].rearrange("p (k c) -> p k c", c=C)
                b1[l] = packC[l][:, 720:]
        wg1, wg2 = packP[3][0][:, C:PC], packP[3][1][0:16, C:PC]
        with ExitStack() as early:
            def eb(name, shape):
                return early.enter_context(nc.sbuf_tensor("s_" + name, shape, F32))
            SC = eb("SC", [128, NPAIR, 2, D])[:, :, :, :]
            BD = eb("BD", [128, NPAIR, 128])[:, :, :]
            BQ = eb("BQ", [128, 4, 128])[:, :, :]
            RW1 = [eb(f"RW1{i}", [128, 512]) for i in range(2)]
            RW2 = [eb(f"RW2{i}", [128, 512]) for i in range(2)]
            ROT = [(RW1[i][:, :], RW2[i][0:17, :]) for i in range(2)]
            VR = [eb(f"VR{i}", [32, 512])[:, :] for i in range(2)]
            HS = eb("HS", [128, NPAIR, D])
            CS2 = eb("CS2", [128, 32, HD])
            MRS = [eb(f"MRS{i}", [32, 4, 80]) for i in range(2)]
            condT1, condT2 = eb("cT1", [128, B]), eb("cT2", [17, B])
            ex1, ex2 = eb("ex1", [128, B]), eb("ex2", [16, B])
            sT1, sT2 = eb("sT1", [128, B]), eb("sT2", [17, B])
            eye2, e3f, gqk = eb("eye2", [128, 64]), eb("e3f", [96, 32]), eb("gqk", [128, 32, HD])
            U1, U2, UT = eb("U1", [128, 128]), eb("U2", [16, 128]), eb("UT", [128, C])
            T1, T2 = eb("T1", [128, C]), eb("T2", [80, C])
            VS, sc, JK = eb("VS", [128, C]), eb("scq", [128, 16]), eb("JK", [128, C])
            ZT, WZ = RW1
            Q2, Q3 = (RW2[i][:, 0:4 * D].rearrange("p (a b) -> p a b", a=4) for i in range(2))
        def split_tiles(name, n, width):
            return tuple(sb(f"{name}{x}{n}", [80 if x == "s" else 128, width], F32R) for x in "hls")

        for l in (3, 0):
            if l == 3:
                packC[3] = sb("pC3", [128, 4 * 725])
                w2[3] = packC[3][:, 0:2880].rearrange("p (k c) -> p k c", c=C)
                b1[3] = packC[3][:, 2880:]
            WF[l] = split_tiles("WF", l, FCOLS[l])
            WQ[l] = split_tiles("WQ", l, 432)
        WQ[2], WF[2] = split_tiles("WQ", 2, 432), WF[0]
        SG, SGS = sb("SG", [128, 2, SGC]), sb("SGS", [80, 2, SGC])
        MT1 = {l: sb(f"MT1{l}", [128, 4, B]) for l in LAY}
        MT2 = {l: sb(f"MT2{l}", [80, 4, B]) for l in LAY}
        MS = {l: sb(f"MS{l}", [96, 2 * C], BF) for l in LAY}

        SLOT = [(sb(f"QA{i}", [128, NH, 64], BF)[:, :, :], sb(f"VA{i}", [128, NH, 32])[:, :, :],
                 sb(f"KT{i}", [128, 8, 128], BF)[:, :, :], sb(f"QT{i}", [128, 8, 128], BF)[:, :, :],
                 sb(f"MX{i}", [128, 2, NH])[:, :, :]) for i in range(NW - 1)]
        KA = [sb(f"KA{i}", [128, NH, 64], BF) for i in range(2)]
        RQ = [sb(f"RQ{i}", [128, 2, NH, HD]) for i in range(2)]
        CQ = [sb(f"CQ{i}", [128, 32, HD]) for i in range(2)]
        s32 = [sb(f"s32{i}", [128, 4, 32]) for i in range(2)]
        Pm = [sb(f"Pm{i}", [128, 1024]) for i in range(4)]
        RP = Ring(q, Pm)
        OT = [sb(f"OT{i}", [128, 512]) for i in range(2)]
        ON = [sb(f"ON{i}", [128, C]) for i in range(2)]
        RD = [sb(f"RD{i}", [128, NH]) for i in range(2)]
        OF = [(sb(f"OF1{i}", [128, 128]), sb(f"OF2{i}", [17, 128])) for i in range(2)]
        GA = [sb(f"GA{i}", [128, C]) for i in range(2)]
        RFr = Ring(q, [(KA[i], RQ[i], CQ[i], s32[i]) for i in range(2)])
        RBk = Ring(q, [(OT[i], ON[i], RD[i], OF[i], GA[i]) for i in range(2)])
        GM = [sb(f"GM{i}", [128, 2, C]) for i in range(2)]
        XTA = [split_tiles("XA", i, 128 * GP) for i in range(2)]
        XTM = split_tiles("XM", 0, 512)
        XF = [(sb(f"XF1{i}", [128, 128 * n]), sb(f"XF2{i}", [80, 128 * n])) for i, n in enumerate((GP, G))]
        XH = [sb(f"XH{i}", [128, n, 208]) for i, n in enumerate((GP, G))]
        ST = [sb(f"ST{i}", [128, G, 6]) for i in range(2)]
        MV = [sb(f"MV{i}", [128, n, 2]) for i, n in enumerate((GP, G))]
        VE = [sb(f"VE{i}", [128, 2, n]) for i, n in enumerate((GP, G))]
        H = [sb(f"H{i}", [128, 5, 512]) for i in range(2)]
        hf1 = H[1][:, :, :].rearrange("p a b -> p (a b)")
        SLOT.append((hf1[:, 0:512].bitcast(BF).rearrange("p (a b) -> p a b", a=NH),
                     hf1[:, 512:1024].rearrange("p (a b) -> p a b", a=NH),
                     hf1[:, 1024:1536].bitcast(BF).rearrange("p (a b) -> p a b", a=8),
                     hf1[:, 1536:2048].bitcast(BF).rearrange("p (a b) -> p a b", a=8),
                     hf1[:, 2048:2080].rearrange("p (a b) -> p a b", a=2)))
        MA = [CQ[n // 2][:].rearrange("p a b -> p (a b)")[:, C * (n % 2):C * (n % 2) + C] for n in range(4)]
        rt = sb("rt", [128, 8, 16])
        rw = sb("rw", [128, 2, 16])
        rt3 = sb("rt3", [128, 2, 64])
        WM = [(Pm[2 * i][:, :], Pm[2 * i + 1][0:17, :]) for i in range(2)]
        MR = H[0][0:32, 0:2, :].rearrange("p a b -> p (a b)")
        MR2 = H[0][0:32, 2:4, :].rearrange("p a b -> p (a b)")

        SB = [pst(f"S{i}", [128, 1024]) for i in range(2)]
        bank = [pst(f"B{i}", [128, 512]) for i in range(4)]
        RS = Ring(q, SB)
        RA = Ring(q, bank)
        RM = RA
        RH = Ring(q, H)
        RSL = {2: Ring(q, SLOT), 3: Ring(q, SLOT[0:NW - 1])}
        RSL[0] = RSL[2]
        RN = Ring(q, [XTM])
        RMA = Ring(q, [CQ])
        RG = Ring(q, GM)

        vsc = nc.dram_tensor("vscratch", (B, 4096), F32, kind="Internal").ap()

        d_cond = [DMA(condT1[:], a["condT"][0:128]), DMA(condT2[:], a["condT"][128:145])]
        d_mod = {}
        d_eye = DMA(eye[:], a["eye"])
        for j, l in enumerate((0,)):
            w = WM[j]
            d_mod[l] = [DMA(w[0][:, 0:864], a[f"mod{l}"][0:128]), DMA(w[1][:, 0:864], a[f"mod{l}"][128:145])]
        d_x = []
        xr = a["x"].rearrange("(g b) t c -> g t b c", b=G)
        d_x.append(DMA(X[:, 0:G, :], xr[0]))
        d_eyeb = DV(I.tensor_copy(eyeb[:], eye[:]), d_eye)
        d_e3 = DV(I.tensor_copy(e3[:], e3f[:]), DMA(e3f[:], a["e3"]))
        d_half = DMA(half[:], a["half"])
        d_w = {}
        d_g = DMA(gqk[:], a["gqk"].rearrange("a (h d) -> a h d", d=HD).to_broadcast([128, 32, HD]))
        d_qr = [DMA(T1[:], a["qr1"]), DMA(T2[:], a["qr2"])]
        d_mod[2] = [DMA(WM[1][0][:, 0:864], a["mod2"][0:128]), DMA(WM[1][1][:, 0:864], a["mod2"][128:145])]
        for g in range(1, NG):
            d_x.append(DMA(X[:, G * g:G * g + G, :], xr[g]))
        d_eye2 = DMA(eye2[:], a["eye2"])
        d_ltm = DMA(ltm[:], a["ltm"])

        sg_free = [None, None]

        def load_split(W_, l, lo, width, *w):
            ops = []
            for c0 in range(0, width, SGC):
                k, r = nstage[0] % 2, slice(c0, min(c0 + SGC, width))
                nstage[0] += 1
                c = r.stop - c0
                d1 = DMA(SG[:, k, 0:c], a[f"main{l}"][0:128, lo + c0:lo + c0 + c], sg_free[k])
                d2 = DMA(SGS[:, k, 0:c], a[f"mains{l}"][:, lo + c0:lo + c0 + c], sg_free[k])
                if l == 0 and lo + c0 < 2 * C:
                    for n, d in ((128, SG), (80, SGS)):
                        v = d[:, k, :].rearrange("p (h d) -> p h d", d=HD)
                        t = JK[0:n, 0:NH]
                        o = DV(I.tensor_reduce(t, v, AX.X, ALU.add), d1, d2, jk_free[0])
                        o = DV(I.tensor_scalar(t, t, 1.0 / HD, None, ALU.mult), o)
                        o = DV(I.tensor_tensor(v, v, t.unsqueeze(2).to_broadcast([n, NH, HD]), ALU.subtract), o)
                        jk_free[0] = o
                    d1 = d2 = o
                h1 = AC(I.copy(W_[0][:, r], SG[:, k, 0:c]), d1, w)
                h2 = AC(I.copy(W_[2][:, r], SGS[:, k, 0:c]), d2, w)
                l1 = DV(I.tensor_tensor(W_[1][:, r], SG[:, k, 0:c], W_[0][:, r].bitcast(F32), ALU.subtract), h1)
                l2 = DV(I.tensor_tensor(W_[2][32:49, r], SGS[32:49, k, 0:c], W_[2][32:49, r].bitcast(F32), ALU.subtract),
                        h2)
                sg_free[k] = [h1, h2, l1, l2]
                ops += [l1, l2, h2]
                yield
            return ops

        nstage, jk_free = [0], [None]

        def load_att(l, *w):
            d_p = [DMA(packP[l][0][:], a[f"proj{l}"][0:128], w), DMA(packP[l][1][:], a[f"proj{l}"][128:145], w)]
            d_w[l] = yield from load_split(WQ[l], l, 0, 432, w)
            d_wp[l] = d_p

        def load_mlp(l, *w):
            d_c = DMA(packC[l][:], a[f"pack{l}"], w)
            o = yield from load_split(WF[l], l, 432, FCOLS[l], w)
            d_wf[l] = [d_c, o]

        d_wp, d_wf = {}, {}

        for i, (QA, VA, _, _, _) in enumerate(SLOT):
            m1 = PO(I.memset(QA, 0.0))
            m3 = PO(I.memset(VA, 0.0))
            RSL[2].give(i, m1, PO(I.memset(VA[:, :, HD:HD + 1], 1.0), m3))
            if i < NW - 1:
                RSL[3].free[i] = None
        RH.free[1] = None
        for i in range(2):
            m2 = PO(I.memset(KA[i][:], 0.0))
            RFr.give(i, PO(I.memset(KA[i][:, :, 54:57], 1.0), m2))
            RBk.give(i, DV(I.memset(OF[i][1][:], 1.0)))
        z_xh = [PO(I.memset(XH[i][:], 0.0)) for i in range(2)]
        z_mrs = []
        for i in range(2):
            o = DV(I.memset(MRS[i][:], 0.0))
            z_mrs.append(DV(I.memset(MRS[i][:, 0:4:2, 16:49:32], 1.0), o))
        ones_h = None
        ones_s = DV(I.memset(sT2[:], 1.0))
        z_bd = PO(I.memset(BD, 0.0))

        sil = []
        for cT, ex, sT, n, dd in ((condT1, ex1, sT1, 128, d_cond[0]), (condT2, ex2, sT2, 16, d_cond[1])):
            o = AC(I.activation(ex[0:n, :], cT[0:n, :], ACT.Exp, scale=-1.0), dd)
            o = DV(I.tensor_scalar(ex[0:n, :], ex[0:n, :], 1.0, None, ALU.add), o)
            o = DV(I.reciprocal(ex[0:n, :], ex[0:n, :]), o)
            sil.append(DV(I.tensor_tensor(sT[0:n, :], ex[0:n, :], cT[0:n, :], ALU.mult),
                          o, ones_s))

        mod_t, mod_s = {}, {}

        def modulation(l, w, dw, mr, mrs, rwait):
            cp = []
            for hf in range(2):
                i, bk, fr = yield from RM.take()
                PE(I.matmul(bk[0:32, 0:432], sT1[:, :], w[0][:, 432 * hf:432 * hf + 432],
                                                    start=True, stop=False), fr, sil, dw)
                m = PE(I.matmul(bk[0:32, 0:432], sT2[:, :], w[1][:, 432 * hf:432 * hf + 432],
                                                        start=False, stop=True))
                c = AC(I.copy(mr[:, 432 * hf:432 * hf + 432], bk[0:32, 0:432]), m, rwait)
                RM.give(i, c)
                cp.append(c)
            yield
            rs = []
            for k, kind in enumerate((SH_A, SC_A, SH_M, SC_M)):
                rs.append(DV(I.tensor_copy(mrs[:, k, :].rearrange("p (a c) -> p a c", c=16)[:, 0:5:2, :],
                                           mr[:, C * kind + 128:C * kind + 144].unsqueeze(1).to_broadcast([32, 3, 16])),
                             cp, z_mrs, rwait))
            i, bk, fr = yield from RM.take()
            for k, kind in enumerate((SH_A, SC_A, SH_M, SC_M)):
                PE(I.transpose(bk[:, 64 * k:64 * k + 32], mr[:, C * kind:C * kind + 128],
                                                                eye[0:32, 0:32]), fr, cp, d_eye)
                t = PE(I.transpose(bk[0:80, 64 * k + 32:64 * k + 64], mrs[:, k, :], eye[0:32, 0:32]), rs)
            bv = bk[:, 0:256].rearrange("p (k c) -> p k c", k=4)
            e1 = DV(I.tensor_copy(MT1[l][:, :, :], bv[:, :, 0:32]), t)
            e2 = DV(I.tensor_copy(MT2[l][:, :, :], bv[0:80, :, 32:64]), t)
            s1 = DV(I.tensor_scalar(MT1[l][:, 1:4:2, :], MT1[l][:, 1:4:2, :], 1.0, None, ALU.add), e1)
            s2 = DV(I.tensor_scalar(MT2[l][:, 1:4:2, :], MT2[l][:, 1:4:2, :], 1.0, None, ALU.add), e2)
            RM.give(i, e1, e2)
            mod_t[l] = [s1, s2]
            yield
            last = []
            for k, kind in enumerate((G_A, G_M)):
                src = mr[:, C * kind:C * kind + C]
                dst = [MS[l][32 * j:32 * j + 32, C * k:C * k + C] for j in range(3)]
                h = DV(I.tensor_copy(dst[0], src), cp)
                r = DV(I.tensor_tensor(src, src, dst[0], ALU.subtract), h)
                m = DV(I.tensor_copy(dst[1], src), r)
                mm = DV(I.tensor_copy(mr[:, 864:864 + C], dst[1]), m, r)
                r = DV(I.tensor_tensor(src, src, mr[:, 864:864 + C], ALU.subtract), mm)
                last.append(DV(I.tensor_copy(dst[2], src), r))
            mod_s[l] = last
            yield


        xw = [d_x[b // G] for b in range(B)]
        xr_ = [[] for _ in range(B)]
        xh_free = [None, None]
        xta_free, xta_ready = [[], []], {}
        xtm_free = [[]]

        def norm_t(l, bs, which, XT, xt_free, ring, keep):
            p = which
            st_ops = []
            for i, b in enumerate(bs):
                o = DV(I.bn_stats(ST[p][:, i, :], X[:, b, :]), xw[b], st_free[p])
                st_ops.append(DV(I.bn_aggr(MV[p][:, i, :], ST[p][:, i, :]), o))
            yield
            o = DV(I.tensor_scalar(VE[p][:, 0, :], MV[p][:, :, 1], EPS, None, ALU.add), st_ops, ve_free[p])
            yield
            o = PO(I.tensor_tensor(VE[p][:, 1, :], VE[p][:, 0, :], half[:, 0:len(bs)], ALU.pow), o, d_half)
            yield
            nz = []
            for i, b in enumerate(bs):
                m_, r_ = MV[p][:, i, 0:1], VE[p][:, 1, i:i + 1]
                n = DV(I.tensor_scalar(XH[p][:, i, 0:128], X[:, b, 0:128], m_, r_, ALU.subtract, ALU.mult), o, xh_free[p],
                       z_xh[p])
                n = DV(I.tensor_scalar(XH[p][:, i, 128:208].rearrange("p (a c) -> p a c", c=16)[:, 0:5:2, :],
                                       X[:, b, 128:144].unsqueeze(1).to_broadcast([128, 3, 16]), m_, r_,
                                       ALU.subtract, ALU.mult))
                nz.append(n)
                xr_[b] = [n]
            st_free[p] = ve_free[p] = nz[-1]
            yield
            yield from turn(XH[p], nz, l, bs, p, XT, xt_free, ring, keep)

        st_free, ve_free = [None, None], [None, None]

        def turn(src, ready, l, bs, p, XT, xt_free, ring, keep):
            outs, tr = [], []
            F1, F2 = XF[p]
            for i, b in enumerate(bs):
                k, bk, fr = yield from ring.take()
                PE(I.transpose(bk[:, 0:128], src[:, i, 0:128], eye[:, :]), fr, ready[i], d_eye)
                o1 = F1[:, 128 * i:128 * i + 128]
                if l is None:
                    t = PE(I.transpose(bk[0:16, 128:256], src[:, i, 128:144], eye[:, :]))
                    yield
                    c1 = DV(I.tensor_copy(o1, bk[:, 0:128]), t, xf_free[p])
                    c2 = AC(I.copy(F2[0:16, 128 * i:128 * i + 128], bk[0:16, 128:256]), t, c1, xf_free[p])
                else:
                    f = 2 * p
                    t = PE(I.transpose(bk[0:80, 128:256], src[:, i, 128:208], eye[:, :]))
                    yield
                    if l == 0:
                        c1 = AC(I.activation(o1, bk[:, 0:128], ACT.Identity, bias=MT1[l][:, f, b:b + 1],
                                             scale=MT1[l][:, f + 1, b:b + 1]), t, xf_free[p], mod_t[l])
                    else:
                        c1 = DV(I.tensor_scalar(o1, bk[:, 0:128], MT1[l][:, f + 1, b:b + 1], MT1[l][:, f, b:b + 1],
                                                ALU.mult, ALU.add), t, xf_free[p], mod_t[l])
                    c2 = AC(I.activation(F2[:, 128 * i:128 * i + 128], bk[0:80, 128:256], ACT.Identity,
                                         bias=MT2[l][:, f, b:b + 1], scale=MT2[l][:, f + 1, b:b + 1]),
                            t, c1, xf_free[p], mod_t[l])
                tr.append(t)
                ring.give(k, c1, c2)
                outs += [c1, c2]
                yield
            xh_free[p] = tr[-1]
            if l is None:
                keep.append(outs)
                return
            h1 = AC(I.copy(XT[0][:, :], F1[:, :]), outs, xt_free)
            h2 = AC(I.copy(XT[2][:, :], F2[:, :]), outs, xt_free)
            yield
            l1 = DV(I.tensor_tensor(XT[1][:, :], F1[:, :], XT[0][:, :].bitcast(F32), ALU.subtract), h1, xt_free)
            l2 = DV(I.tensor_tensor(XT[2][64:80, :], F2[64:80, :], XT[2][64:80, :].bitcast(F32), ALU.subtract), h2)
            xf_free[p] = [l1, l2]
            keep.append([l1, l2, h2])
            keep.append(outs)

        xf_free = [None, None]

        def mm_split(o, X_, W_, m, n, swap, *w):
            for j, (x_, w_) in enumerate(((0, 0), (1, 0), (0, 1), (2, 2))):
                x, y = X_[x_][:, m], W_[w_][:, n]
                r = PE(I.matmul(o, x if swap else y, y if swap else x, start=(j == 0), stop=(j == 3)), w)
            return r

        def gates(l, bs, k, dst, ring, free):
            kb, bk, fr = yield from ring.take()
            for n, b in enumerate(bs):
                m = PE(I.matmul(bk[:, 256 * n:256 * n + C], e3[:, b:b + 1].to_broadcast([96, 128]),
                                MS[l][:, C * k:C * k + C], start=True, stop=True), fr, mod_s[l], d_e3)
            yield
            c = AC(I.copy(dst, bk[:, :].rearrange("p (n c) -> p n c", n=2)[:, 0:len(bs), 0:C]), m, free)
            ring.give(kb, c)
            return c


        def prep_att(l, u):
            p = u % 2
            keep = []
            yield from norm_t(l, range(GP * u, GP * u + GP), 0, XTA[p], xta_free[p], RA, keep)
            xta_ready[l, u] = keep[0]
            xta_free[p] = []

        RC = Ring(q, [CS2])

        def att(l, b):
            u, i = b // GP, b % GP
            si, (QA, VA, KT, QT, MX), slot_free = yield from RSL[l].take()
            done["s", l, b] = q.clock["tensor"]
            fi, (KA_, R, CQ_, s), frf = yield from RFr.take()
            kb, bk, fr = yield from RA.take()
            m = mm_split(bk[:, 0:432], XTA[u % 2], WQ[l], slice(128 * i, 128 * i + 128),
                         slice(0, 432), True, fr, xta_ready[l, u], d_w[l])
            xta_free[u % 2].append(m)
            done["x", l, b] = m.end
            yield
            cv = AC(I.copy(VA[:, :, 0:HD], bk[:, 288:432].rearrange("p (h d) -> p h d", d=HD)),
                    m, slot_free)
            if l == 0:
                yield
                x3 = bk[:, 0:288].rearrange("p (h d) -> p h d", d=HD)
                cc = AC(I.copy(CQ_[:], x3), m, frf)
                RA.give(kb, cc, cv)
                yield
                ci, _, cf = yield from RC.take()
                o = DV(I.tensor_tensor(CS2[:], CQ_[:], CQ_[:], ALU.mult), cc, cf)
                yield
                o = DV(I.tensor_reduce(s[:, 0, :], CS2[:], AX.X, ALU.add), o, frf)
                RC.give(ci, o)
                yield
                o = DV(I.tensor_scalar(s[:, 2, :], s[:, 0, :], 1.0 / HD, EPS, ALU.mult, ALU.add), o)
                o = PO(I.tensor_tensor(s[:, 3, :], s[:, 2, :], half[:, :], ALU.pow), o, d_half)
                yield
                o = DV(I.tensor_tensor(CQ_[:], CQ_[:], s[:, 3, :].unsqueeze(2).to_broadcast([128, 32, HD]),
                                       ALU.mult), o, frf)
                yield
                m = DV(I.tensor_tensor(CQ_[:], CQ_[:], gqk[:], ALU.mult), o, d_g)
                src = CQ_[:].rearrange("p (w h) d -> p w h d", w=2)
            else:
                src = bk[:, 0:288].rearrange("p (w h d) -> p w h d", w=2, d=HD)
            qs = QA[:, :, 0:54].rearrange("p h (s d) -> p h s d", d=HD)
            ks = KA_[:, :, 0:54].rearrange("p h (s d) -> p h s d", d=HD)

            def bc(x, n):
                return x.unsqueeze(2).to_broadcast([128, NH, n, HD])

            hq = AC(I.copy(qs[:, :, 0:5:2, :], bc(src[:, 0], 3)), m, cv, slot_free)
            hk = AC(I.copy(ks[:, :, 3:6, :], bc(src[:, 1], 3)), m, frf)
            yield
            rq = DV(I.tensor_tensor(R[:, 0], src[:, 0], qs[:, :, 0, :], ALU.subtract), hk, frf)
            rk = DV(I.tensor_tensor(R[:, 1], src[:, 1], ks[:, :, 3, :], ALU.subtract), hk)
            if l != 0:
                RA.give(kb, rk, hk)
            yield
            mq = AC(I.copy(qs[:, :, 1:4:2, :], bc(R[:, 0], 2)), rq)
            mk = AC(I.copy(ks[:, :, 0:2, :], bc(R[:, 1], 2)), rk)
            yield
            lq = DV(I.tensor_tensor(qs[:, :, 5, :], R[:, 0], qs[:, :, 1, :], ALU.subtract), mq)
            lk = DV(I.tensor_tensor(ks[:, :, 2, :], R[:, 1], ks[:, :, 0, :], ALU.subtract), mk)
            z = DV(I.memset(QA[:, :, 54:57], 0.0), slot_free)

            def turn_b(src, ready, dst, eng, *more):
                kb2, bk2, fr2 = yield from RA.take()
                pb = bk2[:, :].bitcast(BF)
                for j in range(8):
                    t = PE(I.transpose(pb[:, 128 * j:128 * j + 128],
                                                      src[:, 2 * j:2 * j + 2, :].rearrange("p a b -> p (a b)"), eyeb[:, :]),
                           fr2, ready, d_eyeb)
                yield
                pv = pb.rearrange("p (j t) -> p j t", j=8)
                if eng == "v":
                    c = DV(I.tensor_copy(dst, pv), t, *more)
                else:
                    c = AC(I.copy(dst, pv), t, *more)
                RA.give(kb2, c)
                return t, c
            yield
            tq, cq = yield from turn_b(QA, [lq, z, mq, hq], QT, "v", slot_free)
            yield
            tk, ck = yield from turn_b(KA_, [lk, mk, hk], KT, "a", slot_free)
            RFr.give(fi, tk, lk)
            yield
            red = []
            for w in range(2):
                ks_, S, frs = yield from RS.take()
                for hh in range(8):
                    h = 8 * w + hh
                    r = 64 * (h % 2)
                    col = 512 * (h % 2) + 128 * (hh // 2)
                    m = PE(I.matmul(
                        S[:, col:col + 128], QT[r:r + 64, h // 2, :], KT[r:r + 64, h // 2, :],
                        start=True, stop=True), frs, cq, ck)
                yield
                o = DV(I.tensor_reduce(
                    MX[:, 0, :].rearrange("p (w j r) -> p w r j", w=2, r=2)[:, w],
                    S[:, :].rearrange("p (r j k) -> p r j k", r=2, j=4), AX.X, ALU.max, negate=True), m, slot_free)
                RS.give(ks_, o)
                red.append(o)
                yield
            s1_last = m
            f = MX
            a0 = DV(I.tensor_copy(QA[:, :, 54], f[:, 0, :]), red, tq)
            yield
            a1 = DV(I.tensor_tensor(f[:, 1, :], f[:, 0, :], QA[:, :, 54], ALU.subtract), a0)
            yield
            a2 = DV(I.tensor_copy(QA[:, :, 55], f[:, 1, :]), a1)
            yield
            a3 = DV(I.tensor_tensor(QA[:, :, 56], f[:, 1, :], QA[:, :, 55], ALU.subtract), a2)
            yield
            tq, cq = yield from turn_b(QA, [a3], QT, "a" if l == 0 else "v", s1_last)
            yield
            ex, ph = [], []
            for w in range(2):
                kp, Pw, frp = yield from RP.take()
                ph.append((kp, Pw))
                ks_, S, frs = yield from RS.take()
                for hh in range(8):
                    h = 8 * w + hh
                    r = 64 * (h % 2)
                    col = 512 * (h % 2) + 128 * (hh // 2)
                    m = PE(I.matmul(
                        S[:, col:col + 128], KT[r:r + 64, h // 2, :], QT[r:r + 64, h // 2, :],
                        start=True, stop=True), frs, cq)
                yield
                o = AC(I.activation(Pw[:, :], S[:, :], ACT.Exp, scale=SCALE), m, frp)
                RS.give(ks_, o)
                ex.append(o)
                yield
            bi, (OT_, ON_, RD_, OF_, GA_), frb = yield from RBk.take()
            ko, bo, fro = yield from RA.take()
            for h in range(NH):
                w, hh = h // 8, h % 8
                col = 512 * (h % 2) + 128 * (hh // 2)
                m = PE(I.matmul(
                    bo[32 * (h % 4):32 * (h % 4) + 32, 128 * (h // 4):128 * (h // 4) + 128],
                    VA[:, h, :], ph[w][1][:, col:col + 128], start=True, stop=True),
                    fro, ex[w], cv)
                if h == 7:
                    RP.give(ph[0][0], m)
                    yield
            RP.give(ph[1][0], m)
            RSL[l if si < NW - 1 else 2].give(si, m)
            yield
            oc = AC(I.copy(OT_[:], bo[:, :]), m, frb)
            RA.give(ko, oc)
            yield
            ga = yield from gates(l, [b], 0, GA_[:, :].unsqueeze(1), RA, frb)
            kd, bd_, frd = yield from RA.take()
            for j in range(4):
                m = PE(I.transpose(bd_[:, 128 * j:128 * j + 128], OT_[:, 128 * j:128 * j + 128], eye[:, :]), frd, oc)
            yield
            o3 = bd_[:, :].rearrange("p (h s) -> p h s", s=32)
            r = DV(I.reciprocal(RD_[:, :], o3[:, :, HD]), m, frb)
            yield
            n = DV(I.tensor_tensor(ON_[:].rearrange("p (h d) -> p h d", d=HD), o3[:, :, 0:HD],
                                   RD_[:].unsqueeze(2).to_broadcast([128, NH, HD]), ALU.mult), r)
            RA.give(kd, n)
            yield
            kt, bt, frt = yield from RA.take()
            PE(I.transpose(bt[:, 0:128], ON_[:, 0:128], eye[:, :]), frt, n)
            m = PE(I.transpose(bt[0:16, 128:256], ON_[:, 128:144], eye[:, :]))
            yield
            c1 = DV(I.tensor_copy(OF_[0][:, :], bt[:, 0:128]), m, frb)
            c2 = AC(I.copy(OF_[1][0:16, :], bt[0:16, 128:256]), c1, frb)
            RA.give(kt, c1, c2)
            yield
            ky, by, fry = yield from RA.take()
            PE(I.matmul(by[:, 0:C], OF_[0][:, :], wp[l][0], start=True, stop=False), fry, c1, c2, d_wp[l])
            m = PE(I.matmul(by[:, 0:C], OF_[1][:, :], wp[l][1], start=False, stop=True))
            yield
            y = DV(I.tensor_tensor(GA_[:], by[:, 0:C], GA_[:, :], ALU.mult), m, ga, frb)
            RA.give(ky, y)
            yield
            xx = PO(I.tensor_tensor(X[:, b, :], X[:, b, :], GA_[:], ALU.add), y, xw[b], xr_[b])
            xw[b], xr_[b] = xx, []
            RBk.give(bi, xx, y, m)
            yield

        rt_free = [None]

        def route(l, ready, p):
            k, bk, fr = yield from RM.take()
            for i in range(G):
                PE(I.matmul(bk[:, 4 * i:4 * i + 4], XF[1][0][:, 128 * i:128 * i + 128], wg1,
                            start=True, stop=False), fr, ready, d_wp[3])
                m = PE(I.matmul(bk[:, 4 * i:4 * i + 4], XF[1][1][0:16, 128 * i:128 * i + 128],
                                wg2, start=False, stop=True))
            xf_free[1].append(m)
            yield
            R = lambda j: rt[:, j, :]
            R2 = lambda j: rt[:, j, :].rearrange("p (b e) -> p b e", e=4)
            W2 = rw[:, p, :].rearrange("p (b e) -> p b e", e=4)
            o = DV(I.tensor_copy(R(0), bk[:, 0:16]), m, rt_free[0])
            RM.give(k, o)
            mx = DV(I.tensor_reduce(rt[:, 1, 0:4], R2(0), AX.X, ALU.max), o)
            yield
            d = DV(I.tensor_tensor(R2(2), R2(0), rt[:, 1, 0:4].unsqueeze(2).to_broadcast([128, 4, 4]),
                                   ALU.subtract), mx)
            exq = AC(I.activation(R(3), R(2), ACT.Exp), d)
            r3 = lambda j: rt3[:, j, :].rearrange("p (b e f) -> p b e f", b=4, e=4)
            le = R2(0).unsqueeze(3).to_broadcast([128, 4, 4, 4])
            lf = R2(0).unsqueeze(2).to_broadcast([128, 4, 4, 4])
            g1 = DV(I.tensor_tensor(r3(0), lf, le, ALU.is_gt), o)
            g2 = DV(I.tensor_tensor(r3(1), lf, le, ALU.is_equal), o)
            yield
            g2 = DV(I.tensor_tensor(rt3[:, 1, :], rt3[:, 1, :], ltm[:], ALU.mult), g2, d_ltm)
            yield
            g2 = DV(I.tensor_tensor(rt3[:, 0, :], rt3[:, 0, :], rt3[:, 1, :], ALU.add), g1, g2)
            yield
            g2 = DV(I.tensor_reduce(R2(4), r3(0), AX.X, ALU.add), g2)
            yield
            g2 = DV(I.tensor_scalar(R(4), R(4), 1.5, None, ALU.is_lt), g2)
            yield
            g2 = DV(I.tensor_tensor(R(5), R(4), R(3), ALU.mult), g2, exq)
            yield
            s = DV(I.tensor_reduce(rt[:, 6, 0:4], R2(5), AX.X, ALU.add), g2)
            yield
            s = DV(I.reciprocal(rt[:, 7, 0:4], rt[:, 6, 0:4]), s)
            yield
            s = DV(I.tensor_tensor(W2, R2(5), rt[:, 7, 0:4].unsqueeze(2).to_broadcast([128, 4, 4]),
                                   ALU.mult), s)
            rt_free[0] = s
            yield
            return s

        def mlp(l, g):
            keep = []
            ni, XT, xfree = yield from RN.take()
            yield from norm_t(l, range(G * g, G * g + G), 1, XT, xfree, RM, keep)
            ready = keep[0]
            cw = None
            if l == 3:
                cw = yield from route(l, keep[1], g % 2)

            def up(x):
                hi, Hx, hfree = yield from RH.take()
                ev = []
                for c in range(5):
                    n = 128 if c < 4 else 64
                    k, bk, fr = yield from RM.take()
                    lo = FF * x + 128 * c
                    m = mm_split(bk[:, :], XT, WF[l], slice(0, 512), slice(lo, lo + 128), False, fr, ready, d_wf[l])
                    yield
                    bias = b1[l][0:n, 5 * x + c:5 * x + c + 1]
                    if c % 2:
                        o = AC(I.activation(Hx[0:n, c, :], bk[0:n, :], ACT.Identity, bias=bias), m, hfree)
                    else:
                        o = DV(I.tensor_scalar(Hx[0:n, c, :], bk[0:n, :], bias, None, ALU.add), m, hfree)
                    RM.give(k, o)
                    ev.append(o)
                if x == NE[l] - 1:
                    RN.give(ni, m)
                yield
                a1 = AC(I.activation(Hx[:, 0:4, :], Hx[:, 0:4, :], ACT.Gelu_apprx_tanh), ev)
                a2 = AC(I.activation(Hx[0:64, 4, :], Hx[0:64, 4, :], ACT.Gelu_apprx_tanh), ev)
                return hi, Hx, [a1, a2]

            hs = [(yield from up(0))]
            if l == 3:
                ai, acc_t, afree = yield from RMA.take()
            for x in range(NE[l]):
                if x + 1 < NE[l]:
                    hs.append((yield from up(x + 1)))
                hi, Hx, hready = hs[x]
                yield
                for hf in range(2):
                    last = x == NE[l] - 1
                    if last:
                        gi, gmt, gfree = yield from RG.take()
                        gm = yield from gates(l, range(G * g + 2 * hf, G * g + 2 * hf + 2), 1, gmt[:], RM, gfree)
                    k, bk, fr = yield from RM.take()
                    for i2 in range(2):
                        i = 2 * hf + i2
                        for c in range(5):
                            n = 128 if c < 4 else 65
                            m = PE(I.matmul(
                                bk[:, 256 * i2:256 * i2 + C], Hx[0:n, c, 128 * i:128 * i + 128], w2[l][0:n, 5 * x + c, :],
                                start=(c == 0), stop=(c == 4)), fr, hready)
                        yield
                    bs = slice(G * g + 2 * hf, G * g + 2 * hf + 2)
                    yv = bk[:, :].rearrange("p (i c) -> p i c", i=2)[:, :, 0:C]
                    if l == 3:
                        os = []
                        ma = acc_t[hf][:].rearrange("p a b -> p (a b)").rearrange("p (n c) -> p n c", n=2)
                        for i2 in range(2):
                            i = 2 * hf + i2
                            s = rw[:, g % 2, 4 * i + x:4 * i + x + 1]
                            if x == 0:
                                o = DV(I.tensor_scalar(ma[:, i2, :], yv[:, i2, :], s, None, ALU.mult), m, cw, afree)
                            else:
                                o = DV(I.scalar_tensor_tensor(ma[:, i2, :], yv[:, i2, :], s, ma[:, i2, :], ALU.mult,
                                                              ALU.add), m, acc[hf])
                            os.append(o)
                        if x == 0 and hf == 0:
                            acc = [None, None]
                        acc[hf] = os
                        RM.give(k, os)
                        if last:
                            y = DV(I.tensor_tensor(gmt[:], ma, gmt[:], ALU.mult), os, gm)
                    else:
                        y = DV(I.tensor_tensor(gmt[:], yv, gmt[:], ALU.mult), m, gm)
                        RM.give(k, y)
                    if last:
                        if l == 3 and hf == 1:
                            RMA.give(ai, y)
                        ws = [xw[b] for b in range(bs.start, bs.stop)] + [xr_[b] for b in range(bs.start, bs.stop)]
                        xx = PO(I.tensor_tensor(X[:, bs, :], X[:, bs, :], gmt[:], ALU.add), y, ws)
                        RG.give(gi, xx)
                        for b in range(bs.start, bs.stop):
                            xw[b], xr_[b] = xx, []
                    yield
                RH.give(hi, m)
            if l == 3:
                outs.append(DMA(out[G * g:G * g + G].rearrange("b t c -> t b c"), X[:, G * g:G * g + G, :],
                                [xw[b] for b in range(G * g, G * g + G)]))

        outs = []

        u_ready = []

        def qr():
            w1 = list(d_qr) + [z_sc]
            w2_ = [d_qr[1]]
            for k in range(D):
                n = C - k
                i, bk, fr = yield from RM.take()
                m = PE(I.matmul(bk[:, 0:n], eye[:, k:k + 1].to_broadcast([128, 128]),
                                                           T1[:, k:C], start=True, stop=True), fr, w1, d_eye)
                yield
                c = AC(I.copy(VS[:, 0:n], bk[:, 0:n]), m, w1, w2_)
                RM.give(i, c)
                yield
                s0 = DV(I.tensor_tensor_reduce(JK[:, 0:n], VS[:, 0:n], VS[:, 0:n], 1.0, 0.0, ALU.mult,
                                               ALU.add, sc[:, 0:1]), c, jk_free[0])
                p0 = PO(I.tensor_tensor(sc[:, 1:2], sc[:, 0:1], half_p[:, :], ALU.pow), s0, d_half2)
                t1 = DV(I.tensor_tensor_reduce(JK[:, 0:n], T1[:, k:C], VS[:, 0:n], 1.0, 0.0, ALU.mult,
                                               ALU.add, sc[:, 6:7]), c, s0)
                t2 = DV(I.tensor_tensor_reduce(JK[0:80, 0:n], T2[:, k:C], VS[0:80, 0:n], 1.0, 0.0,
                                               ALU.mult, ALU.add, sc[0:80, 7:8]), c, t1)
                jk_free[0] = t2
                s1 = DV(I.tensor_scalar(sc[:, 2:3], VS[:, 0:1], 0.0, 2.0, ALU.is_ge, ALU.mult), c)
                yield
                s1 = DV(I.scalar_tensor_tensor(sc[:, 3:4], sc[:, 2:3], -1.0, sc[:, 1:2], ALU.add, ALU.mult), s1, p0)
                s2 = DV(I.scalar_tensor_tensor(sc[:, 4:5], VS[:, 0:1], sc[:, 3:4], sc[:, 0:1],
                                               ALU.mult, ALU.add), s1)
                t1 = DV(I.scalar_tensor_tensor(sc[:, 6:7], T1[:, k:k + 1], sc[:, 3:4], sc[:, 6:7],
                                               ALU.mult, ALU.add), s1, t1)
                s3 = DV(I.reciprocal(sc[:, 5:6], sc[:, 4:5]), s2)
                t2 = DV(I.scalar_tensor_tensor(sc[0:80, 7:8], T2[:, k:k + 1], sc[0:80, 3:4], sc[0:80, 7:8],
                                               ALU.mult, ALU.add), s1, t2)
                v = DV(I.tensor_tensor(VS[:, 0:1], VS[:, 0:1], sc[:, 3:4], ALU.add), s2, t2)
                u = DV(I.tensor_scalar(sc[:, 8:10], sc[:, 6:8], sc[:, 5:6], -1.0, ALU.mult, ALU.mult), t1, t2, s3)
                w1 = [DV(I.scalar_tensor_tensor(T1[:, k:C], VS[:, 0:n], sc[:, 8:9], T1[:, k:C],
                                                ALU.mult, ALU.add), u, v)]
                yield
                w2_ = [DV(I.scalar_tensor_tensor(T2[:, k:C], VS[0:80, 0:n], sc[0:80, 9:10], T2[:, k:C],
                                                 ALU.mult, ALU.add), u)]
                yield

            a = []
            for h in range(2):
                a.append(DMA(U1[0:64, 64 * h:64 * h + 64], T1[64:128, 0:64], w1))
                a.append(DMA(U1[64:128, 64 * h:64 * h + 64], T2[0:64, 0:64], w2_))
                a.append(DMA(U2[:, 64 * h:64 * h + 64], T2[64:80, 0:64], w2_))
            yield
            yield
            i, bk, fr = yield from RM.take()
            PE(I.transpose(bk[:, 0:128], U1[:, :], eye[:, :]), fr, a)
            m = PE(I.transpose(bk[:, 128:144], U2[:, :], eye[0:16, 0:16]))
            c = AC(I.copy(UT[:, :], bk[:, 0:C]), m)
            RM.give(i, c)
            u_ready.append(c)
            u_ready.extend(a)
            yield

        half_p = sb("halfp", [128, 1])
        d_half2 = PO(I.memset(half_p[:], 0.5))
        z_sc = PO(I.memset(sc[:], 0.0))
        cs_ready = []

        def rot():
            wr = []
            stg = [None, None]
            for n in range(8):
                p = n % 2
                w1_, w2s = ROT[p]
                dd = [DMA(w1_, a["rotw"][0:128, 512 * n:512 * n + 512], stg[p]),
                      DMA(w2s, a["rotw"][128:145, 512 * n:512 * n + 512], stg[p])]
                i, bk, fr = yield from RM.take()
                PE(I.matmul(bk[0:32, :], sT1[:, :], w1_, start=True, stop=False), fr, dd, sil)
                m = PE(I.matmul(bk[0:32, :], sT2[:, :], w2s, start=False, stop=True))
                stg[p] = m
                c = AC(I.copy(VR[p][:, :], bk[0:32, :]), m, wr[-2:-1])
                RM.give(i, c)
                wr.append(DMA(vsc[:, 512 * n:512 * n + 512], VR[p][:, :], c))
                yield
            vv = vsc.rearrange("(q t) (i j) -> t i q j", t=2, j=D)
            ld = []
            for t in range(2):
                ld.append(DMA(HS[64 * t:64 * t + 64, :, :], vv[t], wr))
                ld.append(DMA(BD[64 * t:64 * t + 64, :, 64 * t:64 * t + 64], vv[t], wr, z_bd))
            for _ in range(4):
                yield
            S, Cc = SC[:, :, 0, :], SC[:, :, 1, :]
            w = []
            for n in range(4):
                i, bk, fr = yield from RM.take()
                for j in range(4):
                    m = PE(I.matmul(bk[:, 64 * j:64 * j + 64], BD[:, 4 * n + j, :], eye2[:, :],
                                                               start=True, stop=True), fr, ld, d_eye2)
                o = DV(I.tensor_tensor(HS[:, 4 * n:4 * n + 4, :], HS[:, 4 * n:4 * n + 4, :],
                                                             bk[:, 0:256].rearrange("p (a b) -> p a b", a=4),
                                                             ALU.subtract), m)
                RM.give(i, o)
                w.append(o)
                yield

            def spread(n, src, scale, ready, wd):
                o = []
                for t in range(2):
                    r = slice(64 * t, 64 * t + 64)
                    o.append(AC(I.mul(BD[r, 4 * n:4 * n + 4, 64 * t:64 * t + 64],
                                                          src[r, 4 * n:4 * n + 4, :], scale), ready, wd))
                return o
            f = 2.0 ** -S_SQ
            bds, q4 = [], []
            for n in range(4):
                r = slice(4 * n, 4 * n + 4)
                s = DV(I.tensor_scalar(S[:, r, :], HS[:, r, :], f, None, ALU.mult), w[n])
                bds.append([s] + spread(n, HS, f, w[n], None))
                yield
            qs_, pre = [], []
            for n in range(4):
                r = slice(4 * n, 4 * n + 4)
                i, bk, fr = yield from RM.take()
                for j in range(4):
                    m = PE(I.matmul(bk[:, 128 * j:128 * j + 64], BD[:, 4 * n + j, :],
                                                               S[:, 4 * n + j, :], start=True, stop=True), fr, bds[n])
                bv = bk[:, :].rearrange("p (a b) -> p a b", a=4)[:, :, 0:64]
                o = AC(I.mul(HS[:, r, :], bv, -1.0), m)
                RM.give(i, o)
                qs_.append(o)
                yield
            e_ = eye2[:, :].unsqueeze(1).to_broadcast([128, 4, D])
            fin = []
            for n in range(4):
                r = slice(4 * n, 4 * n + 4)
                t0 = DV(I.tensor_scalar(Cc[:, r, :], HS[:, r, :], 1.0 / 24, None, ALU.mult), qs_[n])
                z = [AC(I.copy(BQ[64 * t:64 * t + 64, :, 64 * t:64 * t + 64],
                                                   HS[64 * t:64 * t + 64, r, :]), qs_[n], bq_free[0], z_bq)
                     for t in range(2)]
                i, bk, fr = yield from RM.take()
                for j in range(4):
                    m = PE(I.matmul(bk[:, 128 * j:128 * j + 64], BQ[:, j, :],
                                                               HS[:, 4 * n + j, :], start=True, stop=True), fr, z, t0)
                bq_free[0] = m
                bv = bk[:, :].rearrange("p (a b) -> p a b", a=4)[:, :, 0:64]
                q2 = DV(I.tensor_scalar(Q2[:, :, :], bv, 1.0 / 24, None, ALU.mult), m, q2_free[0])
                RM.give(i, q2)
                cc = DV(I.scalar_tensor_tensor(Cc[:, r, :], HS[:, r, :], 0.5, Q2[:, :, :], ALU.mult,
                                                              ALU.add), q2, t0)
                g1 = DV(I.tensor_scalar(Q2[:, :, :], Q2[:, :, :], 0.2, None, ALU.mult), cc)
                gg = DV(I.scalar_tensor_tensor(Q3[:, :, :], HS[:, r, :], 1.0 / 6, Q2[:, :, :], ALU.mult,
                                                              ALU.add), g1, q3_free[0])
                q2_free[0] = gg
                yield
                i, bk, fr = yield from RM.take()
                for j in range(4):
                    m = PE(I.matmul(bk[:, 128 * j:128 * j + 64], BD[:, 4 * n + j, :],
                                                               Q3[:, j, :], start=True, stop=True), fr, gg)
                q3_free[0] = m
                bv = bk[:, :].rearrange("p (a b) -> p a b", a=4)[:, :, 0:64]
                ss = DV(I.tensor_tensor(HS[:, r, :], S[:, r, :], bv, ALU.subtract), m)
                RM.give(i, ss)
                s2 = DV(I.tensor_copy(S[:, r, :], HS[:, r, :]), ss)
                fin.append([cc, s2] + spread(n, HS, 1.0, ss, m))
                yield
            for k in range(S_SQ):
                nxt = []
                for n in range(4):
                    r = slice(4 * n, 4 * n + 4)
                    i, bk, fr = yield from RM.take()
                    for j in range(4):
                        m = PE(I.matmul(
                            bk[:, 128 * j:128 * j + 128], BD[:, 4 * n + j, :],
                            SC[:, 4 * n + j, :, :].rearrange("p a b -> p (a b)"), start=True, stop=True), fr, fin[n])
                    bv = bk[:, :].rearrange("p (a b) -> p a b", a=4)
                    c = AC(I.mul(Cc[:, r, :], bv[:, :, 0:64], -2.0), m)
                    o = DV(I.tensor_tensor(HS[:, r, :], S[:, r, :], bv[:, :, 64:128],
                                                                 ALU.subtract), m, c)
                    RM.give(i, c, o)
                    s = PO(I.tensor_scalar(S[:, r, :], HS[:, r, :], 2.0, None, ALU.mult), o)
                    nxt.append([c, s] + (spread(n, HS, 2.0, o, m) if k < S_SQ - 1 else []))
                    yield
                fin = nxt
            o = []
            for n in range(4):
                r = slice(4 * n, 4 * n + 4)
                o.append(DV(I.tensor_tensor(HS[:, r, :], S[:, r, :], Cc[:, r, :], ALU.add), fin[n]))
            cs_ready.extend(o)
            yield

        z_bq = PO(I.memset(BQ, 0.0))
        bq_free, q2_free, q3_free = [None], [None], [None]
        RZ = Ring(q, [(ZT, WZ)])

        def rotate(g):
            keep = []
            ni, _, _ = yield from RN.take()
            yield from turn(X[:, G * g:G * g + G, :], [xw[b] for b in range(G * g, G * g + G)], None, range(G), 1, None,
                            None, RM, keep)
            k, bk, fr = yield from RM.take()
            PE(I.matmul(bk[:, :], U1[:, :], XF[1][0][:, :], start=True, stop=False), fr, keep[0], u_ready)
            m = PE(I.matmul(bk[:, :], U2[:, :], XF[1][1][0:16, :], start=False, stop=True))
            xf_free[1] = [m]
            RN.give(ni, m)
            zi, _, zfree = yield from RZ.take()
            z = AC(I.copy(ZT[:, :], bk[:, :]), m, zfree, cs_ready)
            RM.give(k, z)
            yield
            k, bk, fr = yield from RM.take()
            for i in (0, 2, 1, 3):
                b = G * g + i
                r = 64 * (b % 2)
                m = PE(I.matmul(
                    bk[r:r + 64, 128 * i:128 * i + 128], HS[r:r + 64, b // 2, :], ZT[r:r + 64, 128 * i:128 * i + 128],
                    start=True, stop=True), fr, z, cs_ready)
            wv = []
            for t in range(2):
                half_of = lambda x, t=t: x[64 * t:64 * t + 64, :].rearrange("p (a b) -> p a b", a=4)[:, t:4:2, :]
                wv.append(AC(I.copy(half_of(WZ), half_of(bk)), m))
            RM.give(k, wv)
            yield
            for t in range(2):
                k, bk, fr = yield from RM.take()
                for i2 in range(2):
                    i = 2 * i2 + t
                    m = PE(I.matmul(bk[:, 256 * i2:256 * i2 + C],
                                              WZ[64 * t:64 * t + 64, 128 * i:128 * i + 128], UT[64 * t:64 * t + 64, :],
                                              start=True, stop=True), fr, wv)
                bs = range(G * g + t, G * g + G, 2)
                xv = X[:, G * g + t:G * g + G:2, :]
                yv = bk[:, :].rearrange("p (i c) -> p i c", i=2)[:, :, 0:C]
                o = DV(I.tensor_tensor(xv, xv, yv, ALU.add), m, [xr_[b] for b in bs])
                RM.give(k, o)
                for b in bs:
                    xw[b], xr_[b] = o, []
                yield
            RZ.give(zi, m)

        def hand_over():
            for _ in range(NW):
                i, _, w = yield from RSL[2].take()
                if i < NW - 1:
                    RSL[3].give(i, w)
                else:
                    RH.give(1, DV(I.memset(H[1][64:128, 4, :], 1.0), w), w)
                yield

        def load3():
            w = [q.q[e][-1] for e in ("tensor", "scalar", "vector")]
            yield from load_att(3, w)
            yield from load_mlp(3, w)

        for _ in load_att(0):
            pass
        jobs_l = deque([(("w", 0), set(), lambda: load_mlp(0)), (("wa", 2), set(), lambda: load_att(2)),
                        (("w", 2), {("m", 0, g) for g in range(NG)}, lambda: load_mlp(2, q.q["tensor"][-1])),
                        (("w", 3), {("r", g) for g in range(NG)}, load3)])
        for _ in modulation(0, WM[0], d_mod[0], MR, MRS[0], None):
            pass
        for i in range(2):
            RP.give(i, q.q["tensor"][-1])
            RP.free[2 + i] = None
        RH.free[0] = None

        def modulations():
            yield from modulation(2, WM[1], d_mod[2], MR2, MRS[1], None)
            m2q = q.q["tensor"][-1]
            d3 = [DMA(WM[1][0][:, 0:864], a["mod3"][0:128], m2q), DMA(WM[1][1][:, 0:864], a["mod3"][128:145], m2q)]
            yield
            yield from modulation(3, WM[1], d3, MR2, MRS[1], mod_s[2] + mod_t[2])
            for i in range(2, 4):
                RP.give(i, q.q["tensor"][-1])
            RH.give(0, mod_s[0], mod_s[3], DV(I.memset(H[0][64:128, 4, :], 1.0), mod_s[3], mod_s[0]))

        done = {}
        pj, aj, mj = deque(), deque(), deque()
        prep = [(l, u) for l in LAY for u in range(B // GP)]
        for n, (l, u) in enumerate(prep):
            g = GP * u // G
            need = {0: set(), 2: {("r", g), "mods"}, 3: {("m", 2, g), ("w", 3)}}[l]
            prev = {("x", l0, b) for l0, v in prep[max(n - 2, 0):max(n - 1, 0)] for b in range(GP * v, GP * v + GP)}
            pj.append((("p", l, u), need | prev, lambda l=l, u=u: prep_att(l, u)))
            for b in range(GP * u, GP * u + GP):
                aj.append((("a", l, b), {("p", l, u), {0: ("p", 0, 0), 2: ("wa", 2), 3: ("w", 3)}[l]},
                           lambda l=l, b=b: att(l, b)))
        order = [("m", 0, g) for g in range(6)] + [("r", 0), ("r", 1), ("m", 0, 6), ("r", 2), ("r", 3), ("m", 0, 7)]
        order += [("r", g) for g in range(4, NG)] + [("m", l, g) for l in (2, 3) for g in range(NG)]
        for name in order:
            g = name[-1]
            if name[0] == "r":
                mj.append((name, {("m", 0, g), "qr", "rot"}, lambda g=g: rotate(g)))
            else:
                l = name[1]
                mj.append((name, {("a", l, b) for b in range(G * g, G * g + G)} | {("w", l)},
                           lambda l=l, g=g: mlp(l, g)))
        lanes = [(jobs_l, 1, 1), (pj, 1, 1), (aj, NW + 1, 1), (mj, 2, 1), (deque([("rot", set(), rot)]), 1, 1), (deque([("qr", set(), qr)]), 1, 1),
                 (deque([("mods", set(), modulations)]), 1, 1),
                 (deque([("ho", {("s", 2, B - 1)}, hand_over)]), 1, 1)]
        act = []

        def admit():
            for n, (jobs, width, ahead) in enumerate(lanes):
                while sum(j[0] == n for j in act) < width:
                    job = next((j for j in list(jobs)[0:ahead] if j[1] <= done.keys()), None)
                    if job is None:
                        break
                    jobs.remove(job)
                    name, need, make = job
                    act.append([n, name, make(), max([done[x] for x in need], default=0.0),
                                LEAD[name if name in LEAD else name[0]]])

        stuck = []
        admit()
        while act:
            now = q.clock["tensor"]
            j = min([j for j in act if j not in stuck],
                    key=lambda j: (max(j[3] - j[4], now), j[3] - j[4]))
            q.last = 0.0
            try:
                t = next(j[2])
            except StopIteration:
                done[j[1]] = max(q.last, j[3])
                act.remove(j)
                stuck.clear()
                admit()
                continue
            if t == -1:
                stuck.append(j)
            else:
                stuck.clear()
                j[3] = max(q.last, t or 0.0, j[3])
            admit()
        assert not any(jobs for jobs, _, _ in lanes)

        q.put("sync", I.nop(), outs)

        q.count(sem)
        block = st.enter_context(nc.Block())
        block.sync(lambda e: q.play("sync", e))
        block.gpsimd(lambda e: q.play("gpsimd", e))
        block.scalar(lambda e: q.play("scalar", e))
        block.vector(lambda e: q.play("vector", e))
        block.tensor(lambda e: q.play("tensor", e))


def layout(inputs):
    f = np.float32
    g = {k: np.asarray(v) for k, v in inputs.items()}
    a = {"x": np.ascontiguousarray(g["x"])}
    a["condT"] = np.concatenate([g["cond_1152"].T, np.ones((1, B), f)], 0)

    def rows(w, b):
        return np.concatenate([w, b[None, :]], 0)

    names = {0: ("L0_cond_", "w_mod", "b_mod", "w_qkv", "b_qkv", "w_proj", "b_proj", "w1", "b1", "w2", "b2"),
             2: ("L2_cond_", "W_ada", "b_ada", "W_qkv", "b_qkv", "W_proj", "b_proj", "W_fc1", "b_fc1", "W_fc2", "b_fc2"),
             3: ("L3_cond_", "w_adaln", "b_adaln", "w_qkv", "b_qkv", "w_proj", "b_proj", "w1", "b1", "w2", "b2")}
    for l, (pre, *ns) in names.items():
        wm, bm, wq, bq, wp, bp, w1, b1, w2, b2 = (g[pre + n] for n in ns)
        a[f"mod{l}"] = rows(wm, bm)
        if l != 3:
            w1, b1, w2, b2 = w1[None], b1[None], w2[None], b2[None]
        n = len(w1)
        z = np.zeros((1, n * FF), f)
        m = np.concatenate([rows(wq, bq), np.concatenate([w1.transpose(1, 0, 2).reshape(C, n * FF), z], 0),
                            np.zeros((C + 1, 64), f)], 1)
        ms = np.zeros((80, m.shape[1]), f)
        ms[0:17] = ms[32:49] = m[128:145]
        ms[64:80] = m[128:144]
        a[f"main{l}"], a[f"mains{l}"] = m[0:128], ms
        gate = np.concatenate([g["L3_cond_w_gate"], np.zeros((1, 4), f)], 0) if l == 3 else np.zeros((C + 1, 4), f)
        a[f"proj{l}"] = np.concatenate([rows(wp, bp), gate], 1)
        ww = np.zeros((n, 5, 128, C), f)
        ww[:, 0:4] = w2[:, 0:512].reshape(n, 4, 128, C)
        ww[:, 4, 0:64] = w2[:, 512:576]
        ww[:, 4, 64] = b2
        bb = np.zeros((n, 5, 128), f)
        bb[:, 0:4] = b1[:, 0:512].reshape(n, 4, 128)
        bb[:, 4, 0:64] = b1[:, 512:576]
        a[f"pack{l}"] = np.concatenate([ww.reshape(n * 5, 128, C).transpose(1, 0, 2).reshape(128, -1),
                                        bb.reshape(n * 5, 128).T], 1)
    a["gqk"] = np.concatenate([np.tile(g["L0_cond_g_q"], NH), np.tile(g["L0_cond_g_k"], NH)])[None, :]
    qr1 = np.zeros((128, C), f)
    qr1[0:D] = g["L1_cond_P"].T
    qr1[64:128, 0:64] = np.eye(64, dtype=f)
    qr2 = np.zeros((80, C), f)
    qr2[:, 64:144] = np.eye(80, dtype=f)
    a["qr1"], a["qr2"] = qr1, qr2
    iu, ju = np.triu_indices(D, k=1)
    rw = np.zeros((C + 1, D, D), f)
    rw[0:C, iu, ju] = g["L1_cond_W"].T
    rw[C, iu, ju] = g["L1_cond_b"]
    a["rotw"] = rw.reshape(C + 1, D * D)
    a["eye"] = np.eye(128, dtype=f)
    a["eye2"] = np.concatenate([np.eye(64, dtype=f)] * 2, 0)
    a["e3"] = np.concatenate([np.eye(32, dtype=f)] * 3, 0)
    a["half"] = np.full((128, 32), -0.5, f)
    lt = np.zeros((4, 4, 4), f)
    for e in range(4):
        lt[:, e, 0:e] = 1.0
    a["ltm"] = np.broadcast_to(lt.reshape(1, 64), (128, 64))
    return {k: np.ascontiguousarray(v) for k, v in a.items()}


def kernel(**inputs):
    from concourse import bacc
    from concourse.bass_utils import run_bass_kernel_spmd

    nc = bacc.Bacc("TRN2", target_bir_lowering=False, num_devices=1)
    arrays, aps = {}, {}
    for k, v in layout(inputs).items():
        arrays["in_" + k] = v
        aps[k] = nc.dram_tensor("in_" + k, v.shape, mybir.dt.from_np(v.dtype), kind="ExternalInput").ap()
    out = nc.dram_tensor("out_0", (B, T, C), F32, kind="ExternalOutput").ap()
    program(nc, aps, out)
    r = run_bass_kernel_spmd(nc, [arrays], core_ids=[0])
    return r.results[0]["out_0"]
```
